# Optimizing a Trainium2 kernel written in Bass

```python
import numpy as np
import jax
import jax.numpy as jnp

def _softmax(x, axis=-1):
    return jax.nn.softmax(x, axis=axis)

def _gelu(x):
    return jax.nn.gelu(x, approximate=True)

def _silu(x):
    return jax.nn.silu(x)

def _sigmoid(x):
    return jax.nn.sigmoid(x)

def _layernorm(x, axis=-1, eps=1e-05):
    m = jnp.mean(x, axis=axis, keepdims=True)
    v = jnp.var(x, axis=axis, keepdims=True)
    return (x - m) / jnp.sqrt(v + eps)

def _scatter_add(tgt, idx, src, axis=0):
    return tgt.at[idx].add(src)

def _segment_sum(src, seg, n):
    return jax.ops.segment_sum(src, seg, n)
kernel_name = 'mk_adaln_d1_jaxref_r8_90346e'

def setup_inputs(seed: int=0):
    np.random.seed(seed)
    _w = jnp.asarray

    def _L0_attn_setup():
        import jax, jax.numpy as jnp
        import numpy as np
        HIDDEN = 256
        N_HEADS = 16
        N_KV_HEADS = 4
        HEAD_DIM = HIDDEN // N_HEADS
        ROPE_THETA = 10000.0
        B, S = (1, 256)

        def _apply_rope(x, position_ids, theta=ROPE_THETA):
            b, s, h, hd = x.shape
            dim_half = hd // 2
            inv_freq = 1.0 / theta ** (jnp.arange(0, dim_half, 2, dtype=jnp.float32) / dim_half)
            freqs = position_ids[:, :, None].astype(jnp.float32) * inv_freq[None, None, :]
            cos = jnp.cos(freqs)[:, :, None, :]
            sin = jnp.sin(freqs)[:, :, None, :]
            x_rot = x[..., :dim_half].reshape(b, s, h, dim_half // 2, 2)
            x0, x1 = (x_rot[..., 0], x_rot[..., 1])
            rotated = jnp.stack([x0 * cos - x1 * sin, x0 * sin + x1 * cos], axis=-1)
            rotated = rotated.reshape(b, s, h, dim_half)
            return jnp.concatenate([rotated, x[..., dim_half:]], axis=-1)
        key = jax.random.key(seed)
        k0, k1, k2, k3, k4 = jax.random.split(key, 5)
        std = 0.02
        return {'hidden_states': jax.random.normal(k0, (B, S, HIDDEN), dtype=jnp.float32), 'Wq': jax.random.normal(k1, (HIDDEN, N_HEADS * HEAD_DIM), dtype=jnp.float32) * std, 'Wk': jax.random.normal(k2, (HIDDEN, N_KV_HEADS * HEAD_DIM), dtype=jnp.float32) * std, 'Wv': jax.random.normal(k3, (HIDDEN, N_KV_HEADS * HEAD_DIM), dtype=jnp.float32) * std, 'Wo': jax.random.normal(k4, (HIDDEN, HIDDEN), dtype=jnp.float32) * std}
    _L0_attn_in = _L0_attn_setup()

    def _L0_ffn_setup():
        import jax, jax.numpy as jnp
        import numpy as np
        TOP_K = 4
        key = jax.random.key(seed)
        ks = jax.random.split(key, 8)
        B, S, H = (1, 128, 256)
        E, I = (60, 176)
        I_SH = 704
        s = 0.02
        return {'hidden_states': jax.random.normal(ks[0], (B, S, H), jnp.float32), 'gate_w': jax.random.normal(ks[1], (E, H), jnp.float32) * s, 'shared_gate_w': jax.random.normal(ks[2], (1, H), jnp.float32) * s, 'w13': jax.random.normal(ks[3], (E, 2 * I, H), jnp.float32) * s, 'w2': jax.random.normal(ks[4], (E, H, I), jnp.float32) * s, 'se_gate_up_w': jax.random.normal(ks[5], (2 * I_SH, H), jnp.float32) * s, 'se_down_w': jax.random.normal(ks[6], (H, I_SH), jnp.float32) * s}
    _L0_ffn_in = _L0_ffn_setup()
    _L0_c = _w((lambda *s: np.random.randn(*s).astype(np.float32) * 0.05)(1, 256))
    _L0_wmod = _w((lambda *s: np.random.randn(*s).astype(np.float32) * 0.05)(256, 6 * 256) * 256 ** (-0.5))
    _d = {'L0_attn_hidden_states': _L0_attn_in['hidden_states'], 'L0_attn_Wq': _L0_attn_in['Wq'], 'L0_attn_Wk': _L0_attn_in['Wk'], 'L0_attn_Wv': _L0_attn_in['Wv'], 'L0_attn_Wo': _L0_attn_in['Wo'], 'L0_ffn_gate_w': _L0_ffn_in['gate_w'], 'L0_ffn_shared_gate_w': _L0_ffn_in['shared_gate_w'], 'L0_ffn_w13': _L0_ffn_in['w13'], 'L0_ffn_w2': _L0_ffn_in['w2'], 'L0_ffn_se_gate_up_w': _L0_ffn_in['se_gate_up_w'], 'L0_ffn_se_down_w': _L0_ffn_in['se_down_w'], 'L0_c': _L0_c, 'L0_wmod': _L0_wmod}
    _x0 = _d['L0_attn_hidden_states']
    _d['L0_attn_hidden_states'] = jax.random.normal(jax.random.fold_in(jax.random.key(seed), 1), (1, 1024, 256), dtype=_x0.dtype)
    del _x0
    return _d

def reference(L0_attn_hidden_states, L0_attn_Wq, L0_attn_Wk, L0_attn_Wv, L0_attn_Wo, L0_ffn_gate_w, L0_ffn_shared_gate_w, L0_ffn_w13, L0_ffn_w2, L0_ffn_se_gate_up_w, L0_ffn_se_down_w, L0_c, L0_wmod):

    def _L0_attn_ref(hidden_states, Wq, Wk, Wv, Wo):
        import jax, jax.numpy as jnp
        import numpy as np
        HIDDEN = 256
        N_HEADS = 16
        N_KV_HEADS = 4
        HEAD_DIM = HIDDEN // N_HEADS
        ROPE_THETA = 10000.0
        B, S = (1, 256)

        def _apply_rope(x, position_ids, theta=ROPE_THETA):
            b, s, h, hd = x.shape
            dim_half = hd // 2
            inv_freq = 1.0 / theta ** (jnp.arange(0, dim_half, 2, dtype=jnp.float32) / dim_half)
            freqs = position_ids[:, :, None].astype(jnp.float32) * inv_freq[None, None, :]
            cos = jnp.cos(freqs)[:, :, None, :]
            sin = jnp.sin(freqs)[:, :, None, :]
            x_rot = x[..., :dim_half].reshape(b, s, h, dim_half // 2, 2)
            x0, x1 = (x_rot[..., 0], x_rot[..., 1])
            rotated = jnp.stack([x0 * cos - x1 * sin, x0 * sin + x1 * cos], axis=-1)
            rotated = rotated.reshape(b, s, h, dim_half)
            return jnp.concatenate([rotated, x[..., dim_half:]], axis=-1)
        b, s, _ = hidden_states.shape
        groups = N_HEADS // N_KV_HEADS
        q = (hidden_states @ Wq).reshape(b, s, N_HEADS, HEAD_DIM)
        k = (hidden_states @ Wk).reshape(b, s, N_KV_HEADS, HEAD_DIM)
        v = (hidden_states @ Wv).reshape(b, s, N_KV_HEADS, HEAD_DIM)
        position_ids = jnp.broadcast_to(jnp.arange(s)[None, :], (b, s))
        q = _apply_rope(q, position_ids)
        k = _apply_rope(k, position_ids)
        if groups > 1:
            k = jnp.repeat(k, groups, axis=2)
            v = jnp.repeat(v, groups, axis=2)
        scale = 1.0 / jnp.sqrt(jnp.float32(HEAD_DIM))
        scores = jnp.einsum('bshd,bthd->bhst', q, k) * scale
        attn = jax.nn.softmax(scores, axis=-1)
        out = jnp.einsum('bhst,bthd->bshd', attn, v)
        out = out.reshape(b, s, HIDDEN)
        return out @ Wo

    def _L0_ffn_ref(hidden_states, gate_w, shared_gate_w, w13, w2, se_gate_up_w, se_down_w):
        import jax, jax.numpy as jnp
        import numpy as np
        TOP_K = 4
        orig_shape = hidden_states.shape
        E, H = gate_w.shape
        I = w2.shape[2]
        x = hidden_states.reshape(-1, H)
        M = x.shape[0]
        gu = x @ se_gate_up_w.T
        I_sh = se_down_w.shape[1]
        shared = jax.nn.silu(gu[:, :I_sh]) * gu[:, I_sh:] @ se_down_w.T
        shared = shared * jax.nn.sigmoid(x @ shared_gate_w.T)
        logits = x @ gate_w.T
        probs = jax.nn.softmax(logits.astype(jnp.float32), axis=-1)
        weights, sel = jax.lax.top_k(probs, TOP_K)
        cw = jnp.zeros((M, E), jnp.float32).at[jnp.arange(M)[:, None], sel].add(weights)

        def step(acc, ews):
            w13_e, w2_e, cw_e = ews
            gu_e = x @ w13_e.T
            h = jax.nn.silu(gu_e[:, :I]) * gu_e[:, I:]
            return (acc + cw_e[:, None] * (h @ w2_e.T), None)
        sparse, _ = jax.lax.scan(step, jnp.zeros((M, H), jnp.float32), (w13, w2, cw.T))
        return (shared + sparse).reshape(orig_shape)
    x = L0_attn_hidden_states
    mod = (_silu(L0_c) @ L0_wmod).reshape(L0_c.shape[0], 6, 1, -1)
    sa, ca, ga, sb, cb, gb = (mod[:, 0], mod[:, 1], mod[:, 2], mod[:, 3], mod[:, 4], mod[:, 5])
    ga = (2 * (ga >= 0) - 1) * jnp.maximum(jnp.abs(ga), 0.25)
    gb = (2 * (gb >= 0) - 1) * jnp.maximum(jnp.abs(gb), 0.25)
    h = _layernorm(x, axis=-1) * (1 + ca) + sa
    x = x + ga * _L0_attn_ref(h, L0_attn_Wq, L0_attn_Wk, L0_attn_Wv, L0_attn_Wo)
    h = _layernorm(x, axis=-1) * (1 + cb) + sb
    x = x + gb * _L0_ffn_ref(h, L0_ffn_gate_w, L0_ffn_shared_gate_w, L0_ffn_w13, L0_ffn_w2, L0_ffn_se_gate_up_w, L0_ffn_se_down_w)
    return x

_drawn_inputs = setup_inputs


def setup_inputs(seed=0):
    import zlib

    import numpy as np

    out = dict(_drawn_inputs(seed))
    spreads = {}
    factors = {'L0_attn_Wq': 8.0,
     'L0_attn_Wk': 8.0,
     'L0_attn_Wv': 8.0,
     'L0_attn_Wo': 8.0,
     'L0_ffn_gate_w': 8.0,
     'L0_ffn_shared_gate_w': 8.0,
     'L0_ffn_w13': 8.0,
     'L0_ffn_w2': 8.0,
     'L0_ffn_se_gate_up_w': 8.0,
     'L0_ffn_se_down_w': 8.0,
     'L0_c': 8.0,
     'L0_wmod': 8.0}
    for name, (base, spread) in spreads.items():
        noise = np.random.default_rng([zlib.crc32(name.encode()), seed]).standard_normal(out[name].shape)
        drawn = base * np.exp(spread * noise) if base else spread * noise
        out[name] = jnp.asarray(drawn.astype(out[name].dtype))
    for name, factor in factors.items():
        out[name] = (out[name] * factor).astype(out[name].dtype)
    return out
```

```python
import concourse.bass as bass
from concourse import mybir
from contextlib import ExitStack


def adaln_layer(nc, x_in, cos_in, sin_in, c_in, wmod_in, wqkv_in, wo_in, wr_in, segu_in, sedn_in,
                w13_in, w2_in, xdisp, ydisp, out):
    f32, bf16, i32, u32 = mybir.dt.float32, mybir.dt.bfloat16, mybir.dt.int32, mybir.dt.uint32
    ALU, ACT, AX = mybir.AluOpType, mybir.ActivationFunctionType, mybir.AxisListType

    S, D = x_in.shape
    P = 128
    NT, NC = S // P, D // P
    HD, NH, NG = 16, 16, 4
    HP = 32
    QKV = (NH + 2 * NG) * HD
    NE, TOPK = 60, 4
    I13 = w13_in.shape[2] // NC
    I = I13 // 2
    IC = I // 2
    ISH = segu_in.shape[1] // 2
    SHH = ISH // 2
    NSC = (ISH + P - 1) // P
    SLAST = ISH - (NSC - 1) * P
    MAXOV = (S * TOPK) // P - 1
    EPS = 1e-5
    RING = 10
    LAPS = NE // RING
    U = 2 * NG
    LEAD = NT + 1
    STEPS = U * NT

    Q_FILL, O_FILL = [4 * LEAD + 1], []
    fills = 4 * LEAD + 1
    for n in range(STEPS):
        fills += 4 * (n + LEAD < STEPS)
        if n % NT == 2 and n > NT:
            O_FILL.append(fills - 2 * (n + LEAD < STEPS) + 1)
            fills += 1
        if n % NT == NT - 1 and n < STEPS - 1:
            fills += 1
            Q_FILL.append(fills)
    NB = xdisp.shape[0] // P
    ZW = NC * QKV
    N_ZERO = sum((n // ZW + 7) // 8 + (n % ZW > 0) for n in (NB * D, (NB - NE) * D))

    ctx = ExitStack()
    with ctx:
        def sb(name, shape, dt=f32):
            return ctx.enter_context(nc.sbuf_tensor(name, shape, dt))

        def ps(name, shape):
            return ctx.enter_context(nc.psum_tensor(name, shape, f32))

        def sem(name):
            return ctx.enter_context(nc.semaphore(name))

        x = sb("x", [P, NT, D])
        xh = sb("xh", [P, NT, D])
        hT = sb("hT", [P, NC, S])
        qkv = sb("qkv", [P, NT, QKV])
        QA = sb("QA", [P, NT, NG, 4 * HP])
        KA = sb("KA", [P, NT, NG, 4 * HP])
        QT = sb("QT", [P, NG, S])
        KT = sb("KT", [P, NG, S])
        VA = sb("VA", [P, NT, NG, HP])
        PT0 = KA[:, :, :, :].rearrange("p t g c -> p (t g c)").rearrange("p (b j q) -> p b j q", b=2, j=4)
        PT2 = sb("PT2", [P, 4, 512])
        PT = [PT0[:, 0], PT0[:, 1], PT2[:, :, :]]
        OT = sb("OT", [P, 512])
        MOD = sb("MOD", [P, 6, D])
        wide = sb("wide", [P, NC * 6 * D])
        wqkv = sb("wqkv", [P, NC, QKV])
        wo = sb("wo", [P, NC, D])
        wr = sb("wr", [P, NC, NE + 1])
        segu = sb("segu", [P, NC, 2 * ISH])
        sedn = sb("sedn", [P, NSC, D])
        w13 = sb("w13", [P, RING, NC * I13])
        w2 = sb("w2", [IC, RING, 2 * D])
        ident = sb("ident", [P, P])
        ones = sb("ones", [P, P])
        upper = sb("upper", [P, P], bf16)
        onesb = sb("onesb", [P, P], bf16)
        cosr = sb("cosr", [P, NT, 4])
        sinr = sb("sinr", [P, NT, 4])
        ccol = sb("ccol", [P, 4, NC])
        stats = sb("stats", [P, NT, 6])
        mv = sb("mv", [P, NT, 2])
        veps = sb("veps", [P, NT])
        mhalf = sb("mhalf", [P, NT])
        rstd = sb("rstd", [P, NT])
        mx = sb("mx", [P, 2, 4, 4, 2])
        rsum = sb("rsum", [P, 2, 4, 4])
        iota_i = sb("iota_i", [P, NE], i32)
        iotaf = sb("iotaf", [P, NE])
        top = sb("top", [P, NT, 8])
        topi = sb("topi", [P, NT, 8], u32)
        topf = sb("topf", [P, NT, 8])
        sgate = sb("sgate", [P, 2, NT])
        slotk = sb("slotk", [P, NT * TOPK])
        sloti = sb("sloti", [P, NT * TOPK], u32)
        novi = sb("novi", [1, 1], i32)
        ovei = sb("ovei", [1, MAXOV + 1], i32)
        PT2f = PT2[:, :, :].rearrange("p j q -> p (j q)")
        nrt = 4 * 4 * (NH + NG) * 4
        rt = PT2f[:, 0:nrt].rearrange("p (k t n) -> p k t n", k=4, t=4)
        crep = PT2f[:, nrt:nrt + NC * P].rearrange("p (c n) -> p c n", c=NC)
        small = wqkv[:, :, :].rearrange("p c n -> p (c n)")
        grid = NT * NE
        probs = PT2f[:, 0:grid].rearrange("p (t e) -> p t e", t=NT)
        slot = PT2f[:, grid:2 * grid].rearrange("p (t e) -> p t e", t=NT)
        mask = PT2[:, :, :].rearrange("p j q -> p (j q)").bitcast(bf16)[:, 4 * grid:5 * grid].rearrange("p (t e) -> p t e", t=NT)
        gt = PT2f[:, 3 * grid:3 * grid + NE * (NT - 1)].rearrange("p (e k) -> p e k", e=NE)
        gtmp = OT[:, 0:2 * D].rearrange("p (k n) -> p k n", k=2)
        wog = wide[:, 0:NC * D].rearrange("p (c n) -> p c n", c=NC)
        AT = qkv[:, :, :].rearrange("p t n -> p (t n)")[:, 0:NT * D].rearrange("p (t n) -> p t n", t=NT)
        QAf = QA[:, :, :, :].rearrange("p t g c -> p (t g c)")
        SH = QAf[:, 0:NT * D].rearrange("p (t n) -> p t n", t=NT)
        OH = QAf[:, NT * D:NT * D + NT * TOPK * NE].rearrange("p (t k e) -> p t k e", t=NT, k=TOPK)
        PR = KA[:, :, :, :].rearrange("p t g c -> p (t g c)")[:, 0:NT * TOPK * NE]\
            .rearrange("p (t k e) -> p t k e", t=NT, k=TOPK)
        KTf = KT[:, :, :].rearrange("p g s -> p (g s)")
        QTf = QT[:, :, :].rearrange("p g s -> p (g s)")
        h2T = KTf[:, 0:NC * S].rearrange("p (c s) -> p c s", c=NC)
        XG = [QTf[:, 512 * b:512 * b + D] for b in range(2)]
        XGT = [QTf[:, 1024 + 512 * b:1024 + 512 * b + D] for b in range(2)]
        SL = [QTf[:, 2048 + 256 * b:2048 + 256 * b + I] for b in range(2)]
        HS = [QTf[:, 2560 + 256 * b:2560 + 256 * b + I] for b in range(2)]
        HST = [QTf[0:IC, 3072 + 256 * b:3072 + 256 * b + 2 * P] for b in range(2)]
        YS = [QTf[:, 3584 + 256 * b:3584 + 256 * b + D] for b in range(2)]
        wmod = wide[:, :].rearrange("p (c n) -> p c n", c=NC)
        shg = wide[:, 0:ISH]
        shh = [wide[:, ISH * (1 + b):ISH * (2 + b)] for b in range(2)]
        shT = wide[:, 3 * ISH:3 * ISH + NSC * P].rearrange("p (c n) -> p c n", c=NSC)
        YG = [KTf[:, 2048 + 1024 * b:3072 + 1024 * b].rearrange("p (k n) -> p k n", k=TOPK) for b in range(2)] + \
             [w13[:, 2 * b:2 * b + 2, :].rearrange("p r n -> p (r n)")[:, 0:TOPK * D]
              .rearrange("p (k n) -> p k n", k=TOPK) for b in range(2)]

        EP = [ps(f"EP{p}", [P, 2, 512]) for p in range(2)]
        M2 = ps("M2", [P, 2, 512])
        PV = ps("PV", [P, 512])
        M3 = ps("M3", [P, 512])
        BANK = [EP[0][:, 0], EP[0][:, 1], EP[1][:, 0], EP[1][:, 1], M2[:, 0], M2[:, 1], PV[:, :], M3[:, :]]
        MR = [BANK[4], BANK[5], BANK[7]]

        ld_x, ld_c, ld_rope, ld_mod = [sem("ld_x0"), sem("ld_x1")], sem("ld_c"), sem("ld_rope"), sem("ld_mod")
        ld_qkv, ld_wo, ld_wr, ld_sh = sem("ld_qkv"), sem("ld_wo"), sem("ld_wr"), sem("ld_sh")
        ld_w = [sem(f"ld_w{r}") for r in range(RING // 2)]
        zero_st, zeros_ok = sem("zero_st"), sem("zeros_ok")
        s_ident, s_const, s_iota, s_pad, s_rstd, s_krep = (sem(n) for n in ("s_ident", "s_const", "s_iota", "s_pad", "s_rstd", "s_krep"))
        s_ec, s_crep, s_mod, s_modev, s_modok = (sem(n) for n in ("s_ec", "s_crep", "s_mod", "s_modev", "s_modok"))
        s_var, s_h, s_tr, s_trev = (sem(n) for n in ("s_var", "s_h", "s_tr", "s_trev"))
        s_qkv, s_qkvev, s_rope, s_qa = (sem(n) for n in ("s_qkv", "s_qkvev", "s_rope", "s_qa"))
        s_qk, s_qkA, s_qkD = (sem(n) for n in ("s_qk", "s_qkA", "s_qkD"))
        m_fill, m_free, s_negm = sem("m_fill"), sem("m_free"), sem("s_negm")
        e_fill, e_done, pv_step = sem("e_fill"), sem("e_done"), sem("pv_step")
        s_at, s_atev, s_wog, s_ao, s_x1 = (sem(n) for n in ("s_at", "s_atev", "s_wog", "s_ao", "s_x1"))
        s_var2, s_h2, s_tr2, s_tr2ev = (sem(n) for n in ("s_var2", "s_h2", "s_tr2", "s_tr2ev"))
        s_lg, s_ld, s_pe, s_mask, s_rank, s_slot, s_disp = (sem(n) for n in ("s_lg", "s_ld", "s_pe", "s_mask", "s_rank", "s_slot", "s_disp"))
        s_gate, s_up, s_silu, s_shh, s_shtr, s_shT, s_dn, s_sh = (sem(n) for n in ("s_gate", "s_up", "s_silu", "s_shh", "s_shtr", "s_shT", "s_dn", "s_sh"))
        xg_ld, y_st = [sem("xg_ld0"), sem("xg_ld1")], [sem("y_st0"), sem("y_st1")]
        m_xt, m_xtev, m_gu, m_silu, m_h, m_ht, m_htev, m_y, m_yev = (sem(f"m_{n}") for n in ("xt", "xtev", "gu", "silu", "h", "ht", "htev", "y", "yev"))
        o_ld = sem("o_ld")
        s_yg = [sem(f"s_yg{t}") for t in range(NT)]
        s_acc, s_fin, out_st, dv = sem("s_acc"), sem("s_fin"), sem("out_st"), sem("dv")

        block = ctx.enter_context(nc.Block())

        def q_unit(n):
            return divmod(n, 2)

        @block.sync
        def _(sp):
            for h in range(2):
                sp.dma_start(x[:, 4 * h:4 * h + 4, :],
                             x_in[512 * h:512 * h + 512, :].rearrange("(t p) d -> p t d", p=P)).then_inc(ld_x[h], 16)
                if h == 0:
                    sp.dma_start(ccol[:, 0, :], c_in).then_inc(ld_c, 16)
            sp.dma_start(wmod, wmod_in.rearrange("(c p) n -> p c n", p=P)).then_inc(ld_mod, 16)
            sp.dma_start(cosr[:, :, :], cos_in).then_inc(ld_rope, 16)
            sp.dma_start(sinr[:, :, :], sin_in).then_inc(ld_rope, 16)
            sp.dma_start(wqkv[:, :, :], wqkv_in.rearrange("(c p) n -> p c n", p=P)).then_inc(ld_qkv, 16)
            sp.dma_start(wo[:, :, :], wo_in.rearrange("(c p) n -> p c n", p=P)).then_inc(ld_wo, 16)
            sp.dma_start(wr[:, :, :], wr_in.rearrange("(c p) n -> p c n", p=P)).then_inc(ld_wr, 16)
            sp.dma_start(segu[:, :, :], segu_in.rearrange("(c p) n -> p c n", p=P)).then_inc(ld_sh, 16)
            sp.dma_start(sedn[:, 0:NSC - 1, :],
                         sedn_in[0:(NSC - 1) * P, :].rearrange("(c p) n -> p c n", p=P)).then_inc(ld_sh, 16)
            sp.dma_start(sedn[0:SLAST, NSC - 1, :], sedn_in[(NSC - 1) * P:ISH, :]).then_inc(ld_sh, 16)

            def load_pair(e, k):
                sp.dma_start(w13[:, k:k + 2, :], w13_in[bass.ds(e, 2), :, :].rearrange("e p n -> p e n")).then_inc(ld_w[k // 2], 16)
                sp.dma_start(w2[:, k:k + 2, :], w2_in[bass.ds(e, 2), :, :].rearrange("e p n -> p e n")).then_inc(ld_w[k // 2], 16)

            for k in range(0, RING, 2):
                load_pair(k, k)
            sp.wait_ge(zeros_ok, 1)
            for table in (xdisp, ydisp[NE * P:, :]):
                z = table.rearrange("(p r) n -> p (r n)", p=P)
                n = z.shape[1]
                for o in range(0, n // ZW, 8):
                    k = min(8, n // ZW - o)
                    sp.dma_start(z[:, o * ZW:(o + k) * ZW].rearrange("p (a n) -> p a n", n=ZW),
                                 small.unsqueeze(1).to_broadcast([P, k, ZW])).then_inc(zero_st, 16)
                if n % ZW:
                    sp.dma_start(z[:, n - n % ZW:], small[:, 0:n % ZW]).then_inc(zero_st, 16)

            def load_rows(e, b):
                sp.dma_start(XG[b], xdisp[bass.ds(e * P, P), :]).then_inc(xg_ld[b], 16)

            def store_rows(e, b):
                sp.dma_start(ydisp[bass.ds(e * P, P), :], YS[b]).then_inc(y_st[b], 16)

            def expert(e, k, weights, rows, store):
                if weights and k % 2 == 0:
                    sp.wait_ge(m_y, e - 2)
                    load_pair(e + 6, (k + 6) % RING)
                if rows:
                    sp.wait_ge(m_xt, e + 1)
                    load_rows(e + 2, k % 2)
                if store:
                    sp.wait_ge(m_yev, e - 2)
                    store_rows(e - 3, 1 - k % 2)

            sp.wait_ge(s_disp, 16 * NT * TOPK)
            load_rows(0, 0)
            load_rows(1, 1)
            for k in range(RING):
                expert(k, k, weights=k >= 4, rows=True, store=k >= 3)
            with sp.Fori(1, LAPS - 1) as o:
                for k in range(RING):
                    expert(o * RING + k, k, weights=True, rows=True, store=True)
            for k in range(RING + 3):
                e = NE - RING + k
                expert(e, k, weights=e + 7 < NE, rows=e + 2 < NE, store=True)
            sp.wait_ge(s_slot, 2)
            nov = sp.value_load(novi[0:1, 0:1], min_val=1, max_val=MAXOV)
            with sp.Fori(0, nov) as b:
                sp.wait_ge(m_yev, b + NE)
                e = sp.value_load(ovei[0:1, bass.ds(b, 1)], min_val=0, max_val=NE - 1)
                sp.dma_start(w13[:, 0, :], w13_in[bass.ds(e, 1), :, :].rearrange("e p n -> p (e n)")).then_inc(o_ld, 16)
                sp.dma_start(w2[:, 0, :], w2_in[bass.ds(e, 1), :, :].rearrange("e p n -> p (e n)")).then_inc(o_ld, 16)
                sp.dma_start(XG[0], xdisp[bass.ds((b + NE) * P, P), :]).then_inc(o_ld, 16)
                sp.wait_ge(m_yev, b + (NE + 1))
                sp.dma_start(ydisp[bass.ds((b + NE) * P, P), :], YS[0]).then_inc(y_st[0], 16)
            for t in range(NT):
                sp.wait_ge(s_fin, t + 1)
                sp.dma_start(out[t * P:(t + 1) * P, :], x[:, t, :]).then_inc(out_st, 16)
            sp.wait_ge(out_st, 16 * NT)

        @block.gpsimd
        def _(pool):
            pool.memset(ident[:, :], 0.0).then_inc(s_ident, 1)
            pool.memset(ones[:, :], 1.0).then_inc(s_const, 1)
            pool.memset(onesb[:, :], 1.0).then_inc(s_const, 1)
            pool.wait_ge(s_ident, 1)
            pool.affine_select(out=ident[:, :], in_=ident[:, :], compare_op=ALU.not_equal, fill=1.0,
                               base=0, pattern=[[-1, P]], channel_multiplier=1).then_inc(s_ident, 1)
            pool.memset(mhalf[:, :], -0.5).then_inc(s_const, 1)
            for h in range(2):
                pool.wait_ge(s_const, 3)
                pool.wait_ge(s_var, h + 1)
                pool.tensor_tensor(rstd[:, 4 * h:4 * h + 4], veps[:, 4 * h:4 * h + 4], mhalf[:, 0:4], ALU.pow).then_inc(s_rstd, 1)
            pool.memset(QA[:, :, :, :], 0.0).then_inc(s_pad, 1)
            pool.memset(KA[:, :, :, :], 0.0).then_inc(s_pad, 1)
            pool.memset(VA[:, :, :, :], 0.0).then_inc(s_pad, 1)
            pool.wait_ge(s_pad, 3)
            pool.memset(KA[:, :, :, :].rearrange("p t g (j c) -> p (t g j) c", c=HP)[:, :, HD:HD + 1], 1.0).then_inc(s_pad, 1)
            pool.memset(VA[:, :, :, HD:HD + 1], 1.0).then_inc(s_pad, 1)
            pool.wait_ge(s_pad, 5)
            KA5 = KA[:, :, :, :].rearrange("p t g (j c) -> p t g j c", c=HP)
            for h in range(2):
                tt = slice(4 * h, 4 * h + 4)
                pool.wait_ge(s_rope, h + 1)
                for j in range(4):
                    pool.tensor_copy(KA5[:, tt, :, j, 0:HD],
                                     qkv[:, tt, NH * HD:(NH + NG) * HD].rearrange("p t (g d) -> p t g d", g=NG))\
                        .then_inc(s_krep, 1)
                pool.tensor_copy(VA[:, tt, :, 0:HD],
                                 qkv[:, tt, (NH + NG) * HD:].rearrange("p t (g d) -> p t g d", g=NG)).then_inc(s_krep, 1)
            pool.wait_ge(s_qkv, NT)
            pool.memset(small, 0.0).then_inc(zeros_ok, 1)
            pool.affine_select(out=upper[:, :], in_=onesb[:, :], compare_op=ALU.is_gt, fill=0.0,
                               base=0, pattern=[[1, P]], channel_multiplier=-1).then_inc(s_const, 1)
            pool.iota(iota_i[:, :], pattern=[[1, NE]], base=0, channel_multiplier=0).then_inc(s_iota, 1)
            pool.wait_ge(s_iota, 1)
            pool.tensor_copy(iotaf[:, :], iota_i[:, :]).then_inc(s_iota, 1)
            for h in range(2):
                pool.wait_ge(s_var2, h + 1)
                pool.tensor_tensor(rstd[:, 4 * h:4 * h + 4], veps[:, 4 * h:4 * h + 4], mhalf[:, 0:4], ALU.pow).then_inc(s_rstd, 1)
            pool.wait_ge(zero_st, 16 * N_ZERO)
            pool.wait_ge(s_slot, 1)
            pool.wait_ge(s_h2, 2)
            for t in range(NT):
                for k in range(TOPK):
                    i = t * TOPK + k
                    pool.indirect_dma_start(out=xdisp, out_offset=bass.IndirectOffsetOnAxis(ap=sloti[:, i:i + 1], axis=0),
                                            in_=xh[:, t, :], in_offset=None).then_inc(s_disp, 16)
            pool.wait_ge(s_slot, 2)
            nov = pool.value_load(novi[0:1, 0:1], min_val=1, max_val=MAXOV)
            with pool.Fori(0, nov) as b:
                pool.wait_ge(y_st[0], b * 16 + 16 * (NE // 2 + 1))
            pool.wait_ge(y_st[1], 16 * (NE // 2))
            for t in range(NT):
                if t >= 4:
                    pool.wait_ge(s_acc, t - 3)
                for k in range(TOPK):
                    i = t * TOPK + k
                    pool.indirect_dma_start(out=YG[t % 4][:, k, :], out_offset=None, in_=ydisp,
                                            in_offset=bass.IndirectOffsetOnAxis(ap=sloti[:, i:i + 1], axis=0)).then_inc(s_yg[t], 16)

        @block.scalar
        def _(act):
            act.wait_ge(ld_c, 16)
            nc.scalar.activation(ccol[:, 1, :], ccol[:, 0, :], ACT.Exp, scale=-1.0).then_inc(s_ec, 1)
            act.wait_ge(s_mod, 1)
            nc.scalar.activation(MOD[:, 0:4, :], EP[0][:, :, :].rearrange("p a (b n) -> p (a b) n", b=2), ACT.Copy).then_inc(s_modev, 1)
            nc.scalar.activation(MOD[:, 4:6, :], BANK[2].rearrange("p (b n) -> p b n", b=2), ACT.Copy).then_inc(s_modev, 1)
            for tp in range(NT // 2):
                act.wait_ge(s_tr, tp + 1)
                for c in range(NC):
                    ins = nc.scalar.activation(hT[:, c, 256 * tp:256 * tp + 256].rearrange("p (t n) -> p t n", t=2),
                                               BANK[3 + tp].rearrange("p (t c n) -> p t c n", t=2, c=NC)[:, :, c, :], ACT.Copy)
                ins.then_inc(s_trev, 1)
            for t in range(NT):
                act.wait_ge(s_qkv, t + 1)
                nc.scalar.activation(qkv[:, t, :], BANK[(7 + t) % 8][:, 0:QKV], ACT.Copy).then_inc(s_qkvev, 1)
            act.wait_ge(s_pad, 1)
            for h in range(2):
                tt = slice(4 * h, 4 * h + 4)
                act.wait_ge(s_rope, h + 1)
                nc.scalar.activation(QA[:, tt, :, :].rearrange("p t g (j c) -> p t (g j) c", c=HP)[:, :, :, 0:HD],
                                     qkv[:, tt, 0:NH * HD].rearrange("p t (h d) -> p t h d", d=HD), ACT.Copy).then_inc(s_qa, 1)
            for n in range(0, 16, 2):
                h, g = n // 8, (n % 8) // 2
                act.wait_ge(s_qk, n + 1)
                nc.scalar.activation(QT[:, g, 512 * h:512 * h + 512], BANK[n % 8], ACT.Copy).then_inc(s_qkA, 1)

            for n in range(STEPS):
                for p in range(2):
                    if p == 1 and n % NT == 0 and n:
                        u = n // NT - 1
                        act.wait_ge(pv_step, NT * (u + 1))
                        if u:
                            act.wait_ge(m_fill, O_FILL[u - 1])
                        nc.scalar.activation(OT[:, :], PV[:, :], ACT.Copy).then_inc(s_atev, 1)
                    act.wait_ge(e_fill, 2 * n + p + 1)
                    if n >= 3 and p == 0:
                        act.wait_ge(pv_step, n - 2)
                    nc.scalar.activation(PT[n % 3][:, 2 * p:2 * p + 2, :], EP[p][:, :, :], ACT.Exp, scale=HD ** -0.5).then_inc(e_done, 1)
            act.wait_ge(pv_step, STEPS)
            act.wait_ge(m_fill, O_FILL[U - 2])
            nc.scalar.activation(OT[:, :], PV[:, :], ACT.Copy).then_inc(s_atev, 1)

            for tp in range(NT // 2):
                act.wait_ge(s_at, tp + 1)
                for c in range(NC):
                    ins = nc.scalar.activation(hT[:, c, 256 * tp:256 * tp + 256].rearrange("p (t n) -> p t n", t=2),
                                               BANK[tp].rearrange("p (t c n) -> p t c n", t=2, c=NC)[:, :, c, :], ACT.Copy)
                ins.then_inc(s_trev, 1)
            for tp in range(NT // 2):
                act.wait_ge(s_tr2, tp + 1)
                for c in range(NC):
                    ins = nc.scalar.activation(h2T[:, c, 256 * tp:256 * tp + 256].rearrange("p (t n) -> p t n", t=2),
                                               BANK[tp].rearrange("p (t c n) -> p t c n", t=2, c=NC)[:, :, c, :], ACT.Copy)
                ins.then_inc(s_tr2ev, 1)
            act.wait_ge(s_ld, 1)
            nc.scalar.activation(probs[:, :, :], probs[:, :, :], ACT.Exp).then_inc(s_pe, 1)
            nc.scalar.activation(sgate[:, 0, :], sgate[:, 1, :], ACT.Exp, scale=-1.0).then_inc(s_pe, 1)
            def shared_evac(t):
                act.wait_ge(s_shtr, t + 1)
                if t:
                    act.wait_ge(s_dn, t)
                nc.scalar.activation(shT[:, 0:4, :], BANK[4].rearrange("p (c n) -> p c n", c=4), ACT.Copy)
                nc.scalar.activation(shT[:, 4, :], BANK[5][:, 0:P], ACT.Copy)
                nc.scalar.activation(shT[0:SLAST, 5, :], BANK[5][0:SLAST, P:2 * P], ACT.Copy).then_inc(s_shT, 1)

            for t in range(NT):
                act.wait_ge(s_gate, t + 1)
                if t:
                    act.wait_ge(s_shh, t)
                nc.scalar.activation(shg.rearrange("p (a n) -> p a n", a=2), EP[0][:, :, 0:SHH], ACT.Silu).then_inc(s_silu, 1)
                if t > 1:
                    shared_evac(t - 2)
            shared_evac(NT - 2)
            shared_evac(NT - 1)

            def silu(e, b, first=False):
                act.wait_ge(m_gu, e + 1)
                if not first:
                    act.wait_ge(m_h, e - 1)
                nc.scalar.activation(SL[b], BANK[b][:, 0:I], ACT.Silu).then_inc(m_silu, 1)

            def result(e, b, stored):
                act.wait_ge(m_y, e + 1)
                if stored is not None:
                    act.wait_ge(y_st[b], stored)
                nc.scalar.activation(YS[b], BANK[6 + b][:, 0:D], ACT.Copy).then_inc(m_yev, 1)

            for k in range(RING):
                silu(k, k % 2, first=k < 2)
                if k >= 2:
                    result(k - 2, k % 2, 16 * ((k - 2) // 2) if k >= 4 else None)
            with act.Fori(1, LAPS - 1) as o:
                for k in range(RING):
                    silu(o * RING + k, k % 2)
                    result(o * RING + (k - 2), k % 2, o * (16 * RING // 2) + 16 * (k // 2 - 1))
            for e in range(NE - RING, NE):
                silu(e, e % 2)
                result(e - 2, e % 2, 16 * ((e - 2) // 2))
            for e in (NE - 2, NE - 1):
                result(e, e % 2, 16 * (e // 2))
            act.wait_ge(s_slot, 2)
            nov = act.value_load(novi[0:1, 0:1], min_val=1, max_val=MAXOV)
            with act.Fori(0, nov) as i:
                act.wait_ge(m_gu, i + (NE + 1))
                act.wait_ge(m_h, i + NE)
                nc.scalar.activation(SL[0], BANK[0][:, 0:I], ACT.Silu).then_inc(m_silu, 1)
                act.wait_ge(m_y, i + (NE + 1))
                act.wait_ge(y_st[0], i * 16 + 16 * (NE // 2))
                nc.scalar.activation(YS[0], BANK[6][:, 0:D], ACT.Copy).then_inc(m_yev, 1)

        @block.vector
        def _(dve):
            count = [0]

            def then(ins):
                count[0] += 1
                ins.then_inc(dv, 1)
                dve.wait_ge(dv, count[0])

            def statistics(h, var_sem):
                for t in range(4 * h, 4 * h + 4):
                    ins = nc.vector.bn_stats(stats[:, t, :], x[:, t, :])
                then(ins)
                for t in range(4 * h, 4 * h + 4):
                    ins = nc.vector.bn_aggr(mv[:, t, :], stats[:, t, :])
                then(ins)
                nc.vector.tensor_scalar(veps[:, 4 * h:4 * h + 4], mv[:, 4 * h:4 * h + 4, 1], EPS, None, ALU.add).then_inc(var_sem, 1)

            def modulate(h, k, done):
                tt = slice(4 * h, 4 * h + 4)
                for t in range(4 * h, 4 * h + 4):
                    ins = nc.vector.tensor_scalar(xh[:, t, :], x[:, t, :], mv[:, t, 0:1], rstd[:, t:t + 1], ALU.subtract, ALU.mult)
                then(ins)
                then(nc.vector.tensor_tensor(xh[:, tt, :], xh[:, tt, :], MOD[:, k + 1:k + 2, :].to_broadcast([P, 4, D]), ALU.mult))
                nc.vector.tensor_tensor(xh[:, tt, :], xh[:, tt, :], MOD[:, k:k + 1, :].to_broadcast([P, 4, D]), ALU.add).then_inc(done, 1)

            dve.wait_ge(s_ec, 1)
            then(nc.vector.tensor_scalar(ccol[:, 2, :], ccol[:, 1, :], 1.0, None, ALU.add))
            then(nc.vector.reciprocal(ccol[:, 2, :], ccol[:, 2, :]))
            then(nc.vector.tensor_tensor(ccol[:, 3, :], ccol[:, 0, :], ccol[:, 2, :], ALU.mult))
            dve.wait_ge(s_const, 1)
            for c in range(NC):
                ins = nc.vector.tensor_scalar(crep[:, c, :], ones[:, :], ccol[:, 3, c:c + 1], None, ALU.mult)
            ins.then_inc(s_crep, 1)
            for h in range(2):
                dve.wait_ge(ld_x[h], 16)
                statistics(h, s_var)
            dve.wait_ge(s_modev, 2)
            for k in (1, 4):
                ins = nc.vector.tensor_scalar(MOD[:, k, :], MOD[:, k, :], 1.0, None, ALU.add)
            then(ins)
            for h in range(2):
                dve.wait_ge(s_rstd, h + 1)
                modulate(h, 0, s_h)
            dve.wait_ge(ld_rope, 32)
            for h in range(2):
                tt = slice(4 * h, 4 * h + 4)
                dve.wait_ge(s_qkvev, 4 * h + 4)
                pr = qkv[:, tt, 0:(NH + NG) * HD].rearrange("p t (h i two) -> p t h i two", h=NH + NG, two=2)
                a, b = pr[:, :, :, 0:4, 0], pr[:, :, :, 0:4, 1]
                cs = [w[:, tt, :].unsqueeze(2).to_broadcast([P, 4, NH + NG, 4]) for w in (cosr, sinr)]
                R = [rt[:, k].rearrange("p t (h i) -> p t h i", i=4) for k in range(4)]
                nc.vector.tensor_tensor(R[0], a, cs[0], ALU.mult)
                nc.vector.tensor_tensor(R[1], b, cs[1], ALU.mult)
                nc.vector.tensor_tensor(R[2], a, cs[1], ALU.mult)
                then(nc.vector.tensor_tensor(R[3], b, cs[0], ALU.mult))
                nc.vector.tensor_tensor(a, R[0], R[1], ALU.subtract)
                nc.vector.tensor_tensor(b, R[2], R[3], ALU.add).then_inc(s_rope, 1)
                dve.wait_ge(s_rope, h + 1)
            for n in range(1, 16, 2):
                h, g = n // 8, (n % 8) // 2
                dve.wait_ge(s_qk, n + 1)
                nc.vector.tensor_copy(KT[:, g, 512 * h:512 * h + 512], BANK[n % 8]).then_inc(s_qkD, 1)
            for k in (2, 5):
                g0 = gtmp[:, 0, :]
                g1 = gtmp[:, 1, :]
                nc.vector.tensor_scalar(g0, MOD[:, k, :], 0.0, 2.0, ALU.is_ge, ALU.mult)
                then(nc.vector.scalar_tensor_tensor(out=g1, in0=MOD[:, k, :], scalar=-1.0, in1=MOD[:, k, :], op0=ALU.mult, op1=ALU.max))
                then(nc.vector.tensor_scalar(g1, g1, 0.25, None, ALU.max))
                then(nc.vector.scalar_tensor_tensor(out=MOD[:, k, :], in0=g0, scalar=-1.0, in1=g1, op0=ALU.add, op1=ALU.mult))
            dve.wait_ge(ld_wo, 16)
            nc.vector.tensor_tensor(wog[:, :, :], wo[:, :, :], MOD[:, 2:3, :].to_broadcast([P, NC, D]), ALU.mult).then_inc(s_wog, 1)

            ring = [0]

            def take():
                ring[0] += 1
                dve.wait_ge(m_fill, ring[0])
                return MR[(ring[0] - 1) % 3]

            def row_max(k, heads):
                u, s = divmod(k, NT)
                for j in heads:
                    src = take()
                    nc.vector.reduce_max(mx[:, u % 2, s // 2, j, s % 2:s % 2 + 1], src, AX.X).then_inc(m_free, 1)

            def minus_max(u):
                g, qh = q_unit(u)
                dve.wait_ge(m_free, ring[0])
                nc.vector.tensor_reduce(out=QA[:, 4 * qh:4 * qh + 4, g, :].rearrange("p t (j c) -> p t j c", c=HP)[:, :, :, HD],
                                        in_=mx[:, u % 2], axis=AX.X, op=ALU.max, negate=True).then_inc(s_negm, 1)

            def take_q(u):
                g, qh = q_unit(u)
                src = take()
                nc.vector.tensor_copy(QT[:, g, 512 * qh:512 * qh + 512], src).then_inc(m_free, 1)

            def take_output(u):
                g, qh = q_unit(u)
                o = take().rearrange("p (t j c) -> p t j c", t=4, j=4)
                then(nc.vector.reciprocal(rsum[:, u % 2], o[:, :, :, HD]))
                for t in range(4):
                    ins = nc.vector.tensor_tensor(AT[:, 4 * qh + t, 4 * HD * g:4 * HD * (g + 1)].rearrange("p (j d) -> p j d", j=4),
                                                  o[:, t, :, 0:HD], rsum[:, u % 2, t, :].unsqueeze(2).to_broadcast([P, 4, HD]), ALU.mult)
                ins.then_inc(m_free, 1)

            for k in range(LEAD):
                row_max(k, (2, 3, 0, 1))
                if k % NT == NT - 1:
                    minus_max(k // NT)
            take_q(0)
            for n in range(STEPS):
                k = n + LEAD
                if k < STEPS:
                    row_max(k, (2, 3))
                if n % NT == 2 and n > NT:
                    take_output(n // NT - 1)
                if k < STEPS:
                    row_max(k, (0, 1))
                    if k % NT == NT - 1:
                        minus_max(k // NT)
                if n % NT == NT - 1 and n < STEPS - 1:
                    take_q(n // NT + 1)
            take_output(U - 1)

            for tp in range(NT // 2):
                dve.wait_ge(s_ao, tp + 1)
                nc.vector.tensor_tensor(x[:, 2 * tp:2 * tp + 2, :], x[:, 2 * tp:2 * tp + 2, :],
                                        BANK[4 + tp].rearrange("p (t n) -> p t n", t=2), ALU.add).then_inc(s_x1, 1)
                if tp % 2:
                    dve.wait_ge(s_x1, tp + 1)
                    statistics(tp // 2, s_var2)
            for h in range(2):
                dve.wait_ge(s_rstd, h + 3)
                modulate(h, 3, s_h2)

            dve.wait_ge(s_lg, 1)
            lg = BANK[7][:, 0:NT * (NE + 1)].rearrange("p (t e) -> p t e", t=NT)
            sm = small
            dve.wait_ge(zero_st, 16 * N_ZERO)
            mxl, sml = sm[:, 0:NT], sm[:, NT:2 * NT]
            then(nc.vector.reduce_max(mxl, lg[:, :, 0:NE], AX.X))
            nc.vector.tensor_copy(sgate[:, 1, :], lg[:, :, NE])
            nc.vector.tensor_tensor(probs[:, :, :], lg[:, :, 0:NE], mxl.unsqueeze(2).to_broadcast([P, NT, NE]), ALU.subtract).then_inc(s_ld, 1)
            dve.wait_ge(s_pe, 2)
            then(nc.vector.reduce_sum(sml, probs[:, :, :], AX.X))
            then(nc.vector.reciprocal(sml, sml))
            then(nc.vector.tensor_tensor(probs[:, :, :], probs[:, :, :], sml.unsqueeze(2).to_broadcast([P, NT, NE]), ALU.mult))
            for t in range(NT):
                ins = nc.vector.max(top[:, t, :], probs[:, t, :])
            then(ins)
            for t in range(NT):
                ins = nc.vector.max_index(topi[:, t, :], top[:, t, :], probs[:, t, :])
            then(ins)
            then(nc.vector.tensor_copy(topf[:, :, :], topi[:, :, :]))
            dve.wait_ge(s_iota, 2)
            for t in range(NT):
                ins = nc.vector.tensor_tensor(OH[:, t], iotaf[:, :].unsqueeze(1).to_broadcast([P, TOPK, NE]),
                                              topf[:, t, 0:TOPK].unsqueeze(2).to_broadcast([P, TOPK, NE]), ALU.is_equal)
            then(ins)
            nc.vector.tensor_reduce(out=mask[:, :, :], in_=OH.rearrange("p t k e -> p t e k"), axis=AX.X, op=ALU.max).then_inc(s_mask, 1)
            then(nc.vector.tensor_scalar(sgate[:, 1, :], sgate[:, 0, :], 1.0, None, ALU.add))
            then(nc.vector.reciprocal(sgate[:, 0, :], sgate[:, 1, :]))
            cnt, nov, inc, off, base = (sm[:, 64 * (k + 1):64 * (k + 1) + NE] for k in range(5))
            thr = sm[:, 400:400 + NT - 1]
            nc.vector.tensor_scalar(thr, iotaf[:, 1:NT], float(P), None, ALU.mult)
            then(nc.vector.tensor_scalar(base, iotaf[:, :], float(P), None, ALU.mult))
            dve.wait_ge(s_rank, 1)
            rank = BANK[6][:, 0:NT * NE].rearrange("p (t e) -> p t e", t=NT)
            then(nc.vector.tensor_copy(cnt, BANK[5][:, 0:NE]))
            then(nc.vector.tensor_tensor(gt, cnt.unsqueeze(2).to_broadcast([P, NE, NT - 1]),
                                         thr.unsqueeze(1).to_broadcast([P, NE, NT - 1]), ALU.is_gt))
            then(nc.vector.reduce_sum(nov, gt, AX.X))
            then(nc.vector.tensor_tensor_scan(inc, ones[:, 0:NE], nov, 0.0, ALU.mult, ALU.add))
            then(nc.vector.tensor_tensor(off, inc, nov, ALU.subtract))
            then(nc.vector.tensor_scalar(off, off, float(P), float(P * (NE - 1)), ALU.mult, ALU.add))
            then(nc.vector.tensor_tensor(off, off, base, ALU.subtract))
            nc.vector.scalar_tensor_tensor(out=slot[:, :, :], in0=rank, scalar=float(P), in1=off.unsqueeze(1).to_broadcast([P, NT, NE]),
                                           op0=ALU.is_ge, op1=ALU.mult)
            then(nc.vector.tensor_tensor(probs[:, :, :], rank, base.unsqueeze(1).to_broadcast([P, NT, NE]), ALU.add))
            then(nc.vector.tensor_tensor(slot[:, :, :], slot[:, :, :], probs[:, :, :], ALU.add))
            then(nc.vector.tensor_tensor(PR, OH, slot[:, :, :].unsqueeze(2).to_broadcast([P, NT, TOPK, NE]), ALU.mult))
            then(nc.vector.reduce_sum(slotk[:, :], PR.rearrange("p t k e -> p (t k) e"), AX.X))
            nc.vector.tensor_copy(sloti[:, :], slotk[:, :]).then_inc(s_slot, 1)
            nc.vector.tensor_scalar(novi[0:1, 0:1], inc[0:1, NE - 1:NE], 1.0, None, ALU.max)
            ove = PR.rearrange("p t k e -> p (t k) e")[0:1, 0:MAXOV]
            then(nc.vector.tensor_tensor(ove, inc[0:1, :].unsqueeze(1).to_broadcast([1, MAXOV, NE]),
                                         iotaf[0:1, 0:MAXOV].unsqueeze(2).to_broadcast([1, MAXOV, NE]), ALU.is_le))
            then(nc.vector.reduce_sum(slotk[0:1, 0:MAXOV], ove, AX.X))
            nc.vector.tensor_scalar(ovei[0:1, 0:MAXOV], slotk[0:1, 0:MAXOV], float(NE - 1), None, ALU.min).then_inc(s_slot, 1)

            def shared_out(t):
                dve.wait_ge(s_dn, t + 1)
                nc.vector.tensor_scalar(SH[:, t, :], BANK[6 + t % 2][:, 0:D], sgate[:, 0, t:t + 1], None, ALU.mult).then_inc(s_sh, 1)

            for t in range(NT):
                dve.wait_ge(s_silu, t + 1)
                dve.wait_ge(s_up, t + 1)
                if t >= 2:
                    dve.wait_ge(s_shtr, t - 1)
                nc.vector.tensor_tensor(shh[t % 2].rearrange("p (a n) -> p a n", a=2), shg.rearrange("p (a n) -> p a n", a=2),
                                        EP[1][:, :, 0:SHH], ALU.mult).then_inc(s_shh, 1)
                if t > 1:
                    shared_out(t - 2)
            shared_out(NT - 2)
            shared_out(NT - 1)

            def hidden_T(e1, b):
                dve.wait_ge(m_ht, e1)
                nc.vector.tensor_copy(HST[b], BANK[4 + b][0:IC, 0:2 * P]).then_inc(m_htev, 1)

            def rows_T(e1, b):
                dve.wait_ge(m_xt, e1)
                nc.vector.tensor_copy(XGT[b], BANK[2 + b][:, 0:D]).then_inc(m_xtev, 1)

            def hidden(e1, b):
                dve.wait_ge(m_silu, e1)
                nc.vector.tensor_tensor(HS[b], SL[b], BANK[b][:, I:2 * I], ALU.mult).then_inc(m_h, 1)

            def expert(e, k, prev, nxt):
                if prev:
                    hidden_T(e, 1 - k % 2)
                if nxt:
                    rows_T(e + 2, 1 - k % 2)
                hidden(e + 1, k % 2)

            rows_T(1, 0)
            for k in range(RING):
                expert(k, k, prev=k > 0, nxt=True)
            with dve.Fori(1, LAPS - 1) as o:
                for k in range(RING):
                    expert(o * RING + k, k, prev=True, nxt=True)
            for e in range(NE - RING, NE):
                expert(e, e, prev=True, nxt=e + 1 < NE)
            hidden_T(NE, 1)
            dve.wait_ge(s_slot, 2)
            nov_r = dve.value_load(novi[0:1, 0:1], min_val=1, max_val=MAXOV)
            with dve.Fori(0, nov_r) as i:
                rows_T(i + (NE + 1), 0)
                hidden(i + (NE + 1), 0)
                hidden_T(i + (NE + 1), 0)

            for t in range(NT):
                dve.wait_ge(s_yg[t], 16 * TOPK)
                for k in range(TOPK):
                    ins = nc.vector.scalar_tensor_tensor(out=SH[:, t, :], in0=YG[t % 4][:, k, :], scalar=top[:, t, k:k + 1],
                                                         in1=SH[:, t, :], op0=ALU.mult, op1=ALU.add)
                    if k < TOPK - 1:
                        then(ins)
                ins.then_inc(s_acc, 1)
                dve.wait_ge(s_acc, t + 1)
                then(nc.vector.tensor_tensor(SH[:, t, :], SH[:, t, :], MOD[:, 5, :], ALU.mult))
                nc.vector.tensor_tensor(x[:, t, :], x[:, t, :], SH[:, t, :], ALU.add).then_inc(s_fin, 1)

        @block.tensor
        def _(pe):
            mm, tr = nc.tensor.matmul, nc.tensor.transpose
            I_ = ident[:, :]

            def transpose_tiles(src, bank, tp):
                for t in range(2):
                    for c in range(NC):
                        o = (t * NC + c) * P
                        ins = tr(bank[:, o:o + P], src[:, 2 * tp + t, c * P:(c + 1) * P], I_)
                return ins

            pe.wait_ge(s_crep, 1)
            pe.wait_ge(ld_mod, 16)
            for b in range(3):
                for c in range(NC):
                    ins = mm(BANK[b], crep[:, c, :], wmod[:, c, 512 * b:512 * b + 512], start=c == 0, stop=c == NC - 1)
            ins.then_inc(s_mod, 1)
            pe.wait_ge(s_ident, 2)
            for tp in range(NT // 2):
                pe.wait_ge(s_h, tp // 2 + 1)
                transpose_tiles(xh, BANK[3 + tp], tp).then_inc(s_tr, 1)
            pe.wait_ge(ld_qkv, 16)
            pe.wait_ge(s_modev, 2)
            for t in range(NT):
                pe.wait_ge(s_trev, max(t // 2 + 1, t - 3))
                for c in range(NC):
                    ins = mm(BANK[(7 + t) % 8][:, 0:QKV], hT[:, c, t * P:(t + 1) * P], wqkv[:, c, :], start=c == 0, stop=c == NC - 1)
                ins.then_inc(s_qkv, 1)
            pe.wait_ge(s_qkvev, NT)
            for n in range(16):
                h, g, k = n // 8, (n % 8) // 2, n % 2
                if n % 8 == 0:
                    pe.wait_ge(s_qa, h + 1)
                    pe.wait_ge(s_krep, 5 * (h + 1))
                if n >= 8:
                    pe.wait_ge(s_qkA if k == 0 else s_qkD, (n - 8) // 2 + 1)
                for t in range(4):
                    ins = tr(BANK[n % 8][:, t * P:(t + 1) * P], (KA if k else QA)[:, 4 * h + t, g, :], I_)
                ins.then_inc(s_qk, 1)
            pe.wait_ge(s_qkA, 8)
            pe.wait_ge(s_qkD, 8)

            ring = [0]

            def fill():
                n = ring[0]
                ring[0] += 1
                if n >= 3:
                    pe.wait_ge(m_free, n - 2)
                return MR[n % 3]

            def scores_for_max(k, heads):
                u, s = divmod(k, NT)
                g, qh = q_unit(u)
                q0 = (4 * qh + s // 2) * P
                for j in heads:
                    r = slice(HP * j, HP * j + HD)
                    mm(fill(), QT[r, g, q0:q0 + P], KT[r, g, 512 * (s % 2):512 * (s % 2) + 512], start=True, stop=True).then_inc(m_fill, 1)

            def transpose_q(u):
                g, qh = q_unit(u)
                pe.wait_ge(s_negm, u + 1)
                b = fill()
                for t in range(4):
                    ins = tr(b[:, t * P:(t + 1) * P], QA[:, 4 * qh + t, g, :], I_)
                ins.then_inc(m_fill, 1)

            def transpose_output(u):
                pe.wait_ge(s_atev, u + 1)
                b = fill()
                for t in range(4):
                    ins = tr(b[:, t * P:(t + 1) * P], OT[:, t * P:(t + 1) * P], I_)
                ins.then_inc(m_fill, 1)

            def scores(n, p):
                u, tt = divmod(n, NT)
                g, qh = q_unit(u)
                if n:
                    pe.wait_ge(e_done, 2 * (n - 1) + p + 1)
                for i in range(2):
                    j = 2 * p + i
                    r = slice(HP * j, HP * j + HD + 1)
                    ins = mm(EP[p][:, i, :], KT[r, g, tt * P:(tt + 1) * P], QT[r, g, 512 * qh:512 * qh + 512], start=True, stop=True)
                ins.then_inc(e_fill, 1)

            def output(n):
                u, tt = divmod(n, NT)
                g, qh = q_unit(u)
                pe.wait_ge(e_done, 2 * n + 2)
                if tt == 0 and u:
                    pe.wait_ge(s_atev, u)
                for j in range(4):
                    ins = mm(PV[HP * j:HP * j + HP, :], VA[:, tt, g, :], PT[n % 3][:, j, :], start=tt == 0, stop=tt == NT - 1)
                ins.then_inc(pv_step, 1)

            for k in range(LEAD):
                scores_for_max(k, (2, 3, 0, 1))
            transpose_q(0)
            for n in range(STEPS):
                k = n + LEAD
                u = n // NT
                if n % NT == 0:
                    pe.wait_ge(m_free, Q_FILL[u])
                scores(n, 0)
                if k < STEPS:
                    scores_for_max(k, (2, 3))
                if n:
                    output(n - 1)
                if n % NT == 2 and n > NT:
                    transpose_output(u - 1)
                scores(n, 1)
                if k < STEPS:
                    scores_for_max(k, (0, 1))
                if n % NT == NT - 1 and n < STEPS - 1:
                    transpose_q(u + 1)
            output(STEPS - 1)
            transpose_output(U - 1)

            pe.wait_ge(m_free, ring[0])
            for tp in range(NT // 2):
                transpose_tiles(AT, BANK[tp], tp).then_inc(s_at, 1)
            pe.wait_ge(s_wog, 1)
            for tp in range(NT // 2):
                pe.wait_ge(s_trev, NT // 2 + tp + 1)
                for t in range(2):
                    for c in range(NC):
                        ins = mm(BANK[4 + tp][:, t * D:(t + 1) * D], hT[:, c, (2 * tp + t) * P:(2 * tp + t + 1) * P],
                                 wog[:, c, :], start=c == 0, stop=c == NC - 1)
                ins.then_inc(s_ao, 1)
            for tp in range(NT // 2):
                pe.wait_ge(s_h2, tp // 2 + 1)
                transpose_tiles(xh, BANK[tp], tp).then_inc(s_tr2, 1)
            pe.wait_ge(ld_wr, 16)
            for t in range(NT):
                pe.wait_ge(s_tr2ev, t // 2 + 1)
                for c in range(NC):
                    ins = mm(BANK[7][:, t * (NE + 1):(t + 1) * (NE + 1)], h2T[:, c, t * P:(t + 1) * P], wr[:, c, :],
                             start=c == 0, stop=c == NC - 1)
            ins.then_inc(s_lg, 1)

            def ranks():
                pe.wait_ge(s_mask, 1)
                for t in range(NT):
                    for s in range(t):
                        mm(BANK[6][:, t * NE:(t + 1) * NE], onesb[:, :], mask[:, s, :], start=s == 0, stop=False)
                    mm(BANK[6][:, t * NE:(t + 1) * NE], upper[:, :], mask[:, t, :], start=t == 0, stop=True)
                for t in range(NT):
                    ins = mm(BANK[5][:, 0:NE], onesb[:, :], mask[:, t, :], start=t == 0, stop=t == NT - 1)
                ins.then_inc(s_rank, 1)

            def shared_in(t, part, done):
                for a in range(2):
                    for c in range(NC):
                        o = part * ISH + a * SHH
                        ins = mm(EP[part][:, a, 0:SHH], h2T[:, c, t * P:(t + 1) * P], segu[:, c, o:o + SHH], start=c == 0, stop=c == NC - 1)
                ins.then_inc(done, 1)

            def shared_T(t):
                pe.wait_ge(s_shh, t + 1)
                if t:
                    pe.wait_ge(s_shT, t)
                for c in range(NSC):
                    w = P if c < NSC - 1 else SLAST
                    ins = tr(BANK[4 + c // 4][0:w, (c % 4) * P:(c % 4 + 1) * P], shh[t % 2][:, c * P:c * P + w], I_)
                ins.then_inc(s_shtr, 1)

            def shared_down(t):
                pe.wait_ge(s_shT, t + 1)
                if t >= 2:
                    pe.wait_ge(s_sh, t - 1)
                for c in range(NSC):
                    w = P if c < NSC - 1 else SLAST
                    ins = mm(BANK[6 + t % 2][:, 0:D], shT[0:w, c, :], sedn[0:w, c, :], start=c == 0, stop=c == NSC - 1)
                ins.then_inc(s_dn, 1)

            pe.wait_ge(ld_sh, 48)
            for t in range(NT):
                if t:
                    pe.wait_ge(s_silu, t)
                shared_in(t, 0, s_gate)
                if t == 1:
                    ranks()
                if t == 2:
                    pe.wait_ge(s_slot, 1)
                if t > 1:
                    shared_T(t - 2)
                if t:
                    pe.wait_ge(s_shh, t)
                shared_in(t, 1, s_up)
                if t > 1:
                    shared_down(t - 2)
            for t in (NT - 2, NT - 1):
                shared_T(t)
                shared_down(t)

            def rows(b, ld, n):
                pe.wait_ge(ld, n)
                for c in range(NC):
                    ins = tr(BANK[2 + b][:, c * P:(c + 1) * P], XG[b][:, c * P:(c + 1) * P], I_)
                ins.then_inc(m_xt, 1)

            def gate_up(e1, b, r):
                pe.wait_ge(m_xtev, e1)
                for c in range(NC):
                    ins = mm(BANK[b][:, 0:I13], XGT[b][:, c * P:(c + 1) * P], w13[:, r, c * I13:(c + 1) * I13], start=c == 0, stop=c == NC - 1)
                ins.then_inc(m_gu, 1)

            def hidden_T(e1, b):
                pe.wait_ge(m_h, e1)
                for c in range(2):
                    ins = tr(BANK[4 + b][0:IC, c * P:(c + 1) * P], HS[b][:, c * IC:(c + 1) * IC], I_)
                ins.then_inc(m_ht, 1)

            def down(e1, b, r):
                pe.wait_ge(m_htev, e1)
                for c in range(2):
                    ins = mm(BANK[6 + b][:, 0:D], HST[b][:, c * P:(c + 1) * P], w2[:, r, c * D:(c + 1) * D], start=c == 0, stop=c == 1)
                ins.then_inc(m_y, 1)

            def expert(e, k, loads, nxt, first=False):
                b = k % 2
                if k % 2 == 0:
                    pe.wait_ge(ld_w[k // 2], loads)
                gate_up(e + 1, b, k)
                if not (first and k == 0):
                    hidden_T(e, 1 - b)
                if nxt is not None:
                    rows(1 - b, xg_ld[1 - b], nxt)
                if not (first and k < 2):
                    if not (first and k < 4):
                        pe.wait_ge(m_yev, e - 3)
                    down(e - 1, b, (k - 2) % RING)

            pe.wait_ge(s_sh, NT)
            rows(0, xg_ld[0], 16)
            for k in range(RING):
                expert(k, k, 32, 16 * ((k + 1) // 2 + 1), first=True)
            with pe.Fori(1, LAPS - 1) as o:
                for k in range(RING):
                    expert(o * RING + k, k, o * 32 + 32, o * (16 * RING // 2) + 16 * ((k + 1) // 2 + 1))
            for e in range(NE - RING, NE):
                expert(e, e % RING, 32 * LAPS, 16 * ((e + 1) // 2 + 1) if e + 1 < NE else None)
            hidden_T(NE, 1)
            pe.wait_ge(m_yev, NE - 3)
            down(NE - 1, 0, RING - 2)
            pe.wait_ge(m_yev, NE - 2)
            down(NE, 1, RING - 1)
            pe.wait_ge(s_slot, 2)
            nov = pe.value_load(novi[0:1, 0:1], min_val=1, max_val=MAXOV)
            with pe.Fori(0, nov) as i:
                rows(0, o_ld, i * 48 + 48)
                gate_up(i + (NE + 1), 0, 0)
                hidden_T(i + (NE + 1), 0)
                pe.wait_ge(m_yev, i + NE)
                down(i + (NE + 1), 0, 0)


def kernel(**inputs):
    import numpy as np
    import concourse.bacc as bacc
    from concourse.bass_utils import run_bass_kernel_spmd

    a = {k[3:]: np.asarray(v) for k, v in inputs.items()}
    S, D = a["attn_hidden_states"].shape[1:]
    P, NC = 128, D // 128
    E, I2, _ = a["ffn_w13"].shape
    I = I2 // 2
    half = 8
    inv = (np.float32(1.0) / np.float32(10000.0) ** (np.arange(0, half, 2, dtype=np.float32) / np.float32(half))).astype(np.float32)
    ang = np.arange(S, dtype=np.float32)[:, None] * inv[None, :]
    table = lambda f: np.ascontiguousarray(f(ang).astype(np.float32).reshape(S // P, P, half // 2).transpose(1, 0, 2))
    arrays = {
        "x": a["attn_hidden_states"][0],
        "cos": table(np.cos), "sin": table(np.sin),
        "c": a["c"][0].reshape(NC, P).T,
        "wmod": a["wmod"],
        "wqkv": np.concatenate([a["attn_Wq"], a["attn_Wk"], a["attn_Wv"]], axis=1),
        "wo": a["attn_Wo"],
        "wr": np.concatenate([a["ffn_gate_w"], a["ffn_shared_gate_w"]], axis=0).T,
        "segu": a["ffn_se_gate_up_w"].T,
        "sedn": a["ffn_se_down_w"].T,
        "w13": a["ffn_w13"].reshape(E, I2, NC, P).transpose(0, 3, 2, 1).reshape(E, P, NC * I2),
        "w2": a["ffn_w2"].reshape(E, D, 2, I // 2).transpose(0, 3, 2, 1).reshape(E, I // 2, 2 * D),
    }
    arrays = {k: np.ascontiguousarray(v) for k, v in arrays.items()}
    nc = bacc.Bacc("TRN2", target_bir_lowering=False, num_devices=1)
    f32 = mybir.dt.float32
    args = [nc.dram_tensor("in_" + k, v.shape, f32, kind="ExternalInput").ap() for k, v in arrays.items()]
    rows = (E + S * 4 // P - 1) * P
    tables = [nc.dram_tensor(k, (rows, D), f32, kind="Internal").ap() for k in ("xdisp", "ydisp")]
    o = nc.dram_tensor("out", (S, D), f32, kind="ExternalOutput").ap()
    adaln_layer(nc, *args, *tables, o)
    r = run_bass_kernel_spmd(nc, [{"in_" + k: v for k, v in arrays.items()}], core_ids=[0])
    return np.asarray(r.results[0]["out"]).reshape(1, S, D)
```

```python
import concourse.bass as bass
from concourse import mybir
from contextlib import ExitStack


def adaln_layer(nc, x_in, cos_in, sin_in, c_in, wmod_in, wqkv_in, wo_in, wr_in, segu_in, sedn_in,
                w13_in, w2_in, xdisp, ydisp, out):
    f32, bf16, i32, u32 = mybir.dt.float32, mybir.dt.bfloat16, mybir.dt.int32, mybir.dt.uint32
    ALU, ACT, AX = mybir.AluOpType, mybir.ActivationFunctionType, mybir.AxisListType

    S, D = x_in.shape
    P = 128
    NT, NC = S // P, D // P
    HD, NH, NG = 16, 16, 4
    HP = 32
    Q_PARTS, K_PARTS = "hhhmml", "hmlhmh"
    SR = 6 * HD
    SM = SR + 3
    QKV = (NH + 2 * NG) * HD
    NE, TOPK = 60, 4
    I13 = w13_in.shape[2] // NC
    I = I13 // 2
    IC = I // 2
    ISH = segu_in.shape[1] // 2
    SHH = ISH // 2
    NSC = (ISH + P - 1) // P
    SLAST = ISH - (NSC - 1) * P
    MAXOV = (S * TOPK) // P - 1
    EPS = 1e-5
    RING = 10
    LAPS = NE // RING
    U = 2 * NG
    LEAD = NT + 1
    STEPS = U * NT

    Q_FILL, O_FILL = [4 * LEAD + 2], []
    fills = 4 * LEAD + 2
    for n in range(STEPS):
        fills += 4 * (n + LEAD < STEPS)
        if n % NT == 2 and n > NT:
            O_FILL.append(fills - 2 * (n + LEAD < STEPS) + 1)
            fills += 1
        if n % NT == NT - 1 and n < STEPS - 1:
            fills += 2
            Q_FILL.append(fills)
    NB = xdisp.shape[0] // P
    ZW = NC * QKV
    N_ZERO = sum((n // ZW + 7) // 8 + (n % ZW > 0) for n in (NB * D, (NB - NE) * D))

    ctx = ExitStack()
    with ctx:
        def sb(name, shape, dt=f32):
            return ctx.enter_context(nc.sbuf_tensor(name, shape, dt))

        def ps(name, shape):
            return ctx.enter_context(nc.psum_tensor(name, shape, f32))

        def sem(name):
            return ctx.enter_context(nc.semaphore(name))

        x = sb("x", [P, NT, D])
        xh = sb("xh", [P, NT, D])
        hT = sb("hT", [P, NC, S])
        qkv = sb("qkv", [P, NT, QKV])
        QS = sb("QS", [P, NT, NH, SR], bf16)
        QT = sb("QT", [P, NH, S], bf16)
        KT = sb("KT", [P, NG, S], bf16)
        MS = sb("MS", [P, 2, 4, 4, 3], bf16)
        negm = sb("negm", [P, 2, 4, 4])
        SC = sb("SC", [P, 2048])
        VA = sb("VA", [P, NT, NG, HP])
        QSf = QS[:, :, :, :].rearrange("p t h c -> p (t h c)").bitcast(f32)
        PT = [QSf[:, 2048 * b:2048 * b + 2048].rearrange("p (j q) -> p j q", j=4) for b in range(3)]
        OT = sb("OT", [P, 512])
        MOD = sb("MOD", [P, 6, D])
        wide = sb("wide", [P, NC * 6 * D])
        wqkv = sb("wqkv", [P, NC, QKV])
        wo = sb("wo", [P, NC, D])
        wr = sb("wr", [P, NC, NE + 1])
        segu = sb("segu", [P, NC, 2 * ISH])
        sedn = sb("sedn", [P, NSC, D])
        w13 = sb("w13", [P, RING, NC * I13])
        w2 = sb("w2", [IC, RING, 2 * D])
        ident = sb("ident", [P, P])
        identb = sb("identb", [P, P], bf16)
        ones = sb("ones", [P, P])
        upper = sb("upper", [P, P], bf16)
        onesb = sb("onesb", [P, P], bf16)
        cosr = sb("cosr", [P, NT, 4])
        sinr = sb("sinr", [P, NT, 4])
        ccol = sb("ccol", [P, 4, NC])
        stats = sb("stats", [P, NT, 6])
        mv = sb("mv", [P, NT, 2])
        veps = sb("veps", [P, NT])
        mhalf = sb("mhalf", [P, NT])
        rstd = sb("rstd", [P, NT])
        mx = sb("mx", [P, 2, 4, 4, 2])
        rsum = sb("rsum", [P, 2, 4, 4])
        iota_i = sb("iota_i", [P, NE], i32)
        iotaf = sb("iotaf", [P, NE])
        top = sb("top", [P, NT, 8])
        topi = sb("topi", [P, NT, 8], u32)
        topf = sb("topf", [P, NT, 8])
        sgate = sb("sgate", [P, 2, NT])
        slotk = sb("slotk", [P, NT * TOPK])
        sloti = sb("sloti", [P, NT * TOPK], u32)
        novi = sb("novi", [1, 1], i32)
        ovei = sb("ovei", [1, MAXOV + 1], i32)
        KS = SC[:, :].bitcast(bf16)[:, 0:NT * NG * (SM + 1)].rearrange("p (t g c) -> p t g c", t=NT, g=NG)
        crep = SC[:, 1600:1600 + NC * P].rearrange("p (c n) -> p c n", c=NC)
        rt = wide[:, 1024:1024 + 16 * (NH + NG) * 4].rearrange("p (k t n) -> p k t n", k=4, t=4)
        small = wqkv[:, :, :].rearrange("p c n -> p (c n)")
        grid = NT * NE
        probs = SC[:, 0:grid].rearrange("p (t e) -> p t e", t=NT)
        slot = SC[:, grid:2 * grid].rearrange("p (t e) -> p t e", t=NT)
        mask = SC[:, :].bitcast(bf16)[:, 4 * grid:5 * grid].rearrange("p (t e) -> p t e", t=NT)
        gt = SC[:, 3 * grid:3 * grid + NE * (NT - 1)].rearrange("p (e k) -> p e k", e=NE)
        gtmp = OT[:, 0:2 * D].rearrange("p (k n) -> p k n", k=2)
        wog = wide[:, 0:NC * D].rearrange("p (c n) -> p c n", c=NC)
        AT = qkv[:, :, :].rearrange("p t n -> p (t n)")[:, 0:NT * D].rearrange("p (t n) -> p t n", t=NT)
        QTf = QT[:, :, :].rearrange("p h s -> p (h s)").bitcast(f32)
        SH = QTf[:, 0:NT * D].rearrange("p (t n) -> p t n", t=NT)
        OH = QTf[:, 2048:2048 + NT * TOPK * NE].rearrange("p (t k e) -> p t k e", t=NT, k=TOPK)
        PR = QTf[:, 4096:4096 + NT * TOPK * NE].rearrange("p (t k e) -> p t k e", t=NT, k=TOPK)
        h2T = QTf[:, 6144:6144 + NC * S].rearrange("p (c s) -> p c s", c=NC)
        XG = [QSf[:, 512 * b:512 * b + D] for b in range(2)]
        XGT = [QSf[:, 1024 + 512 * b:1024 + 512 * b + D] for b in range(2)]
        SL = [QSf[:, 2048 + 256 * b:2048 + 256 * b + I] for b in range(2)]
        HS = [QSf[:, 2560 + 256 * b:2560 + 256 * b + I] for b in range(2)]
        HST = [QSf[0:IC, 3072 + 256 * b:3072 + 256 * b + 2 * P] for b in range(2)]
        YS = [QSf[:, 3584 + 256 * b:3584 + 256 * b + D] for b in range(2)]
        wmod = wide[:, :].rearrange("p (c n) -> p c n", c=NC)
        shg = wide[:, 0:ISH]
        shh = [wide[:, ISH * (1 + b):ISH * (2 + b)] for b in range(2)]
        shT = wide[:, 3 * ISH:3 * ISH + NSC * P].rearrange("p (c n) -> p c n", c=NSC)
        YG = [QSf[:, 4096 + 1024 * b:5120 + 1024 * b].rearrange("p (k n) -> p k n", k=TOPK) for b in range(2)] + \
             [w13[:, 2 * b:2 * b + 2, :].rearrange("p r n -> p (r n)")[:, 0:TOPK * D]
              .rearrange("p (k n) -> p k n", k=TOPK) for b in range(2)]

        EP = [ps(f"EP{p}", [P, 2, 512]) for p in range(2)]
        M2 = ps("M2", [P, 2, 512])
        PV = ps("PV", [P, 512])
        M3 = ps("M3", [P, 512])
        BANK = [EP[0][:, 0], EP[0][:, 1], EP[1][:, 0], EP[1][:, 1], M2[:, 0], M2[:, 1], PV[:, :], M3[:, :]]
        MR = [BANK[4], BANK[5], BANK[7]]

        ld_x, ld_c, ld_rope, ld_mod = [sem("ld_x0"), sem("ld_x1")], sem("ld_c"), sem("ld_rope"), sem("ld_mod")
        ld_qkv, ld_wo, ld_wr, ld_sh = sem("ld_qkv"), sem("ld_wo"), sem("ld_wr"), sem("ld_sh")
        ld_w = [sem(f"ld_w{r}") for r in range(RING // 2)]
        zero_st, zeros_ok = sem("zero_st"), sem("zeros_ok")
        s_ident, s_const, s_iota, s_pad, s_rstd, s_krep = (sem(n) for n in ("s_ident", "s_const", "s_iota", "s_pad", "s_rstd", "s_krep"))
        s_ec, s_crep, s_mod, s_modev, s_modok = (sem(n) for n in ("s_ec", "s_crep", "s_mod", "s_modev", "s_modok"))
        s_var, s_h, s_tr, s_trev = (sem(n) for n in ("s_var", "s_h", "s_tr", "s_trev"))
        s_qkv, s_qkvev, s_rope, s_split, s_qa = (sem(n) for n in ("s_qkv", "s_qkvev", "s_rope", "s_split", "s_qa"))
        s_qk, s_qkA, s_qkD = (sem(n) for n in ("s_qk", "s_qkA", "s_qkD"))
        m_fill, m_free, s_negm = sem("m_fill"), sem("m_free"), sem("s_negm")
        e_fill, e_done, pv_step = sem("e_fill"), sem("e_done"), sem("pv_step")
        s_at, s_atev, s_wog, s_ao, s_x1 = (sem(n) for n in ("s_at", "s_atev", "s_wog", "s_ao", "s_x1"))
        s_var2, s_h2, s_tr2, s_tr2ev = (sem(n) for n in ("s_var2", "s_h2", "s_tr2", "s_tr2ev"))
        s_lg, s_ld, s_pe, s_mask, s_rank, s_slot, s_disp = (sem(n) for n in ("s_lg", "s_ld", "s_pe", "s_mask", "s_rank", "s_slot", "s_disp"))
        s_gate, s_up, s_silu, s_shh, s_shtr, s_shT, s_dn, s_sh = (sem(n) for n in ("s_gate", "s_up", "s_silu", "s_shh", "s_shtr", "s_shT", "s_dn", "s_sh"))
        xg_ld, y_st = [sem("xg_ld0"), sem("xg_ld1")], [sem("y_st0"), sem("y_st1")]
        m_xt, m_xtev, m_gu, m_silu, m_h, m_ht, m_htev, m_y, m_yev = (sem(f"m_{n}") for n in ("xt", "xtev", "gu", "silu", "h", "ht", "htev", "y", "yev"))
        o_ld = sem("o_ld")
        s_yg = [sem(f"s_yg{t}") for t in range(NT)]
        s_acc, s_fin, out_st, dv = sem("s_acc"), sem("s_fin"), sem("out_st"), sem("dv")

        block = ctx.enter_context(nc.Block())

        def q_unit(n):
            return divmod(n, 2)

        def qk_part(n):
            h, i = divmod(n, 10)
            return h, i < 2, 2 * i if i < 2 else 2 * (i - 2)

        def qk_evac(n):
            h, is_k, j = qk_part(n)
            rows = SM if is_k else SR
            return ((KT if is_k else QT)[0:rows, j:j + 2, 512 * h:512 * h + 512],
                    BANK[n % 8][0:rows, :].bitcast(bf16).rearrange("p (j s) -> p j s", j=2))

        @block.sync
        def _(sp):
            for h in range(2):
                sp.dma_start(x[:, 4 * h:4 * h + 4, :],
                             x_in[512 * h:512 * h + 512, :].rearrange("(t p) d -> p t d", p=P)).then_inc(ld_x[h], 16)
                if h == 0:
                    sp.dma_start(ccol[:, 0, :], c_in).then_inc(ld_c, 16)
            sp.dma_start(wmod, wmod_in.rearrange("(c p) n -> p c n", p=P)).then_inc(ld_mod, 16)
            sp.dma_start(cosr[:, :, :], cos_in).then_inc(ld_rope, 16)
            sp.dma_start(sinr[:, :, :], sin_in).then_inc(ld_rope, 16)
            sp.dma_start(wqkv[:, :, :], wqkv_in.rearrange("(c p) n -> p c n", p=P)).then_inc(ld_qkv, 16)
            sp.dma_start(wo[:, :, :], wo_in.rearrange("(c p) n -> p c n", p=P)).then_inc(ld_wo, 16)
            sp.dma_start(wr[:, :, :], wr_in.rearrange("(c p) n -> p c n", p=P)).then_inc(ld_wr, 16)
            sp.dma_start(segu[:, :, :], segu_in.rearrange("(c p) n -> p c n", p=P)).then_inc(ld_sh, 16)
            sp.dma_start(sedn[:, 0:NSC - 1, :],
                         sedn_in[0:(NSC - 1) * P, :].rearrange("(c p) n -> p c n", p=P)).then_inc(ld_sh, 16)
            sp.dma_start(sedn[0:SLAST, NSC - 1, :], sedn_in[(NSC - 1) * P:ISH, :]).then_inc(ld_sh, 16)

            def load_pair(e, k):
                sp.dma_start(w13[:, k:k + 2, :], w13_in[bass.ds(e, 2), :, :].rearrange("e p n -> p e n")).then_inc(ld_w[k // 2], 16)
                sp.dma_start(w2[:, k:k + 2, :], w2_in[bass.ds(e, 2), :, :].rearrange("e p n -> p e n")).then_inc(ld_w[k // 2], 16)

            for k in range(0, RING, 2):
                load_pair(k, k)
            sp.wait_ge(zeros_ok, 1)
            for table in (xdisp, ydisp[NE * P:, :]):
                z = table.rearrange("(p r) n -> p (r n)", p=P)
                n = z.shape[1]
                for o in range(0, n // ZW, 8):
                    k = min(8, n // ZW - o)
                    sp.dma_start(z[:, o * ZW:(o + k) * ZW].rearrange("p (a n) -> p a n", n=ZW),
                                 small.unsqueeze(1).to_broadcast([P, k, ZW])).then_inc(zero_st, 16)
                if n % ZW:
                    sp.dma_start(z[:, n - n % ZW:], small[:, 0:n % ZW]).then_inc(zero_st, 16)

            def load_rows(e, b):
                sp.dma_start(XG[b], xdisp[bass.ds(e * P, P), :]).then_inc(xg_ld[b], 16)

            def store_rows(e, b):
                sp.dma_start(ydisp[bass.ds(e * P, P), :], YS[b]).then_inc(y_st[b], 16)

            def expert(e, k, weights, rows, store):
                if weights and k % 2 == 0:
                    sp.wait_ge(m_y, e - 2)
                    load_pair(e + 6, (k + 6) % RING)
                if rows:
                    sp.wait_ge(m_xt, e + 1)
                    load_rows(e + 2, k % 2)
                if store:
                    sp.wait_ge(m_yev, e - 2)
                    store_rows(e - 3, 1 - k % 2)

            sp.wait_ge(s_disp, 16 * NT * TOPK)
            load_rows(0, 0)
            load_rows(1, 1)
            for k in range(RING):
                expert(k, k, weights=k >= 4, rows=True, store=k >= 3)
            with sp.Fori(1, LAPS - 1) as o:
                for k in range(RING):
                    expert(o * RING + k, k, weights=True, rows=True, store=True)
            for k in range(RING + 3):
                e = NE - RING + k
                expert(e, k, weights=e + 7 < NE, rows=e + 2 < NE, store=True)
            sp.wait_ge(s_slot, 2)
            nov = sp.value_load(novi[0:1, 0:1], min_val=1, max_val=MAXOV)
            with sp.Fori(0, nov) as b:
                sp.wait_ge(m_yev, b + NE)
                e = sp.value_load(ovei[0:1, bass.ds(b, 1)], min_val=0, max_val=NE - 1)
                sp.dma_start(w13[:, 0, :], w13_in[bass.ds(e, 1), :, :].rearrange("e p n -> p (e n)")).then_inc(o_ld, 16)
                sp.dma_start(w2[:, 0, :], w2_in[bass.ds(e, 1), :, :].rearrange("e p n -> p (e n)")).then_inc(o_ld, 16)
                sp.dma_start(XG[0], xdisp[bass.ds((b + NE) * P, P), :]).then_inc(o_ld, 16)
                sp.wait_ge(m_yev, b + (NE + 1))
                sp.dma_start(ydisp[bass.ds((b + NE) * P, P), :], YS[0]).then_inc(y_st[0], 16)
            for t in range(NT):
                sp.wait_ge(s_fin, t + 1)
                sp.dma_start(out[t * P:(t + 1) * P, :], x[:, t, :]).then_inc(out_st, 16)
            sp.wait_ge(out_st, 16 * NT)

        @block.gpsimd
        def _(pool):
            pool.memset(ident[:, :], 0.0).then_inc(s_ident, 1)
            pool.memset(ones[:, :], 1.0).then_inc(s_const, 1)
            pool.memset(onesb[:, :], 1.0).then_inc(s_const, 1)
            pool.wait_ge(s_ident, 1)
            pool.affine_select(out=ident[:, :], in_=ident[:, :], compare_op=ALU.not_equal, fill=1.0,
                               base=0, pattern=[[-1, P]], channel_multiplier=1).then_inc(s_ident, 1)
            pool.memset(mhalf[:, :], -0.5).then_inc(s_const, 1)
            for h in range(2):
                pool.wait_ge(s_const, 3)
                pool.wait_ge(s_var, h + 1)
                pool.tensor_tensor(rstd[:, 4 * h:4 * h + 4], veps[:, 4 * h:4 * h + 4], mhalf[:, 0:4], ALU.pow).then_inc(s_rstd, 1)
            pool.memset(KS[:, :, :, SR:SM], 1.0).then_inc(s_pad, 1)
            pool.wait_ge(s_ident, 2)
            pool.tensor_copy(identb[:, :], ident[:, :]).then_inc(s_ident, 1)
            pool.memset(VA[:, :, :, :], 0.0).then_inc(s_pad, 1)
            pool.wait_ge(s_pad, 2)
            pool.memset(VA[:, :, :, HD:HD + 1], 1.0).then_inc(s_pad, 1)
            pool.wait_ge(s_pad, 3)
            for h in range(2):
                tt = slice(4 * h, 4 * h + 4)
                pool.wait_ge(s_qkvev, 4 * h + 4)
                pool.tensor_copy(VA[:, tt, :, 0:HD],
                                 qkv[:, tt, (NH + NG) * HD:].rearrange("p t (g d) -> p t g d", g=NG)).then_inc(s_krep, 1)
                pool.wait_ge(s_split, h + 1)
                for i in range(3, 6):
                    o = HD * K_PARTS.index(K_PARTS[i])
                    pool.tensor_copy(KS[:, tt, :, HD * i:HD * i + HD], KS[:, tt, :, o:o + HD]).then_inc(s_krep, 1)
            pool.wait_ge(s_qkv, NT)
            pool.memset(small, 0.0).then_inc(zeros_ok, 1)
            pool.affine_select(out=upper[:, :], in_=onesb[:, :], compare_op=ALU.is_gt, fill=0.0,
                               base=0, pattern=[[1, P]], channel_multiplier=-1).then_inc(s_const, 1)
            pool.iota(iota_i[:, :], pattern=[[1, NE]], base=0, channel_multiplier=0).then_inc(s_iota, 1)
            pool.wait_ge(s_iota, 1)
            pool.tensor_copy(iotaf[:, :], iota_i[:, :]).then_inc(s_iota, 1)
            for h in range(2):
                pool.wait_ge(s_var2, h + 1)
                pool.tensor_tensor(rstd[:, 4 * h:4 * h + 4], veps[:, 4 * h:4 * h + 4], mhalf[:, 0:4], ALU.pow).then_inc(s_rstd, 1)
            pool.wait_ge(zero_st, 16 * N_ZERO)
            pool.wait_ge(s_slot, 1)
            pool.wait_ge(s_h2, 2)
            for t in range(NT):
                for k in range(TOPK):
                    i = t * TOPK + k
                    pool.indirect_dma_start(out=xdisp, out_offset=bass.IndirectOffsetOnAxis(ap=sloti[:, i:i + 1], axis=0),
                                            in_=xh[:, t, :], in_offset=None).then_inc(s_disp, 16)
            pool.wait_ge(s_slot, 2)
            nov = pool.value_load(novi[0:1, 0:1], min_val=1, max_val=MAXOV)
            with pool.Fori(0, nov) as b:
                pool.wait_ge(y_st[0], b * 16 + 16 * (NE // 2 + 1))
            pool.wait_ge(y_st[1], 16 * (NE // 2))
            for t in range(NT):
                if t >= 4:
                    pool.wait_ge(s_acc, t - 3)
                for k in range(TOPK):
                    i = t * TOPK + k
                    pool.indirect_dma_start(out=YG[t % 4][:, k, :], out_offset=None, in_=ydisp,
                                            in_offset=bass.IndirectOffsetOnAxis(ap=sloti[:, i:i + 1], axis=0)).then_inc(s_yg[t], 16)

        @block.scalar
        def _(act):
            act.wait_ge(ld_c, 16)
            nc.scalar.activation(ccol[:, 1, :], ccol[:, 0, :], ACT.Exp, scale=-1.0).then_inc(s_ec, 1)
            act.wait_ge(s_mod, 1)
            nc.scalar.activation(MOD[:, 0:4, :], EP[0][:, :, :].rearrange("p a (b n) -> p (a b) n", b=2), ACT.Copy).then_inc(s_modev, 1)
            nc.scalar.activation(MOD[:, 4:6, :], BANK[2].rearrange("p (b n) -> p b n", b=2), ACT.Copy).then_inc(s_modev, 1)
            for tp in range(NT // 2):
                act.wait_ge(s_tr, tp + 1)
                for c in range(NC):
                    ins = nc.scalar.activation(hT[:, c, 256 * tp:256 * tp + 256].rearrange("p (t n) -> p t n", t=2),
                                               BANK[3 + tp].rearrange("p (t c n) -> p t c n", t=2, c=NC)[:, :, c, :], ACT.Copy)
                ins.then_inc(s_trev, 1)
            for t in range(NT):
                act.wait_ge(s_qkv, t + 1)
                nc.scalar.activation(qkv[:, t, :], BANK[(7 + t) % 8][:, 0:QKV], ACT.Copy).then_inc(s_qkvev, 1)
            for h in range(2):
                tt = slice(4 * h, 4 * h + 4)
                act.wait_ge(s_split, h + 1)
                for i in (1, 2, 4):
                    o = HD * Q_PARTS.index(Q_PARTS[i])
                    ins = nc.scalar.activation(QS[:, tt, :, HD * i:HD * i + HD], QS[:, tt, :, o:o + HD], ACT.Copy)
                ins.then_inc(s_qa, 1)
            for n in range(0, 20, 2):
                act.wait_ge(s_qk, n + 1)
                dst, src = qk_evac(n)
                nc.scalar.activation(dst, src, ACT.Copy).then_inc(s_qkA, 1)

            for n in range(STEPS):
                for p in range(2):
                    if p == 1 and n % NT == 0 and n:
                        u = n // NT - 1
                        act.wait_ge(pv_step, NT * (u + 1))
                        if u:
                            act.wait_ge(m_fill, O_FILL[u - 1])
                        nc.scalar.activation(OT[:, :], PV[:, :], ACT.Copy).then_inc(s_atev, 1)
                    act.wait_ge(e_fill, 2 * n + p + 1)
                    if n >= 3 and p == 0:
                        act.wait_ge(pv_step, n - 2)
                    nc.scalar.activation(PT[n % 3][:, 2 * p:2 * p + 2, :], EP[p][:, :, :], ACT.Exp, scale=HD ** -0.5).then_inc(e_done, 1)
            act.wait_ge(pv_step, STEPS)
            act.wait_ge(m_fill, O_FILL[U - 2])
            nc.scalar.activation(OT[:, :], PV[:, :], ACT.Copy).then_inc(s_atev, 1)

            for tp in range(NT // 2):
                act.wait_ge(s_at, tp + 1)
                for c in range(NC):
                    ins = nc.scalar.activation(hT[:, c, 256 * tp:256 * tp + 256].rearrange("p (t n) -> p t n", t=2),
                                               BANK[tp].rearrange("p (t c n) -> p t c n", t=2, c=NC)[:, :, c, :], ACT.Copy)
                ins.then_inc(s_trev, 1)
            for tp in range(NT // 2):
                act.wait_ge(s_tr2, tp + 1)
                for c in range(NC):
                    ins = nc.scalar.activation(h2T[:, c, 256 * tp:256 * tp + 256].rearrange("p (t n) -> p t n", t=2),
                                               BANK[tp].rearrange("p (t c n) -> p t c n", t=2, c=NC)[:, :, c, :], ACT.Copy)
                ins.then_inc(s_tr2ev, 1)
            act.wait_ge(s_ld, 1)
            nc.scalar.activation(probs[:, :, :], probs[:, :, :], ACT.Exp).then_inc(s_pe, 1)
            nc.scalar.activation(sgate[:, 0, :], sgate[:, 1, :], ACT.Exp, scale=-1.0).then_inc(s_pe, 1)
            def shared_evac(t):
                act.wait_ge(s_shtr, t + 1)
                if t:
                    act.wait_ge(s_dn, t)
                nc.scalar.activation(shT[:, 0:4, :], BANK[4].rearrange("p (c n) -> p c n", c=4), ACT.Copy)
                nc.scalar.activation(shT[:, 4, :], BANK[5][:, 0:P], ACT.Copy)
                nc.scalar.activation(shT[0:SLAST, 5, :], BANK[5][0:SLAST, P:2 * P], ACT.Copy).then_inc(s_shT, 1)

            for t in range(NT):
                act.wait_ge(s_gate, t + 1)
                if t:
                    act.wait_ge(s_shh, t)
                nc.scalar.activation(shg.rearrange("p (a n) -> p a n", a=2), EP[0][:, :, 0:SHH], ACT.Silu).then_inc(s_silu, 1)
                if t > 1:
                    shared_evac(t - 2)
            shared_evac(NT - 2)
            shared_evac(NT - 1)

            def silu(e, b, first=False):
                act.wait_ge(m_gu, e + 1)
                if not first:
                    act.wait_ge(m_h, e - 1)
                nc.scalar.activation(SL[b], BANK[b][:, 0:I], ACT.Silu).then_inc(m_silu, 1)

            def result(e, b, stored):
                act.wait_ge(m_y, e + 1)
                if stored is not None:
                    act.wait_ge(y_st[b], stored)
                nc.scalar.activation(YS[b], BANK[6 + b][:, 0:D], ACT.Copy).then_inc(m_yev, 1)

            for k in range(RING):
                silu(k, k % 2, first=k < 2)
                if k >= 2:
                    result(k - 2, k % 2, 16 * ((k - 2) // 2) if k >= 4 else None)
            with act.Fori(1, LAPS - 1) as o:
                for k in range(RING):
                    silu(o * RING + k, k % 2)
                    result(o * RING + (k - 2), k % 2, o * (16 * RING // 2) + 16 * (k // 2 - 1))
            for e in range(NE - RING, NE):
                silu(e, e % 2)
                result(e - 2, e % 2, 16 * ((e - 2) // 2))
            for e in (NE - 2, NE - 1):
                result(e, e % 2, 16 * (e // 2))
            act.wait_ge(s_slot, 2)
            nov = act.value_load(novi[0:1, 0:1], min_val=1, max_val=MAXOV)
            with act.Fori(0, nov) as i:
                act.wait_ge(m_gu, i + (NE + 1))
                act.wait_ge(m_h, i + NE)
                nc.scalar.activation(SL[0], BANK[0][:, 0:I], ACT.Silu).then_inc(m_silu, 1)
                act.wait_ge(m_y, i + (NE + 1))
                act.wait_ge(y_st[0], i * 16 + 16 * (NE // 2))
                nc.scalar.activation(YS[0], BANK[6][:, 0:D], ACT.Copy).then_inc(m_yev, 1)

        @block.vector
        def _(dve):
            count = [0]

            def then(ins):
                count[0] += 1
                ins.then_inc(dv, 1)
                dve.wait_ge(dv, count[0])

            def statistics(h, var_sem):
                for t in range(4 * h, 4 * h + 4):
                    ins = nc.vector.bn_stats(stats[:, t, :], x[:, t, :])
                then(ins)
                for t in range(4 * h, 4 * h + 4):
                    ins = nc.vector.bn_aggr(mv[:, t, :], stats[:, t, :])
                then(ins)
                nc.vector.tensor_scalar(veps[:, 4 * h:4 * h + 4], mv[:, 4 * h:4 * h + 4, 1], EPS, None, ALU.add).then_inc(var_sem, 1)

            def modulate(h, k, done):
                tt = slice(4 * h, 4 * h + 4)
                for t in range(4 * h, 4 * h + 4):
                    ins = nc.vector.tensor_scalar(xh[:, t, :], x[:, t, :], mv[:, t, 0:1], rstd[:, t:t + 1], ALU.subtract, ALU.mult)
                then(ins)
                then(nc.vector.tensor_tensor(xh[:, tt, :], xh[:, tt, :], MOD[:, k + 1:k + 2, :].to_broadcast([P, 4, D]), ALU.mult))
                nc.vector.tensor_tensor(xh[:, tt, :], xh[:, tt, :], MOD[:, k:k + 1, :].to_broadcast([P, 4, D]), ALU.add).then_inc(done, 1)

            dve.wait_ge(s_ec, 1)
            then(nc.vector.tensor_scalar(ccol[:, 2, :], ccol[:, 1, :], 1.0, None, ALU.add))
            then(nc.vector.reciprocal(ccol[:, 2, :], ccol[:, 2, :]))
            then(nc.vector.tensor_tensor(ccol[:, 3, :], ccol[:, 0, :], ccol[:, 2, :], ALU.mult))
            dve.wait_ge(s_const, 1)
            for c in range(NC):
                ins = nc.vector.tensor_scalar(crep[:, c, :], ones[:, :], ccol[:, 3, c:c + 1], None, ALU.mult)
            ins.then_inc(s_crep, 1)
            for h in range(2):
                dve.wait_ge(ld_x[h], 16)
                statistics(h, s_var)
            dve.wait_ge(s_modev, 2)
            for k in (1, 4):
                ins = nc.vector.tensor_scalar(MOD[:, k, :], MOD[:, k, :], 1.0, None, ALU.add)
            then(ins)
            for h in range(2):
                dve.wait_ge(s_rstd, h + 1)
                modulate(h, 0, s_h)
            dve.wait_ge(ld_rope, 32)
            for h in range(2):
                tt = slice(4 * h, 4 * h + 4)
                dve.wait_ge(s_qkvev, 4 * h + 4)
                pr = qkv[:, tt, 0:(NH + NG) * HD].rearrange("p t (h i two) -> p t h i two", h=NH + NG, two=2)
                a, b = pr[:, :, :, 0:4, 0], pr[:, :, :, 0:4, 1]
                cs = [w[:, tt, :].unsqueeze(2).to_broadcast([P, 4, NH + NG, 4]) for w in (cosr, sinr)]
                R = [rt[:, k].rearrange("p t (h i) -> p t h i", i=4) for k in range(4)]
                nc.vector.tensor_tensor(R[0], a, cs[0], ALU.mult)
                nc.vector.tensor_tensor(R[1], b, cs[1], ALU.mult)
                nc.vector.tensor_tensor(R[2], a, cs[1], ALU.mult)
                then(nc.vector.tensor_tensor(R[3], b, cs[0], ALU.mult))
                nc.vector.tensor_tensor(a, R[0], R[1], ALU.subtract)
                nc.vector.tensor_tensor(b, R[2], R[3], ALU.add).then_inc(s_rope, 1)
                dve.wait_ge(s_rope, h + 1)
                both = [(qkv[:, tt, 0:NH * HD].rearrange("p t (h d) -> p t h d", d=HD), QS[:, tt, :, :], Q_PARTS),
                        (qkv[:, tt, NH * HD:(NH + NG) * HD].rearrange("p t (h d) -> p t h d", d=HD), KS[:, tt, :, :], K_PARTS)]
                part = lambda dst, parts, c: dst[:, :, :, HD * parts.index(c):HD * parts.index(c) + HD]
                for src, dst, parts in both:
                    ins = nc.vector.tensor_copy(part(dst, parts, "h"), src)
                then(ins)
                for src, dst, parts in both:
                    ins = nc.vector.tensor_tensor(src, src, part(dst, parts, "h"), ALU.subtract)
                then(ins)
                for src, dst, parts in both:
                    ins = nc.vector.tensor_copy(part(dst, parts, "m"), src)
                then(ins)
                for src, dst, parts in both:
                    ins = nc.vector.tensor_tensor(part(dst, parts, "l"), src, part(dst, parts, "m"), ALU.subtract)
                ins.then_inc(s_split, 1)
            for n in range(1, 20, 2):
                dve.wait_ge(s_qk, n + 1)
                dst, src = qk_evac(n)
                nc.vector.tensor_copy(dst, src).then_inc(s_qkD, 1)
            for k in (2, 5):
                g0 = gtmp[:, 0, :]
                g1 = gtmp[:, 1, :]
                nc.vector.tensor_scalar(g0, MOD[:, k, :], 0.0, 2.0, ALU.is_ge, ALU.mult)
                then(nc.vector.scalar_tensor_tensor(out=g1, in0=MOD[:, k, :], scalar=-1.0, in1=MOD[:, k, :], op0=ALU.mult, op1=ALU.max))
                then(nc.vector.tensor_scalar(g1, g1, 0.25, None, ALU.max))
                then(nc.vector.scalar_tensor_tensor(out=MOD[:, k, :], in0=g0, scalar=-1.0, in1=g1, op0=ALU.add, op1=ALU.mult))
            dve.wait_ge(ld_wo, 16)
            nc.vector.tensor_tensor(wog[:, :, :], wo[:, :, :], MOD[:, 2:3, :].to_broadcast([P, NC, D]), ALU.mult).then_inc(s_wog, 1)

            ring = [0]

            def take():
                ring[0] += 1
                dve.wait_ge(m_fill, ring[0])
                return MR[(ring[0] - 1) % 3]

            def row_max(k, heads):
                u, s = divmod(k, NT)
                for j in heads:
                    src = take()
                    nc.vector.reduce_max(mx[:, u % 2, s // 2, j, s % 2:s % 2 + 1], src, AX.X).then_inc(m_free, 1)

            def minus_max(u):
                dve.wait_ge(m_free, ring[0])
                m, part = negm[:, u % 2], MS[:, u % 2]
                then(nc.vector.tensor_reduce(out=m, in_=mx[:, u % 2], axis=AX.X, op=ALU.max, negate=True))
                then(nc.vector.tensor_copy(part[:, :, :, 0], m))
                then(nc.vector.tensor_tensor(m, m, part[:, :, :, 0], ALU.subtract))
                then(nc.vector.tensor_copy(part[:, :, :, 1], m))
                nc.vector.tensor_tensor(part[:, :, :, 2], m, part[:, :, :, 1], ALU.subtract).then_inc(s_negm, 1)

            def take_max(u):
                g, qh = q_unit(u)
                for i in range(2):
                    src = take()[SR:SM, :].bitcast(bf16).rearrange("p (j s) -> p j s", j=2)
                    nc.vector.tensor_copy(QT[SR:SM, 4 * g + 2 * i:4 * g + 2 * i + 2, 512 * qh:512 * qh + 512], src).then_inc(m_free, 1)

            def take_output(u):
                g, qh = q_unit(u)
                o = take().rearrange("p (t j c) -> p t j c", t=4, j=4)
                then(nc.vector.reciprocal(rsum[:, u % 2], o[:, :, :, HD]))
                for t in range(4):
                    ins = nc.vector.tensor_tensor(AT[:, 4 * qh + t, 4 * HD * g:4 * HD * (g + 1)].rearrange("p (j d) -> p j d", j=4),
                                                  o[:, t, :, 0:HD], rsum[:, u % 2, t, :].unsqueeze(2).to_broadcast([P, 4, HD]), ALU.mult)
                ins.then_inc(m_free, 1)

            for k in range(LEAD):
                row_max(k, (2, 3, 0, 1))
                if k % NT == NT - 1:
                    minus_max(k // NT)
            take_max(0)
            for n in range(STEPS):
                k = n + LEAD
                if k < STEPS:
                    row_max(k, (2, 3))
                if n % NT == 2 and n > NT:
                    take_output(n // NT - 1)
                if k < STEPS:
                    row_max(k, (0, 1))
                    if k % NT == NT - 1:
                        minus_max(k // NT)
                if n % NT == NT - 1 and n < STEPS - 1:
                    take_max(n // NT + 1)
            take_output(U - 1)

            for tp in range(NT // 2):
                dve.wait_ge(s_ao, tp + 1)
                nc.vector.tensor_tensor(x[:, 2 * tp:2 * tp + 2, :], x[:, 2 * tp:2 * tp + 2, :],
                                        BANK[4 + tp].rearrange("p (t n) -> p t n", t=2), ALU.add).then_inc(s_x1, 1)
                if tp % 2:
                    dve.wait_ge(s_x1, tp + 1)
                    statistics(tp // 2, s_var2)
            for h in range(2):
                dve.wait_ge(s_rstd, h + 3)
                modulate(h, 3, s_h2)

            dve.wait_ge(s_lg, 1)
            lg = BANK[7][:, 0:NT * (NE + 1)].rearrange("p (t e) -> p t e", t=NT)
            sm = small
            dve.wait_ge(zero_st, 16 * N_ZERO)
            mxl, sml = sm[:, 0:NT], sm[:, NT:2 * NT]
            then(nc.vector.reduce_max(mxl, lg[:, :, 0:NE], AX.X))
            nc.vector.tensor_copy(sgate[:, 1, :], lg[:, :, NE])
            nc.vector.tensor_tensor(probs[:, :, :], lg[:, :, 0:NE], mxl.unsqueeze(2).to_broadcast([P, NT, NE]), ALU.subtract).then_inc(s_ld, 1)
            dve.wait_ge(s_pe, 2)
            then(nc.vector.reduce_sum(sml, probs[:, :, :], AX.X))
            then(nc.vector.reciprocal(sml, sml))
            then(nc.vector.tensor_tensor(probs[:, :, :], probs[:, :, :], sml.unsqueeze(2).to_broadcast([P, NT, NE]), ALU.mult))
            for t in range(NT):
                ins = nc.vector.max(top[:, t, :], probs[:, t, :])
            then(ins)
            for t in range(NT):
                ins = nc.vector.max_index(topi[:, t, :], top[:, t, :], probs[:, t, :])
            then(ins)
            then(nc.vector.tensor_copy(topf[:, :, :], topi[:, :, :]))
            dve.wait_ge(s_iota, 2)
            for t in range(NT):
                ins = nc.vector.tensor_tensor(OH[:, t], iotaf[:, :].unsqueeze(1).to_broadcast([P, TOPK, NE]),
                                              topf[:, t, 0:TOPK].unsqueeze(2).to_broadcast([P, TOPK, NE]), ALU.is_equal)
            then(ins)
            nc.vector.tensor_reduce(out=mask[:, :, :], in_=OH.rearrange("p t k e -> p t e k"), axis=AX.X, op=ALU.max).then_inc(s_mask, 1)
            then(nc.vector.tensor_scalar(sgate[:, 1, :], sgate[:, 0, :], 1.0, None, ALU.add))
            then(nc.vector.reciprocal(sgate[:, 0, :], sgate[:, 1, :]))
            cnt, nov, inc, off, base = (sm[:, 64 * (k + 1):64 * (k + 1) + NE] for k in range(5))
            thr = sm[:, 400:400 + NT - 1]
            nc.vector.tensor_scalar(thr, iotaf[:, 1:NT], float(P), None, ALU.mult)
            then(nc.vector.tensor_scalar(base, iotaf[:, :], float(P), None, ALU.mult))
            dve.wait_ge(s_rank, 1)
            rank = BANK[6][:, 0:NT * NE].rearrange("p (t e) -> p t e", t=NT)
            then(nc.vector.tensor_copy(cnt, BANK[5][:, 0:NE]))
            then(nc.vector.tensor_tensor(gt, cnt.unsqueeze(2).to_broadcast([P, NE, NT - 1]),
                                         thr.unsqueeze(1).to_broadcast([P, NE, NT - 1]), ALU.is_gt))
            then(nc.vector.reduce_sum(nov, gt, AX.X))
            then(nc.vector.tensor_tensor_scan(inc, ones[:, 0:NE], nov, 0.0, ALU.mult, ALU.add))
            then(nc.vector.tensor_tensor(off, inc, nov, ALU.subtract))
            then(nc.vector.tensor_scalar(off, off, float(P), float(P * (NE - 1)), ALU.mult, ALU.add))
            then(nc.vector.tensor_tensor(off, off, base, ALU.subtract))
            nc.vector.scalar_tensor_tensor(out=slot[:, :, :], in0=rank, scalar=float(P), in1=off.unsqueeze(1).to_broadcast([P, NT, NE]),
                                           op0=ALU.is_ge, op1=ALU.mult)
            then(nc.vector.tensor_tensor(probs[:, :, :], rank, base.unsqueeze(1).to_broadcast([P, NT, NE]), ALU.add))
            then(nc.vector.tensor_tensor(slot[:, :, :], slot[:, :, :], probs[:, :, :], ALU.add))
            then(nc.vector.tensor_tensor(PR, OH, slot[:, :, :].unsqueeze(2).to_broadcast([P, NT, TOPK, NE]), ALU.mult))
            then(nc.vector.reduce_sum(slotk[:, :], PR.rearrange("p t k e -> p (t k) e"), AX.X))
            nc.vector.tensor_copy(sloti[:, :], slotk[:, :]).then_inc(s_slot, 1)
            nc.vector.tensor_scalar(novi[0:1, 0:1], inc[0:1, NE - 1:NE], 1.0, None, ALU.max)
            ove = PR.rearrange("p t k e -> p (t k) e")[0:1, 0:MAXOV]
            then(nc.vector.tensor_tensor(ove, inc[0:1, :].unsqueeze(1).to_broadcast([1, MAXOV, NE]),
                                         iotaf[0:1, 0:MAXOV].unsqueeze(2).to_broadcast([1, MAXOV, NE]), ALU.is_le))
            then(nc.vector.reduce_sum(slotk[0:1, 0:MAXOV], ove, AX.X))
            nc.vector.tensor_scalar(ovei[0:1, 0:MAXOV], slotk[0:1, 0:MAXOV], float(NE - 1), None, ALU.min).then_inc(s_slot, 1)

            def shared_out(t):
                dve.wait_ge(s_dn, t + 1)
                nc.vector.tensor_scalar(SH[:, t, :], BANK[6 + t % 2][:, 0:D], sgate[:, 0, t:t + 1], None, ALU.mult).then_inc(s_sh, 1)

            for t in range(NT):
                dve.wait_ge(s_silu, t + 1)
                dve.wait_ge(s_up, t + 1)
                if t >= 2:
                    dve.wait_ge(s_shtr, t - 1)
                nc.vector.tensor_tensor(shh[t % 2].rearrange("p (a n) -> p a n", a=2), shg.rearrange("p (a n) -> p a n", a=2),
                                        EP[1][:, :, 0:SHH], ALU.mult).then_inc(s_shh, 1)
                if t > 1:
                    shared_out(t - 2)
            shared_out(NT - 2)
            shared_out(NT - 1)

            def hidden_T(e1, b):
                dve.wait_ge(m_ht, e1)
                nc.vector.tensor_copy(HST[b], BANK[4 + b][0:IC, 0:2 * P]).then_inc(m_htev, 1)

            def rows_T(e1, b):
                dve.wait_ge(m_xt, e1)
                nc.vector.tensor_copy(XGT[b], BANK[2 + b][:, 0:D]).then_inc(m_xtev, 1)

            def hidden(e1, b):
                dve.wait_ge(m_silu, e1)
                nc.vector.tensor_tensor(HS[b], SL[b], BANK[b][:, I:2 * I], ALU.mult).then_inc(m_h, 1)

            def expert(e, k, prev, nxt):
                if prev:
                    hidden_T(e, 1 - k % 2)
                if nxt:
                    rows_T(e + 2, 1 - k % 2)
                hidden(e + 1, k % 2)

            rows_T(1, 0)
            for k in range(RING):
                expert(k, k, prev=k > 0, nxt=True)
            with dve.Fori(1, LAPS - 1) as o:
                for k in range(RING):
                    expert(o * RING + k, k, prev=True, nxt=True)
            for e in range(NE - RING, NE):
                expert(e, e, prev=True, nxt=e + 1 < NE)
            hidden_T(NE, 1)
            dve.wait_ge(s_slot, 2)
            nov_r = dve.value_load(novi[0:1, 0:1], min_val=1, max_val=MAXOV)
            with dve.Fori(0, nov_r) as i:
                rows_T(i + (NE + 1), 0)
                hidden(i + (NE + 1), 0)
                hidden_T(i + (NE + 1), 0)

            for t in range(NT):
                dve.wait_ge(s_yg[t], 16 * TOPK)
                for k in range(TOPK):
                    ins = nc.vector.scalar_tensor_tensor(out=SH[:, t, :], in0=YG[t % 4][:, k, :], scalar=top[:, t, k:k + 1],
                                                         in1=SH[:, t, :], op0=ALU.mult, op1=ALU.add)
                    if k < TOPK - 1:
                        then(ins)
                ins.then_inc(s_acc, 1)
                dve.wait_ge(s_acc, t + 1)
                then(nc.vector.tensor_tensor(SH[:, t, :], SH[:, t, :], MOD[:, 5, :], ALU.mult))
                nc.vector.tensor_tensor(x[:, t, :], x[:, t, :], SH[:, t, :], ALU.add).then_inc(s_fin, 1)

        @block.tensor
        def _(pe):
            mm, tr = nc.tensor.matmul, nc.tensor.transpose
            I_ = ident[:, :]

            def transpose_tiles(src, bank, tp):
                for t in range(2):
                    for c in range(NC):
                        o = (t * NC + c) * P
                        ins = tr(bank[:, o:o + P], src[:, 2 * tp + t, c * P:(c + 1) * P], I_)
                return ins

            pe.wait_ge(s_crep, 1)
            pe.wait_ge(ld_mod, 16)
            for b in range(3):
                for c in range(NC):
                    ins = mm(BANK[b], crep[:, c, :], wmod[:, c, 512 * b:512 * b + 512], start=c == 0, stop=c == NC - 1)
            ins.then_inc(s_mod, 1)
            pe.wait_ge(s_ident, 2)
            for tp in range(NT // 2):
                pe.wait_ge(s_h, tp // 2 + 1)
                transpose_tiles(xh, BANK[3 + tp], tp).then_inc(s_tr, 1)
            pe.wait_ge(ld_qkv, 16)
            pe.wait_ge(s_modev, 2)
            for t in range(NT):
                pe.wait_ge(s_trev, max(t // 2 + 1, t - 3))
                for c in range(NC):
                    ins = mm(BANK[(7 + t) % 8][:, 0:QKV], hT[:, c, t * P:(t + 1) * P], wqkv[:, c, :], start=c == 0, stop=c == NC - 1)
                ins.then_inc(s_qkv, 1)
            pe.wait_ge(s_qkvev, NT)
            pe.wait_ge(s_ident, 3)
            for n in range(20):
                h, is_k, j = qk_part(n)
                if n % 10 == 0:
                    pe.wait_ge(s_krep, 4 * (h + 1))
                if n % 10 == 2:
                    pe.wait_ge(s_qa, h + 1)
                if n >= 8:
                    pe.wait_ge(s_qkD if n % 2 else s_qkA, (n - 8) // 2 + 1)
                b = BANK[n % 8].bitcast(bf16)
                for i in range(2):
                    for t in range(4):
                        src = (KS[:, 4 * h + t, j + i, 0:SM] if is_k else QS[:, 4 * h + t, j + i, :])
                        o = (4 * i + t) * P
                        ins = tr(b[0:SM if is_k else SR, o:o + P], src, identb[:, :])
                ins.then_inc(s_qk, 1)
            pe.wait_ge(s_qkA, 10)
            pe.wait_ge(s_qkD, 10)

            ring = [0]

            def fill():
                n = ring[0]
                ring[0] += 1
                if n >= 3:
                    pe.wait_ge(m_free, n - 2)
                return MR[n % 3]

            def scores_for_max(k, heads):
                u, s = divmod(k, NT)
                g, qh = q_unit(u)
                q0 = (4 * qh + s // 2) * P
                for j in heads:
                    mm(fill(), QT[0:SR, 4 * g + j, q0:q0 + P], KT[0:SR, g, 512 * (s % 2):512 * (s % 2) + 512], start=True, stop=True).then_inc(m_fill, 1)

            def transpose_max(u):
                pe.wait_ge(s_negm, u + 1)
                for i in range(2):
                    b = fill().bitcast(bf16)
                    for j in range(2):
                        for t in range(4):
                            o = (4 * j + t) * P
                            ins = tr(b[SR:SM, o:o + P], MS[:, u % 2, t, 2 * i + j, :], identb[:, :])
                    ins.then_inc(m_fill, 1)

            def transpose_output(u):
                pe.wait_ge(s_atev, u + 1)
                b = fill()
                for t in range(4):
                    ins = tr(b[:, t * P:(t + 1) * P], OT[:, t * P:(t + 1) * P], I_)
                ins.then_inc(m_fill, 1)

            def scores(n, p):
                u, tt = divmod(n, NT)
                g, qh = q_unit(u)
                if n:
                    pe.wait_ge(e_done, 2 * (n - 1) + p + 1)
                for i in range(2):
                    j = 2 * p + i
                    ins = mm(EP[p][:, i, :], KT[0:SM, g, tt * P:(tt + 1) * P], QT[0:SM, 4 * g + j, 512 * qh:512 * qh + 512], start=True, stop=True)
                ins.then_inc(e_fill, 1)

            def output(n):
                u, tt = divmod(n, NT)
                g, qh = q_unit(u)
                pe.wait_ge(e_done, 2 * n + 2)
                if tt == 0 and u:
                    pe.wait_ge(s_atev, u)
                for j in range(4):
                    ins = mm(PV[HP * j:HP * j + HP, :], VA[:, tt, g, :], PT[n % 3][:, j, :], start=tt == 0, stop=tt == NT - 1)
                ins.then_inc(pv_step, 1)

            for k in range(LEAD):
                scores_for_max(k, (2, 3, 0, 1))
            transpose_max(0)
            for n in range(STEPS):
                k = n + LEAD
                u = n // NT
                if n % NT == 0:
                    pe.wait_ge(m_free, Q_FILL[u])
                scores(n, 0)
                if k < STEPS:
                    scores_for_max(k, (2, 3))
                if n:
                    output(n - 1)
                if n % NT == 2 and n > NT:
                    transpose_output(u - 1)
                scores(n, 1)
                if k < STEPS:
                    scores_for_max(k, (0, 1))
                if n % NT == NT - 1 and n < STEPS - 1:
                    transpose_max(u + 1)
            output(STEPS - 1)
            transpose_output(U - 1)

            pe.wait_ge(m_free, ring[0])
            for tp in range(NT // 2):
                transpose_tiles(AT, BANK[tp], tp).then_inc(s_at, 1)
            pe.wait_ge(s_wog, 1)
            for tp in range(NT // 2):
                pe.wait_ge(s_trev, NT // 2 + tp + 1)
                for t in range(2):
                    for c in range(NC):
                        ins = mm(BANK[4 + tp][:, t * D:(t + 1) * D], hT[:, c, (2 * tp + t) * P:(2 * tp + t + 1) * P],
                                 wog[:, c, :], start=c == 0, stop=c == NC - 1)
                ins.then_inc(s_ao, 1)
            for tp in range(NT // 2):
                pe.wait_ge(s_h2, tp // 2 + 1)
                transpose_tiles(xh, BANK[tp], tp).then_inc(s_tr2, 1)
            pe.wait_ge(ld_wr, 16)
            for t in range(NT):
                pe.wait_ge(s_tr2ev, t // 2 + 1)
                for c in range(NC):
                    ins = mm(BANK[7][:, t * (NE + 1):(t + 1) * (NE + 1)], h2T[:, c, t * P:(t + 1) * P], wr[:, c, :],
                             start=c == 0, stop=c == NC - 1)
            ins.then_inc(s_lg, 1)

            def ranks():
                pe.wait_ge(s_mask, 1)
                for t in range(NT):
                    for s in range(t):
                        mm(BANK[6][:, t * NE:(t + 1) * NE], onesb[:, :], mask[:, s, :], start=s == 0, stop=False)
                    mm(BANK[6][:, t * NE:(t + 1) * NE], upper[:, :], mask[:, t, :], start=t == 0, stop=True)
                for t in range(NT):
                    ins = mm(BANK[5][:, 0:NE], onesb[:, :], mask[:, t, :], start=t == 0, stop=t == NT - 1)
                ins.then_inc(s_rank, 1)

            def shared_in(t, part, done):
                for a in range(2):
                    for c in range(NC):
                        o = part * ISH + a * SHH
                        ins = mm(EP[part][:, a, 0:SHH], h2T[:, c, t * P:(t + 1) * P], segu[:, c, o:o + SHH], start=c == 0, stop=c == NC - 1)
                ins.then_inc(done, 1)

            def shared_T(t):
                pe.wait_ge(s_shh, t + 1)
                if t:
                    pe.wait_ge(s_shT, t)
                for c in range(NSC):
                    w = P if c < NSC - 1 else SLAST
                    ins = tr(BANK[4 + c // 4][0:w, (c % 4) * P:(c % 4 + 1) * P], shh[t % 2][:, c * P:c * P + w], I_)
                ins.then_inc(s_shtr, 1)

            def shared_down(t):
                pe.wait_ge(s_shT, t + 1)
                if t >= 2:
                    pe.wait_ge(s_sh, t - 1)
                for c in range(NSC):
                    w = P if c < NSC - 1 else SLAST
                    ins = mm(BANK[6 + t % 2][:, 0:D], shT[0:w, c, :], sedn[0:w, c, :], start=c == 0, stop=c == NSC - 1)
                ins.then_inc(s_dn, 1)

            pe.wait_ge(ld_sh, 48)
            for t in range(NT):
                if t:
                    pe.wait_ge(s_silu, t)
                shared_in(t, 0, s_gate)
                if t == 1:
                    ranks()
                if t == 2:
                    pe.wait_ge(s_slot, 1)
                if t > 1:
                    shared_T(t - 2)
                if t:
                    pe.wait_ge(s_shh, t)
                shared_in(t, 1, s_up)
                if t > 1:
                    shared_down(t - 2)
            for t in (NT - 2, NT - 1):
                shared_T(t)
                shared_down(t)

            def rows(b, ld, n):
                pe.wait_ge(ld, n)
                for c in range(NC):
                    ins = tr(BANK[2 + b][:, c * P:(c + 1) * P], XG[b][:, c * P:(c + 1) * P], I_)
                ins.then_inc(m_xt, 1)

            def gate_up(e1, b, r):
                pe.wait_ge(m_xtev, e1)
                for c in range(NC):
                    ins = mm(BANK[b][:, 0:I13], XGT[b][:, c * P:(c + 1) * P], w13[:, r, c * I13:(c + 1) * I13], start=c == 0, stop=c == NC - 1)
                ins.then_inc(m_gu, 1)

            def hidden_T(e1, b):
                pe.wait_ge(m_h, e1)
                for c in range(2):
                    ins = tr(BANK[4 + b][0:IC, c * P:(c + 1) * P], HS[b][:, c * IC:(c + 1) * IC], I_)
                ins.then_inc(m_ht, 1)

            def down(e1, b, r):
                pe.wait_ge(m_htev, e1)
                for c in range(2):
                    ins = mm(BANK[6 + b][:, 0:D], HST[b][:, c * P:(c + 1) * P], w2[:, r, c * D:(c + 1) * D], start=c == 0, stop=c == 1)
                ins.then_inc(m_y, 1)

            def expert(e, k, loads, nxt, first=False):
                b = k % 2
                if k % 2 == 0:
                    pe.wait_ge(ld_w[k // 2], loads)
                gate_up(e + 1, b, k)
                if not (first and k == 0):
                    hidden_T(e, 1 - b)
                if nxt is not None:
                    rows(1 - b, xg_ld[1 - b], nxt)
                if not (first and k < 2):
                    if not (first and k < 4):
                        pe.wait_ge(m_yev, e - 3)
                    down(e - 1, b, (k - 2) % RING)

            pe.wait_ge(s_sh, NT)
            rows(0, xg_ld[0], 16)
            for k in range(RING):
                expert(k, k, 32, 16 * ((k + 1) // 2 + 1), first=True)
            with pe.Fori(1, LAPS - 1) as o:
                for k in range(RING):
                    expert(o * RING + k, k, o * 32 + 32, o * (16 * RING // 2) + 16 * ((k + 1) // 2 + 1))
            for e in range(NE - RING, NE):
                expert(e, e % RING, 32 * LAPS, 16 * ((e + 1) // 2 + 1) if e + 1 < NE else None)
            hidden_T(NE, 1)
            pe.wait_ge(m_yev, NE - 3)
            down(NE - 1, 0, RING - 2)
            pe.wait_ge(m_yev, NE - 2)
            down(NE, 1, RING - 1)
            pe.wait_ge(s_slot, 2)
            nov = pe.value_load(novi[0:1, 0:1], min_val=1, max_val=MAXOV)
            with pe.Fori(0, nov) as i:
                rows(0, o_ld, i * 48 + 48)
                gate_up(i + (NE + 1), 0, 0)
                hidden_T(i + (NE + 1), 0)
                pe.wait_ge(m_yev, i + NE)
                down(i + (NE + 1), 0, 0)


def kernel(**inputs):
    import numpy as np
    import concourse.bacc as bacc
    from concourse.bass_utils import run_bass_kernel_spmd

    a = {k[3:]: np.asarray(v) for k, v in inputs.items()}
    S, D = a["attn_hidden_states"].shape[1:]
    P, NC = 128, D // 128
    E, I2, _ = a["ffn_w13"].shape
    I = I2 // 2
    half = 8
    inv = (np.float32(1.0) / np.float32(10000.0) ** (np.arange(0, half, 2, dtype=np.float32) / np.float32(half))).astype(np.float32)
    ang = np.arange(S, dtype=np.float32)[:, None] * inv[None, :]
    table = lambda f: np.ascontiguousarray(f(ang).astype(np.float32).reshape(S // P, P, half // 2).transpose(1, 0, 2))
    arrays = {
        "x": a["attn_hidden_states"][0],
        "cos": table(np.cos), "sin": table(np.sin),
        "c": a["c"][0].reshape(NC, P).T,
        "wmod": a["wmod"],
        "wqkv": np.concatenate([a["attn_Wq"], a["attn_Wk"], a["attn_Wv"]], axis=1),
        "wo": a["attn_Wo"],
        "wr": np.concatenate([a["ffn_gate_w"], a["ffn_shared_gate_w"]], axis=0).T,
        "segu": a["ffn_se_gate_up_w"].T,
        "sedn": a["ffn_se_down_w"].T,
        "w13": a["ffn_w13"].reshape(E, I2, NC, P).transpose(0, 3, 2, 1).reshape(E, P, NC * I2),
        "w2": a["ffn_w2"].reshape(E, D, 2, I // 2).transpose(0, 3, 2, 1).reshape(E, I // 2, 2 * D),
    }
    arrays = {k: np.ascontiguousarray(v) for k, v in arrays.items()}
    nc = bacc.Bacc("TRN2", target_bir_lowering=False, num_devices=1)
    f32 = mybir.dt.float32
    args = [nc.dram_tensor("in_" + k, v.shape, f32, kind="ExternalInput").ap() for k, v in arrays.items()]
    rows = (E + S * 4 // P - 1) * P
    tables = [nc.dram_tensor(k, (rows, D), f32, kind="Internal").ap() for k in ("xdisp", "ydisp")]
    o = nc.dram_tensor("out", (S, D), f32, kind="ExternalOutput").ap()
    adaln_layer(nc, *args, *tables, o)
    r = run_bass_kernel_spmd(nc, [{"in_" + k: v for k, v in arrays.items()}], core_ids=[0])
    return np.asarray(r.results[0]["out"]).reshape(1, S, D)
```

```python
import concourse.bass as bass
from concourse import mybir
from contextlib import ExitStack


def adaln_layer(nc, x_in, cos_in, sin_in, c_in, wmod_in, wqkv_in, wo_in, wr_in, segu_in, sedn_in,
                w13_in, w2_in, xdisp, ychoice, out):
    f32, bf16, i32, u32 = mybir.dt.float32, mybir.dt.bfloat16, mybir.dt.int32, mybir.dt.uint32
    ALU, ACT, AX = mybir.AluOpType, mybir.ActivationFunctionType, mybir.AxisListType

    S, D = x_in.shape
    P = 128
    NT, NC = S // P, D // P
    HD, NH, NG = 16, 16, 4
    HP = 32
    Q_PARTS, K_PARTS = "hhhmml", "hmlhmh"
    SR = 6 * HD
    SM = SR + 2
    QKV = (NH + 2 * NG) * HD
    NE, TOPK = 60, 4
    I13 = w13_in.shape[2] // NC
    I = I13 // 2
    IC = I // 2
    ISH = segu_in.shape[1] // 2
    SHH = ISH // 2
    NSC = (ISH + P - 1) // P
    SLAST = ISH - (NSC - 1) * P
    MAXOV = (S * TOPK) // P - 1
    EPS = 1e-5
    RING = 10
    LAPS = NE // RING
    BUFS = 5
    U = 2 * NG
    LEAD = NT + 1
    STEPS = U * NT

    Q_FILL, O_FILL = [4 * LEAD + 2], []
    fills = 4 * LEAD + 2
    for n in range(STEPS):
        half = 2 * (n + LEAD < STEPS)
        fills += half
        if n % NT == 2 and n > NT:
            fills += 1
            O_FILL.append(fills)
        if n % NT == NT - 1 and n < STEPS - 1:
            fills += 2
            Q_FILL.append(fills)
        fills += half
    EARLY = NT - 1
    AT_BANK, WO_BANK, H2_BANK = (4, 5, 5, 7), (7, 4, 4, 5), (5, 7, 7, 4)
    NB = xdisp.shape[0] // P
    POOL_TILES = (2, 5)
    RW = D + 1
    N_EMPTY = BUFS + 1

    ctx = ExitStack()
    with ctx:
        def sb(name, shape, dt=f32):
            return ctx.enter_context(nc.sbuf_tensor(name, shape, dt))

        def ps(name, shape):
            return ctx.enter_context(nc.psum_tensor(name, shape, f32))

        def sem(name):
            return ctx.enter_context(nc.semaphore(name))

        x = sb("x", [P, NT, D])
        xh = sb("xh", [P, NT, RW])
        hT = sb("hT", [P, NC, S])
        qkv = sb("qkv", [P, NT, QKV])
        QS = sb("QS", [P, NT, NH, SR], bf16)
        QT = sb("QT", [P, NH, S], bf16)
        KT = sb("KT", [P, NG, S], bf16)
        MS = sb("MS", [P, 2, 4, 4, 2], bf16)
        negm = sb("negm", [P, 2, 4, 4])
        SC = sb("SC", [P, 2048])
        VA = sb("VA", [P, NT, NG, HP])
        QSf = QS[:, :, :, :].rearrange("p t h c -> p (t h c)").bitcast(f32)
        PT = [QSf[:, 2048 * b:2048 * b + 2048].rearrange("p (j q) -> p j q", j=4) for b in range(3)]
        OT = sb("OT", [P, 512])
        MOD = sb("MOD", [P, 6, D])
        modc = sb("modc", [P, 6, NC])
        wide = sb("wide", [P, NC * 6 * D])
        wqkv = sb("wqkv", [P, NC, QKV])
        wo = sb("wo", [P, NC, D])
        wr = sb("wr", [P, NC, NE + 1])
        segu = sb("segu", [P, NC, 2 * ISH])
        sedn = sb("sedn", [P, NSC, D])
        w13 = sb("w13", [P, RING, NC * I13])
        w2 = sb("w2", [IC, RING, 2 * D])
        ident = sb("ident", [P, P])
        identb = sb("identb", [P, P], bf16)
        ones = sb("ones", [P, P])
        upper = sb("upper", [P, P], bf16)
        onesb = sb("onesb", [P, P], bf16)
        cosr = sb("cosr", [P, NT, 4])
        sinr = sb("sinr", [P, NT, 4])
        ccol = sb("ccol", [P, 4, NC])
        stats = sb("stats", [P, NT, 6])
        mv = sb("mv", [P, NT, 2])
        veps = sb("veps", [P, NT])
        mhalf = sb("mhalf", [P, NT])
        rstd = sb("rstd", [P, NT])
        mx = sb("mx", [P, 2, 4, 4, 2])
        rsum = sb("rsum", [P, 2, 4, 4])
        iota_i = sb("iota_i", [P, NE], i32)
        iotaf = sb("iotaf", [P, NE])
        place_i = sb("place_i", [P, TOPK, NT], u32)
        spare_i = sb("spare_i", [P, BUFS], u32)
        zero = sb("zero", [P, 2], u32)
        yplace = sb("yplace", [P, BUFS], u32)
        top = sb("top", [P, NT, 8])
        topi = sb("topi", [P, NT, 8], u32)
        topf = sb("topf", [P, NT, 8])
        sgate = sb("sgate", [P, 2, NT])
        slotk = sb("slotk", [P, NT * TOPK])
        sloti = sb("sloti", [P, NT * TOPK], u32)
        novi = sb("novi", [1, 1], i32)
        ovei = sb("ovei", [1, MAXOV + 1], i32)
        KS = SC[:, :].bitcast(bf16)[:, 0:NT * NG * (SM + 2)].rearrange("p (t g c) -> p t g c", t=NT, g=NG)
        crep = SC[:, 1600:1600 + NC * P].rearrange("p (c n) -> p c n", c=NC)
        rt = xh[:, :, :].rearrange("p t n -> p (t n)")[:, 0:16 * (NH + NG) * 4].rearrange("p (k t n) -> p k t n", k=4, t=4)
        small = wqkv[:, :, :].rearrange("p c n -> p (c n)")
        empty = SC[:, 0:BUFS * RW].rearrange("p (b n) -> p b n", b=BUFS)
        grid = NT * NE
        probs = SC[:, 0:grid].rearrange("p (t e) -> p t e", t=NT)
        slot = SC[:, grid:2 * grid].rearrange("p (t e) -> p t e", t=NT)
        mask = SC[:, :].bitcast(bf16)[:, 4 * grid:5 * grid].rearrange("p (t e) -> p t e", t=NT)
        gt = SC[:, 3 * grid:3 * grid + NE * (NT - 1)].rearrange("p (e k) -> p e k", e=NE)
        gtmp = OT[:, 0:2 * D].rearrange("p (k n) -> p k n", k=2)
        wog = wide[:, 0:NC * D].rearrange("p (c n) -> p c n", c=NC)
        AT = qkv[:, :, :].rearrange("p t n -> p (t n)")[:, 0:NT * D].rearrange("p (t n) -> p t n", t=NT)
        QTf = QT[:, :, :].rearrange("p h s -> p (h s)").bitcast(f32)
        SH = QTf[:, 0:NT * D].rearrange("p (t n) -> p t n", t=NT)
        OH = QTf[:, 2048:2048 + NT * TOPK * NE].rearrange("p (t k e) -> p t k e", t=NT, k=TOPK)
        PR = QTf[:, 4096:4096 + NT * TOPK * NE].rearrange("p (t k e) -> p t k e", t=NT, k=TOPK)
        h2T = QTf[:, 6144:6144 + NC * S].rearrange("p (c s) -> p c s", c=NC)
        rows3 = lambda v: v.rearrange("p (t n) -> p t n", t=NT)
        XC = [xh, rows3(QSf[:, 0:NT * RW]), rows3(QSf[:, NT * RW:2 * NT * RW]),
              rows3(qkv[:, :, :].rearrange("p t n -> p (t n)")[:, 0:NT * RW])]
        at = [0]

        def carve(rows, width, n):
            at[0] += width * n
            return [QSf[0:rows, at[0] - width * (n - b):at[0] - width * (n - b) + width] for b in range(n)]

        XG, YS, XGT = carve(P, RW, BUFS), carve(P, D, BUFS), carve(P, D, 2)
        SL, HS, HST = carve(P, I, 2), carve(P, I, 2), carve(IC, 2 * P, 2)
        wmod = wide[:, :].rearrange("p (c n) -> p c n", c=NC)
        shg = wide[:, 0:ISH]
        shh = [wide[:, ISH * (1 + b):ISH * (2 + b)] for b in range(2)]
        shT = wide[:, 3 * ISH:3 * ISH + NSC * P].rearrange("p (c n) -> p c n", c=NSC)
        ringf = w13[:, :, :].rearrange("p r n -> p (r n)")
        KTf = KT[:, :, :].rearrange("p h s -> p (h s)").bitcast(f32)
        YG = [v[:, TOPK * D * b:TOPK * D * (b + 1)].rearrange("p (k n) -> p k n", k=TOPK)
              for v, b in [(ringf, b) for b in range(NT - 2)] + [(KTf, 0), (KTf, 1)]]

        EP = [ps(f"EP{p}", [P, 2, 512]) for p in range(2)]
        M2 = ps("M2", [P, 2, 512])
        PV = ps("PV", [P, 512])
        M3 = ps("M3", [P, 512])
        BANK = [EP[0][:, 0], EP[0][:, 1], EP[1][:, 0], EP[1][:, 1], M2[:, 0], M2[:, 1], PV[:, :], M3[:, :]]
        MR = [BANK[4], BANK[5], BANK[7]]

        ld_x, ld_c, ld_rope, ld_mod = [sem("ld_x0"), sem("ld_x1")], sem("ld_c"), sem("ld_rope"), [sem("ld_mod0"), sem("ld_mod1")]
        ld_qkv, ld_wo, ld_wr, ld_sh = sem("ld_qkv"), sem("ld_wo"), sem("ld_wr"), sem("ld_sh")
        ld_w = [sem(f"ld_w{r}") for r in range(RING // 2)]
        empty_st, empty_ok = sem("empty_st"), sem("empty_ok")
        s_place, s_placed, s_xc, m_place = sem("s_place"), sem("s_placed"), sem("s_xc"), sem("m_place")
        s_ident, s_const, s_iota, s_pad, s_rstd, s_va, s_ks = (sem(n) for n in ("s_ident", "s_const", "s_iota", "s_pad", "s_rstd", "s_va", "s_ks"))
        s_ec, s_crep, s_mod, s_modev, s_modc, s_mod1 = (sem(n) for n in ("s_ec", "s_crep", "s_mod", "s_modev", "s_modc", "s_mod1"))
        s_var, s_h, s_tr, s_trev = (sem(n) for n in ("s_var", "s_h", "s_tr", "s_trev"))
        s_qkv, s_qkvev, s_rope, s_split, s_qs, s_qa = (sem(n) for n in ("s_qkv", "s_qkvev", "s_rope", "s_split", "s_qs", "s_qa"))
        s_qk, s_qkd, s_qkA, s_qkD = (sem(n) for n in ("s_qk", "s_qkd", "s_qkA", "s_qkD"))
        m_fill, m_free, a_free, s_negm = sem("m_fill"), sem("m_free"), sem("a_free"), sem("s_negm")
        e_fill, e_done, pv_step = sem("e_fill"), sem("e_done"), sem("pv_step")
        s_at, s_atev, s_wog, s_ao, s_x1 = (sem(n) for n in ("s_at", "s_atev", "s_wog", "s_ao", "s_x1"))
        s_var2, s_h2, s_tr2, s_tr2ev = (sem(n) for n in ("s_var2", "s_h2", "s_tr2", "s_tr2ev"))
        s_lg, s_ld, s_pe, s_mask, s_rank, s_cnt, s_slot, s_disp = (sem(n) for n in ("s_lg", "s_ld", "s_pe", "s_mask", "s_rank", "s_cnt", "s_slot", "s_disp"))
        s_gate, s_up, s_silu, s_shh, s_shtr, s_shT, s_dn, s_sh = (sem(n) for n in ("s_gate", "s_up", "s_silu", "s_shh", "s_shtr", "s_shT", "s_dn", "s_sh"))
        xg_ld, y_st = [sem(f"xg_ld{b}") for b in range(BUFS)], [sem(f"y_st{b}") for b in range(BUFS)]
        m_xt, m_xtev, m_gu, m_silu, m_h, m_ht, m_htev, m_y, m_yev = (sem(f"m_{n}") for n in ("xt", "xtev", "gu", "silu", "h", "ht", "htev", "y", "yev"))
        o_ld = sem("o_ld")
        s_yg = [sem(f"s_yg{t}") for t in range(NT)]
        s_acc, s_fin, out_st, dv, s_xm, s_base, s_finp, s_weighted, s_raw = sem("s_acc"), sem("s_fin"), sem("out_st"), sem("dv"), sem("s_xm"), sem("s_base"), sem("s_finp"), sem("s_weighted"), sem("s_raw")

        block = ctx.enter_context(nc.Block())

        def q_unit(n):
            return divmod(n, 2)

        QK = [(0, True, 0), (0, False, 0), (0, False, 2), (0, True, 2)] + [(0, False, j) for j in range(4, NH, 2)] + \
             [(1, False, 0), (1, False, 2), (1, True, 2)] + [(1, False, j) for j in range(4, NH, 2)]
        QK_FIRST, QK_H1 = 4, 10
        QK_DVE = (1, True, 0)

        tt1 = slice(NT // 2, NT)
        q1 = qkv[:, tt1, 0:NH * HD].rearrange("p t (h d) -> p t h d", d=HD)

        def q1_part(c):
            return QS[:, tt1, :, HD * Q_PARTS.index(c):HD * Q_PARTS.index(c) + HD]

        def qk_evac(item, bank):
            h, is_k, j = item
            rows = SM if is_k else SR
            return ((KT if is_k else QT)[0:rows, j:j + 2, 512 * h:512 * h + 512],
                    bank[0:rows, :].bitcast(bf16).rearrange("p (j s) -> p j s", j=2))

        @block.sync
        def _(sp):
            wm = wmod_in.rearrange("(c p) n -> p c n", p=P)
            for h in range(2):
                sp.dma_start(x[:, 4 * h:4 * h + 4, :],
                             x_in[512 * h:512 * h + 512, :].rearrange("(t p) d -> p t d", p=P)).then_inc(ld_x[h], 16)
                if h == 0:
                    sp.dma_start(ccol[:, 0, :], c_in).then_inc(ld_c, 16)
                    sp.dma_start(wmod[:, :, 0:2 * D], wm[:, :, 0:2 * D]).then_inc(ld_mod[0], 16)
            sp.dma_start(wqkv[:, :, :], wqkv_in.rearrange("(c p) n -> p c n", p=P)).then_inc(ld_qkv, 16)
            sp.dma_start(cosr[:, :, :], cos_in).then_inc(ld_rope, 16)
            sp.dma_start(sinr[:, :, :], sin_in).then_inc(ld_rope, 16)
            sp.dma_start(wmod[:, :, 2 * D:6 * D], wm[:, :, 2 * D:6 * D]).then_inc(ld_mod[1], 16)
            sp.dma_start(wo[:, :, :], wo_in.rearrange("(c p) n -> p c n", p=P)).then_inc(ld_wo, 16)
            sp.dma_start(wr[:, :, :], wr_in.rearrange("(c p) n -> p c n", p=P)).then_inc(ld_wr, 16)
            sp.dma_start(segu[:, :, :], segu_in.rearrange("(c p) n -> p c n", p=P)).then_inc(ld_sh, 16)
            sp.dma_start(sedn[:, 0:NSC - 1, :],
                         sedn_in[0:(NSC - 1) * P, :].rearrange("(c p) n -> p c n", p=P)).then_inc(ld_sh, 16)
            sp.dma_start(sedn[0:SLAST, NSC - 1, :], sedn_in[(NSC - 1) * P:ISH, :]).then_inc(ld_sh, 16)

            def load_pair(e, k):
                sp.dma_start(w13[:, k:k + 2, :], w13_in[bass.ds(e, 2), :, :].rearrange("e p n -> p e n")).then_inc(ld_w[k // 2], 16)
                sp.dma_start(w2[:, k:k + 2, :], w2_in[bass.ds(e, 2), :, :].rearrange("e p n -> p e n")).then_inc(ld_w[k // 2], 16)

            for k in range(0, RING, 2):
                load_pair(k, k)
            sp.wait_ge(empty_ok, 2)
            full = NB - NB % BUFS
            for b in range(BUFS):
                sp.dma_start(xdisp[0:full * P, :].rearrange("(a b p) n -> b p a n", b=BUFS, p=P)[b],
                             empty[:, b, :].unsqueeze(1).to_broadcast([P, full // BUFS, RW])).then_inc(empty_st, 16)
            sp.dma_start(xdisp[full * P:, :].rearrange("(b p) n -> p b n", p=P), empty[:, 0:NB - full, :]).then_inc(empty_st, 16)

            def load_rows(e, b):
                sp.dma_start(XG[b], xdisp[bass.ds(e * P, P), :]).then_inc(xg_ld[b], 16)

            def expert(e, k, weights, rows):
                if weights and k % 2 == 0:
                    sp.wait_ge(m_y, e - 2)
                    load_pair(e + 6, (k + 6) % RING)
                if rows:
                    sp.wait_ge(m_xt, e + 1)
                    sp.wait_ge(m_place, e + 1)
                    load_rows(e + BUFS, k % BUFS)

            def overflow_weights(b, done):
                x = sp.value_load(ovei[0:1, bass.ds(b, 1)], min_val=0, max_val=NE - 1)
                sp.dma_start(w13[:, 0, :], w13_in[bass.ds(x, 1), :, :].rearrange("e p n -> p (e n)")).then_inc(done, 16)
                sp.dma_start(w2[:, 0, :], w2_in[bass.ds(x, 1), :, :].rearrange("e p n -> p (e n)")).then_inc(done, 16)

            sp.wait_ge(s_disp, 16 * NT * TOPK)
            for b in range(BUFS):
                load_rows(b, b)
            for k in range(RING):
                expert(k, k, weights=k >= 4, rows=True)
            with sp.Fori(1, LAPS - 1) as o:
                for k in range(RING):
                    expert(o * RING + k, k, weights=True, rows=True)
            sp.wait_ge(s_slot, 3)
            for e in range(NE - RING, NE + 1 - BUFS):
                if e == NE - 6:
                    sp.wait_ge(m_y, NE - RING + 1)
                    overflow_weights(0, ld_w[0])
                expert(e, e % RING, weights=e + 7 < NE, rows=True)
            nov = sp.value_load(novi[0:1, 0:1], min_val=1, max_val=MAXOV)
            with sp.If(nov > 1):
                with sp.Fori(1, nov) as b:
                    sp.wait_ge(m_yev, b + NE)
                    sp.wait_ge(m_place, b + NE)
                    overflow_weights(b, o_ld)
                    sp.dma_start(XG[0], xdisp[bass.ds((b + NE) * P, P), :]).then_inc(o_ld, 16)
            for b in range(1, BUFS):
                sp.wait_ge(y_st[b], 16 * (NE // BUFS))
            sp.wait_ge(y_st[0], nov * 16 + 16 * (NE // BUFS))
            for t in range(NT):
                sp.dma_start(YG[t], ychoice[TOPK * P * t:TOPK * P * (t + 1), :].rearrange("(p k) n -> p k n", k=TOPK)).then_inc(s_yg[t], 16)
            for t in range(NT):
                by_pool = sum(p <= t for p in POOL_TILES)
                if t in POOL_TILES:
                    sp.wait_ge(s_finp, by_pool)
                else:
                    sp.wait_ge(s_fin, t + 1 - by_pool)
                sp.dma_start(out[t * P:(t + 1) * P, :], x[:, t, :]).then_inc(out_st, 16)
            sp.wait_ge(out_st, 16 * NT)

        @block.gpsimd
        def _(pool):
            pool.memset(ident[:, :], 0.0).then_inc(s_ident, 1)
            pool.memset(ones[:, :], 1.0).then_inc(s_const, 1)
            pool.memset(onesb[:, :], 1.0).then_inc(s_const, 1)
            pool.wait_ge(s_ident, 1)
            pool.affine_select(out=ident[:, :], in_=ident[:, :], compare_op=ALU.not_equal, fill=1.0,
                               base=0, pattern=[[-1, P]], channel_multiplier=1).then_inc(s_ident, 1)
            pool.memset(mhalf[:, :], -0.5).then_inc(s_const, 1)
            for h in range(2):
                pool.wait_ge(s_const, 3)
                pool.wait_ge(s_var, h + 1)
                pool.tensor_tensor(rstd[:, 4 * h:4 * h + 4], veps[:, 4 * h:4 * h + 4], mhalf[:, 0:4], ALU.pow).then_inc(s_rstd, 1)
            pool.memset(KS[:, :, :, SR:SM], 1.0).then_inc(s_pad, 1)
            pool.wait_ge(s_ident, 2)
            pool.tensor_copy(identb[:, :], ident[:, :]).then_inc(s_ident, 1)
            pool.memset(VA[:, :, :, :], 0.0).then_inc(s_pad, 1)
            pool.wait_ge(s_pad, 2)
            pool.memset(VA[:, :, :, HD:HD + 1], 1.0).then_inc(s_pad, 1)
            pool.wait_ge(s_pad, 3)
            for h in range(2):
                tt = slice(4 * h, 4 * h + 4)
                pool.wait_ge(s_qkvev, 4 * h + 4)
                pool.tensor_copy(VA[:, tt, :, 0:HD],
                                 qkv[:, tt, (NH + NG) * HD:].rearrange("p t (g d) -> p t g d", g=NG)).then_inc(s_va, 1)
            pool.wait_ge(s_qs, 1)
            pool.tensor_tensor(q1, q1, q1_part("h"), ALU.subtract).then_inc(s_qs, 1)
            pool.wait_ge(s_qs, 3)
            pool.tensor_tensor(q1_part("l"), q1, q1_part("m"), ALU.subtract).then_inc(s_qs, 1)
            pool.memset(zero[:, :], 0).then_inc(s_place, 1)
            pool.iota(place_i[:, :, :], pattern=[[1, TOPK], [TOPK * P, NT]], base=0, channel_multiplier=TOPK).then_inc(s_place, 1)
            pool.iota(spare_i[:, :], pattern=[[P, BUFS]], base=S * TOPK, channel_multiplier=1).then_inc(s_place, 1)
            pool.wait_ge(s_qk, QK_H1 + 3)
            pool.wait_ge(s_qkd, 1)
            pool.memset(empty[:, :, 0:D], 0.0).then_inc(empty_ok, 1)
            pool.wait_ge(s_place, 3)
            pool.tensor_copy(empty[:, :, D].bitcast(u32), spare_i[:, :]).then_inc(empty_ok, 1)
            pool.affine_select(out=upper[:, :], in_=onesb[:, :], compare_op=ALU.is_gt, fill=0.0,
                               base=0, pattern=[[1, P]], channel_multiplier=-1).then_inc(s_const, 1)
            pool.iota(iota_i[:, :], pattern=[[1, NE]], base=0, channel_multiplier=0).then_inc(s_iota, 1)
            pool.wait_ge(s_iota, 1)
            pool.tensor_copy(iotaf[:, :], iota_i[:, :]).then_inc(s_iota, 1)
            for h in range(2):
                tt = slice(4 * h, 4 * h + 4)
                pool.wait_ge(s_var2, h + 1)
                pool.tensor_tensor(rstd[:, tt], veps[:, tt], mhalf[:, 0:4], ALU.pow).then_inc(s_rstd, 1)
                pool.wait_ge(s_tr2, 2 * h + 2)
                pool.tensor_tensor(xh[:, tt, 0:D], xh[:, tt, 0:D], MOD[:, 4:5, :].to_broadcast([P, 4, D]), ALU.mult).then_inc(s_xm, 1)
                pool.wait_ge(s_xm, 2 * h + 1)
                pool.tensor_tensor(xh[:, tt, 0:D], xh[:, tt, 0:D], MOD[:, 3:4, :].to_broadcast([P, 4, D]), ALU.add).then_inc(s_xm, 1)
            pool.wait_ge(s_at, NT // 2)
            for k in range(TOPK):
                pool.tensor_copy(XC[k][:, :, D].bitcast(u32), place_i[:, k, :]).then_inc(s_placed, 1)
            pool.wait_ge(empty_st, 16 * N_EMPTY)
            pool.wait_ge(s_placed, TOPK)
            pool.wait_ge(s_xc, 2)
            pool.wait_ge(s_slot, 1)
            pool.wait_ge(s_xm, 4)
            for t in range(NT):
                if t == 2:
                    pool.wait_ge(s_slot, 2)
                for k in range(TOPK):
                    i = t * TOPK + k
                    pool.indirect_dma_start(out=xdisp, out_offset=bass.IndirectOffsetOnAxis(ap=sloti[:, i:i + 1], axis=0),
                                            in_=XC[k][:, t, :], in_offset=None).then_inc(s_disp, 16)

            pool.wait_ge(s_sh, EARLY)
            pool.tensor_tensor(x[:, 0:EARLY, :], x[:, 0:EARLY, :], SH[:, 0:EARLY, :], ALU.add).then_inc(s_base, 1)

            def send(e, b, ld, n, sent):
                pool.wait_ge(ld, n)
                if sent is not None:
                    pool.wait_ge(y_st[b], sent)
                pool.tensor_tensor(yplace[:, b:b + 1], XG[b][:, D:RW].bitcast(u32), zero[:, 0:1], ALU.add).then_inc(m_place, 1)
                pool.wait_ge(m_place, e + 1)
                pool.wait_ge(m_yev, e + 1)
                pool.tensor_tensor(zero[:, 1:2], zero[:, 0:1], zero[:, 0:1], ALU.add)
                pool.indirect_dma_start(out=ychoice, out_offset=bass.IndirectOffsetOnAxis(ap=yplace[:, b:b + 1], axis=0),
                                        in_=YS[b], in_offset=None).then_inc(y_st[b], 16)

            for e in range(BUFS):
                send(e, e, xg_ld[e], 16, None)
            with pool.Fori(1, NE // BUFS) as o:
                for b in range(BUFS):
                    send(o * BUFS + b, b, xg_ld[b], o * 16 + 16, o * 16)
            send(NE, 0, xg_ld[0], 16 * (NE // BUFS + 1), 16 * (NE // BUFS))
            pool.wait_ge(s_slot, 3)
            nov = pool.value_load(novi[0:1, 0:1], min_val=1, max_val=MAXOV)
            with pool.If(nov > 1):
                with pool.Fori(1, nov) as i:
                    send(i + NE, 0, o_ld, i * 48, i * 16 + 16 * (NE // BUFS))
            for n, t in enumerate(POOL_TILES):
                pool.wait_ge(s_weighted, TOPK * (n + 1))
                for k in range(TOPK):
                    ins = pool.tensor_tensor(x[:, t, :], x[:, t, :], YG[t][:, k, :], ALU.add)
                    if k < TOPK - 1:
                        ins.then_inc(s_acc, 1)
                        pool.wait_ge(s_acc, n * (TOPK - 1) + k + 1)
                ins.then_inc(s_finp, 1)

        @block.scalar
        def _(act):
            act.wait_ge(ld_c, 16)
            nc.scalar.activation(ccol[:, 1, :], ccol[:, 0, :], ACT.Exp, scale=-1.0).then_inc(s_ec, 1)
            def modulated(dst, bank, tp, k):
                for c in range(NC):
                    ins = nc.scalar.activation(dst[:, c, 256 * tp:256 * tp + 256].rearrange("p (t n) -> p t n", t=2),
                                               bank.rearrange("p (t c n) -> p t c n", t=2, c=NC)[:, :, c, :], ACT.Identity,
                                               scale=modc[:, k + 1, c:c + 1], bias=modc[:, k, c:c + 1])
                return ins

            act.wait_ge(s_modc, 1)
            def rows_T1(tp):
                act.wait_ge(s_tr, tp + 1)
                modulated(hT, BANK[3 + tp], tp, 0).then_inc(s_trev, 1)

            rows_T1(0)
            rows_T1(1)
            for t in range(NT):
                if t == 2:
                    rows_T1(2)
                    rows_T1(3)
                act.wait_ge(s_qkv, t + 1)
                nc.scalar.activation(qkv[:, t, :], BANK[(7 + t) % 8][:, 0:QKV], ACT.Copy).then_inc(s_qkvev, 1)

            def q_copies(h):
                tt = slice(4 * h, 4 * h + 4)
                for i in (1, 2, 4):
                    o = HD * Q_PARTS.index(Q_PARTS[i])
                    ins = nc.scalar.activation(QS[:, tt, :, HD * i:HD * i + HD], QS[:, tt, :, o:o + HD], ACT.Copy)
                ins.then_inc(s_qa, 1)

            act.wait_ge(s_split, 1)
            q_copies(0)
            act.wait_ge(s_mod, 2)
            for b in range(2):
                nc.scalar.activation(MOD[:, 2 + 2 * b:4 + 2 * b, :], BANK[4 + b].rearrange("p (b n) -> p b n", b=2), ACT.Copy).then_inc(s_modev, 1)
            nc.scalar.activation(modc[:, 3:5, :], BANK[3][:, 2 * NC:4 * NC].rearrange("p (k c) -> p k c", k=2), ACT.Copy).then_inc(s_modev, 1)
            for n, item in enumerate(QK):
                if n == QK_FIRST - 1:
                    act.wait_ge(s_rope, 2)
                    nc.scalar.activation(q1_part("h"), q1, ACT.Copy).then_inc(s_qs, 1)
                if n == QK_FIRST:
                    act.wait_ge(s_qs, 2)
                    nc.scalar.activation(q1_part("m"), q1, ACT.Copy).then_inc(s_qs, 1)
                if n == QK_H1:
                    act.wait_ge(s_qs, 4)
                    q_copies(1)
                act.wait_ge(s_qk, n + 1)
                dst, src = qk_evac(item, BANK[n % 4])
                nc.scalar.activation(dst, src, ACT.Copy).then_inc(s_qkA, 1)

            def take_max(u):
                g, qh = q_unit(u)
                for i in range(2):
                    f = Q_FILL[u] - 1 + i
                    act.wait_ge(m_fill, f)
                    src = MR[(f - 1) % 3][SR:SM, :].bitcast(bf16).rearrange("p (j s) -> p j s", j=2)
                    nc.scalar.activation(QT[SR:SM, 4 * g + 2 * i:4 * g + 2 * i + 2, 512 * qh:512 * qh + 512], src, ACT.Copy).then_inc(a_free, 1)

            def attention_T(tp):
                act.wait_ge(s_at, tp + 1)
                for c in range(NC):
                    ins = nc.scalar.activation(hT[:, c, 256 * tp:256 * tp + 256].rearrange("p (t n) -> p t n", t=2),
                                               BANK[AT_BANK[tp]].rearrange("p (t c n) -> p t c n", t=2, c=NC)[:, :, c, :], ACT.Copy)
                ins.then_inc(s_trev, 1)

            def rows_T2(tp):
                act.wait_ge(s_tr2, tp + 1)
                modulated(h2T, BANK[H2_BANK[tp]], tp, 3).then_inc(s_tr2ev, 1)

            def row_copies(h):
                act.wait_ge(s_xm, 2 * h + 2)
                tt = slice(4 * h, 4 * h + 4)
                for k in range(1, TOPK):
                    ins = nc.scalar.activation(XC[k][:, tt, 0:D], xh[:, tt, 0:D], ACT.Copy)
                ins.then_inc(s_xc, 1)

            def router_exp(h):
                act.wait_ge(s_ld, h + 1)
                tt = slice(4 * h, 4 * h + 4)
                nc.scalar.activation(probs[:, tt, :], probs[:, tt, :], ACT.Exp).then_inc(s_pe, 1)

            take_max(0)
            for n in range(STEPS):
                for p in range(2):
                    if p == 1 and n % NT == 1 and n > NT:
                        u = n // NT - 1
                        act.wait_ge(pv_step, NT * (u + 1))
                        if u:
                            act.wait_ge(m_fill, O_FILL[u - 1])
                        nc.scalar.activation(OT[:, :], PV[:, :], ACT.Copy).then_inc(s_atev, 1)
                    if p == 1 and n % NT == NT - 1 and n < STEPS - 1:
                        take_max(n // NT + 1)
                    act.wait_ge(e_fill, 2 * n + p + 1)
                    if n >= 3 and p == 0:
                        act.wait_ge(pv_step, n - 2)
                    nc.scalar.activation(PT[n % 3][:, 2 * p:2 * p + 2, :], EP[p][:, :, :], ACT.Exp, scale=HD ** -0.5).then_inc(e_done, 1)
                if n == STEPS - 5:
                    attention_T(0)
                    attention_T(1)
            act.wait_ge(pv_step, STEPS)
            act.wait_ge(m_fill, O_FILL[U - 2])
            nc.scalar.activation(OT[:, :], PV[:, :], ACT.Copy).then_inc(s_atev, 1)
            act.wait_ge(s_mod1, 1)
            rows_T2(0)
            rows_T2(1)
            router_exp(0)
            attention_T(2)
            attention_T(3)
            row_copies(0)
            act.wait_ge(s_gate, 1)
            nc.scalar.activation(shg.rearrange("p (a n) -> p a n", a=2), EP[0][:, :, 0:SHH], ACT.Copy).then_inc(s_raw, 1)
            rows_T2(2)
            rows_T2(3)
            router_exp(1)
            nc.scalar.activation(sgate[:, 0, :], sgate[:, 1, :], ACT.Exp, scale=-1.0).then_inc(s_pe, 1)

            def shared_evac(t):
                act.wait_ge(s_shtr, t + 1)
                if t:
                    act.wait_ge(s_dn, t)
                nc.scalar.activation(shT[:, 0:4, :], BANK[4].rearrange("p (c n) -> p c n", c=4), ACT.Copy)
                nc.scalar.activation(shT[:, 4, :], BANK[5][:, 0:P], ACT.Copy)
                nc.scalar.activation(shT[0:SLAST, 5, :], BANK[5][0:SLAST, P:2 * P], ACT.Copy).then_inc(s_shT, 1)

            def shared_silu(t):
                act.wait_ge(s_gate, t + 1)
                if t:
                    act.wait_ge(s_shh, t)
                nc.scalar.activation(shg.rearrange("p (a n) -> p a n", a=2), EP[0][:, :, 0:SHH], ACT.Silu).then_inc(s_silu, 1)

            act.wait_ge(s_raw, 1)
            nc.scalar.activation(shg, shg, ACT.Silu).then_inc(s_silu, 1)
            shared_silu(1)
            shared_evac(0)
            row_copies(1)
            for t in range(2, EARLY):
                shared_silu(t)
                shared_evac(t - 1)
            shared_evac(EARLY - 1)

            def silu(e, b, first=False):
                act.wait_ge(m_gu, e + 1)
                if not first:
                    act.wait_ge(m_h, e - 1)
                nc.scalar.activation(SL[b], BANK[b][:, 0:I], ACT.Silu).then_inc(m_silu, 1)

            for k in range(RING):
                silu(k, k % 2, first=k < 2)
            with act.Fori(1, LAPS - 1) as o:
                for k in range(RING):
                    silu(o * RING + k, k % 2)
            for e in range(NE - RING, NE + 1):
                silu(e, e % 2)
            act.wait_ge(s_slot, 3)
            nov = act.value_load(novi[0:1, 0:1], min_val=1, max_val=MAXOV)
            with act.If(nov > 1):
                with act.Fori(1, nov) as i:
                    act.wait_ge(m_gu, i + (NE + 1))
                    act.wait_ge(m_h, i + NE)
                    nc.scalar.activation(SL[0], BANK[0][:, 0:I], ACT.Silu).then_inc(m_silu, 1)
            for t in range(EARLY, NT):
                shared_silu(t)
                if t > EARLY:
                    shared_evac(t - 1)
            shared_evac(NT - 1)
            for t in POOL_TILES:
                act.wait_ge(s_yg[t], 16)
                for k in range(TOPK):
                    nc.scalar.activation(YG[t][:, k, :], YG[t][:, k, :], ACT.Copy, scale=top[:, t, k:k + 1]).then_inc(s_weighted, 1)

        @block.vector
        def _(dve):
            count = [0]

            def then(ins):
                count[0] += 1
                ins.then_inc(dv, 1)
                dve.wait_ge(dv, count[0])

            def statistics(h, var_sem):
                for t in range(4 * h, 4 * h + 4):
                    ins = nc.vector.bn_stats(stats[:, t, :], x[:, t, :])
                then(ins)
                for t in range(4 * h, 4 * h + 4):
                    ins = nc.vector.bn_aggr(mv[:, t, :], stats[:, t, :])
                then(ins)
                nc.vector.tensor_scalar(veps[:, 4 * h:4 * h + 4], mv[:, 4 * h:4 * h + 4, 1], EPS, None, ALU.add).then_inc(var_sem, 1)

            def normalise(h, done):
                for t in range(4 * h, 4 * h + 4):
                    ins = nc.vector.tensor_scalar(xh[:, t, 0:D], x[:, t, :], mv[:, t, 0:1], rstd[:, t:t + 1], ALU.subtract, ALU.mult)
                ins.then_inc(done, 1)

            dve.wait_ge(s_ec, 1)
            then(nc.vector.tensor_scalar(ccol[:, 2, :], ccol[:, 1, :], 1.0, None, ALU.add))
            then(nc.vector.reciprocal(ccol[:, 2, :], ccol[:, 2, :]))
            then(nc.vector.tensor_tensor(ccol[:, 3, :], ccol[:, 0, :], ccol[:, 2, :], ALU.mult))
            dve.wait_ge(s_const, 1)
            for c in range(NC):
                ins = nc.vector.tensor_scalar(crep[:, c, :], ones[:, :], ccol[:, 3, c:c + 1], None, ALU.mult)
            ins.then_inc(s_crep, 1)
            for h in range(2):
                dve.wait_ge(ld_x[h], 16)
                statistics(h, s_var)
            for h in range(2):
                dve.wait_ge(s_rstd, h + 1)
                normalise(h, s_h)
                if h == 0:
                    dve.wait_ge(s_mod, 1)
                    nc.vector.tensor_copy(modc[:, 0, :], BANK[0][:, 0:NC])
                    nc.vector.tensor_scalar(modc[:, 1, :], BANK[0][:, NC:2 * NC], 1.0, None, ALU.add).then_inc(s_modc, 1)
            dve.wait_ge(ld_rope, 32)
            dve.wait_ge(s_tr, NT // 2)
            for h in range(2):
                tt = slice(4 * h, 4 * h + 4)
                dve.wait_ge(s_qkvev, 4 * h + 4)
                pr = qkv[:, tt, 0:(NH + NG) * HD].rearrange("p t (h i two) -> p t h i two", h=NH + NG, two=2)
                a, b = pr[:, :, :, 0:4, 0], pr[:, :, :, 0:4, 1]
                cs = [w[:, tt, :].unsqueeze(2).to_broadcast([P, 4, NH + NG, 4]) for w in (cosr, sinr)]
                R = [rt[:, k].rearrange("p t (h i) -> p t h i", i=4) for k in range(4)]
                nc.vector.tensor_tensor(R[0], a, cs[0], ALU.mult)
                nc.vector.tensor_tensor(R[1], b, cs[1], ALU.mult)
                nc.vector.tensor_tensor(R[2], a, cs[1], ALU.mult)
                then(nc.vector.tensor_tensor(R[3], b, cs[0], ALU.mult))
                nc.vector.tensor_tensor(a, R[0], R[1], ALU.subtract)
                nc.vector.tensor_tensor(b, R[2], R[3], ALU.add).then_inc(s_rope, 1)
                dve.wait_ge(s_rope, h + 1)
                both = [(qkv[:, tt, 0:NH * HD].rearrange("p t (h d) -> p t h d", d=HD), QS[:, tt, :, :], Q_PARTS),
                        (qkv[:, tt, NH * HD:(NH + NG) * HD].rearrange("p t (h d) -> p t h d", d=HD), KS[:, tt, :, :], K_PARTS)]
                if h:
                    both = both[1:]
                part = lambda dst, parts, c: dst[:, :, :, HD * parts.index(c):HD * parts.index(c) + HD]
                for src, dst, parts in both:
                    ins = nc.vector.tensor_copy(part(dst, parts, "h"), src)
                then(ins)
                for src, dst, parts in both:
                    ins = nc.vector.tensor_tensor(src, src, part(dst, parts, "h"), ALU.subtract)
                then(ins)
                for src, dst, parts in both:
                    ins = nc.vector.tensor_copy(part(dst, parts, "m"), src)
                then(ins)
                for src, dst, parts in both:
                    ins = nc.vector.tensor_tensor(part(dst, parts, "l"), src, part(dst, parts, "m"), ALU.subtract)
                ins.then_inc(s_split, 1)
                dve.wait_ge(s_split, h + 1)
                for i in range(3, 6):
                    o = HD * K_PARTS.index(K_PARTS[i])
                    ins = nc.vector.tensor_copy(KS[:, tt, :, HD * i:HD * i + HD], KS[:, tt, :, o:o + HD])
                ins.then_inc(s_ks, 1)
            dve.wait_ge(s_qkd, 1)
            dst, src = qk_evac(QK_DVE, BANK[6])
            nc.vector.tensor_copy(dst, src).then_inc(s_qkD, 1)
            ring, taken = [0], [0]

            def take():
                ring[0] += 1
                taken[0] += 1
                dve.wait_ge(m_fill, ring[0])
                return MR[(ring[0] - 1) % 3]

            def row_max(k, heads):
                u, s = divmod(k, NT)
                for j in heads:
                    src = take()
                    nc.vector.reduce_max(mx[:, u % 2, s // 2, j, s % 2:s % 2 + 1], src, AX.X).then_inc(m_free, 1)

            def minus_max(u):
                dve.wait_ge(m_free, taken[0])
                m, part = negm[:, u % 2], MS[:, u % 2]
                then(nc.vector.tensor_reduce(out=m, in_=mx[:, u % 2], axis=AX.X, op=ALU.max, negate=True))
                then(nc.vector.tensor_copy(part[:, :, :, 0], m))
                nc.vector.tensor_tensor(part[:, :, :, 1], m, part[:, :, :, 0], ALU.subtract).then_inc(s_negm, 1)

            def take_output(u):
                g, qh = q_unit(u)
                bank = take()
                if u == U - 1:
                    bank = BANK[4]
                o = bank.rearrange("p (t j c) -> p t j c", t=4, j=4)
                then(nc.vector.reciprocal(rsum[:, u % 2], o[:, :, :, HD]))
                nc.vector.tensor_tensor(AT[:, 4 * qh:4 * qh + 4, 4 * HD * g:4 * HD * (g + 1)].rearrange("p t (j d) -> p t j d", j=4),
                                        o[:, :, :, 0:HD], rsum[:, u % 2].unsqueeze(3).to_broadcast([P, 4, 4, HD]), ALU.mult).then_inc(m_free, 1)

            for k in range(LEAD):
                row_max(k, (2, 3, 0, 1))
                if k % NT == NT - 1:
                    minus_max(k // NT)
            ring[0] += 2
            dve.wait_ge(s_modev, 3)
            nc.vector.tensor_scalar(MOD[:, 4, :], MOD[:, 4, :], 1.0, None, ALU.add)
            nc.vector.tensor_scalar(modc[:, 4, :], modc[:, 4, :], 1.0, None, ALU.add).then_inc(s_mod1, 1)
            for k in (2, 5):
                g0 = gtmp[:, 0, :]
                g1 = gtmp[:, 1, :]
                nc.vector.tensor_scalar(g0, MOD[:, k, :], 0.0, 2.0, ALU.is_ge, ALU.mult)
                then(nc.vector.scalar_tensor_tensor(out=g1, in0=MOD[:, k, :], scalar=-1.0, in1=MOD[:, k, :], op0=ALU.mult, op1=ALU.max))
                then(nc.vector.tensor_scalar(g1, g1, 0.25, None, ALU.max))
                then(nc.vector.scalar_tensor_tensor(out=MOD[:, k, :], in0=g0, scalar=-1.0, in1=g1, op0=ALU.add, op1=ALU.mult))
            dve.wait_ge(ld_wo, 16)
            nc.vector.tensor_tensor(wog[:, :, :], wo[:, :, :], MOD[:, 2:3, :].to_broadcast([P, NC, D]), ALU.mult).then_inc(s_wog, 1)

            for n in range(STEPS):
                k = n + LEAD
                if k < STEPS:
                    row_max(k, (2, 3))
                if n % NT == 2 and n > NT:
                    take_output(n // NT - 1)
                if n % NT == NT - 1 and n < STEPS - 1:
                    ring[0] += 2
                if k < STEPS:
                    row_max(k, (0, 1))
                    if k % NT == NT - 1:
                        minus_max(k // NT)
            def second_norm(h):
                for tp in (2 * h, 2 * h + 1):
                    dve.wait_ge(s_ao, tp + 1)
                    nc.vector.tensor_tensor(x[:, 2 * tp:2 * tp + 2, :], x[:, 2 * tp:2 * tp + 2, :],
                                            BANK[WO_BANK[tp]].rearrange("p (t n) -> p t n", t=2), ALU.add).then_inc(s_x1, 1)
                dve.wait_ge(s_x1, 2 * h + 2)
                statistics(h, s_var2)
                dve.wait_ge(s_rstd, h + 3)
                normalise(h, s_h2)

            def shared_mul(t):
                dve.wait_ge(s_silu, t + 1)
                dve.wait_ge(s_up, t + 1)
                if t >= 2:
                    dve.wait_ge(s_shtr, t - 1)
                nc.vector.tensor_tensor(shh[t % 2].rearrange("p (a n) -> p a n", a=2), shg.rearrange("p (a n) -> p a n", a=2),
                                        EP[1][:, :, 0:SHH], ALU.mult).then_inc(s_shh, 1)

            def shared_out(t):
                dve.wait_ge(s_dn, t + 1)
                nc.vector.scalar_tensor_tensor(out=SH[:, t, :], in0=BANK[6 + t % 2][:, 0:D], scalar=sgate[:, 0, t:t + 1],
                                               in1=MOD[:, 5, :], op0=ALU.mult, op1=ALU.mult).then_inc(s_sh, 1)

            lg = BANK[6][:, 0:NT * (NE + 1)].rearrange("p (t e) -> p t e", t=NT)
            sm = small
            mxl, sml = sm[:, 0:NT], sm[:, NT:2 * NT]

            def router(h):
                tt = slice(4 * h, 4 * h + 4)
                wide4 = lambda v: v[:, tt].unsqueeze(2).to_broadcast([P, 4, NE])
                dve.wait_ge(s_lg, h + 1)
                then(nc.vector.reduce_max(mxl[:, tt], lg[:, tt, 0:NE], AX.X))
                nc.vector.tensor_copy(sgate[:, 1, tt], lg[:, tt, NE])
                nc.vector.tensor_tensor(probs[:, tt, :], lg[:, tt, 0:NE], wide4(mxl), ALU.subtract).then_inc(s_ld, 1)
                dve.wait_ge(s_pe, 2 * h + 1)
                then(nc.vector.reduce_sum(sml[:, tt], probs[:, tt, :], AX.X))
                then(nc.vector.reciprocal(sml[:, tt], sml[:, tt]))
                then(nc.vector.tensor_tensor(probs[:, tt, :], probs[:, tt, :], wide4(sml), ALU.mult))
                if h:
                    shared_mul(0)
                for t in range(4 * h, 4 * h + 4):
                    ins = nc.vector.max(top[:, t, :], probs[:, t, :])
                then(ins)
                for t in range(4 * h, 4 * h + 4):
                    ins = nc.vector.max_index(topi[:, t, :], top[:, t, :], probs[:, t, :])
                then(ins)
                then(nc.vector.tensor_copy(topf[:, tt, :], topi[:, tt, :]))
                for t in range(4 * h, 4 * h + 4):
                    ins = nc.vector.tensor_tensor(OH[:, t], iotaf[:, :].unsqueeze(1).to_broadcast([P, TOPK, NE]),
                                                  topf[:, t, 0:TOPK].unsqueeze(2).to_broadcast([P, TOPK, NE]), ALU.is_equal)
                then(ins)
                nc.vector.tensor_reduce(out=mask[:, tt, :], in_=OH[:, tt].rearrange("p t k e -> p t e k"), axis=AX.X, op=ALU.max).then_inc(s_mask, 1)

            dve.wait_ge(empty_st, 16 * N_EMPTY)
            dve.wait_ge(s_iota, 2)
            second_norm(0)
            take_output(U - 1)
            router(0)
            second_norm(1)
            router(1)
            then(nc.vector.tensor_scalar(sgate[:, 1, :], sgate[:, 0, :], 1.0, None, ALU.add))
            then(nc.vector.reciprocal(sgate[:, 0, :], sgate[:, 1, :]))
            shared_mul(1)
            cnt, nov, inc, off, base = (sm[:, 64 * (k + 1):64 * (k + 1) + NE] for k in range(5))
            thr = sm[:, 400:400 + NT - 1]
            nc.vector.tensor_scalar(thr, iotaf[:, 1:NT], float(P), None, ALU.mult)
            then(nc.vector.tensor_scalar(base, iotaf[:, :], float(P), None, ALU.mult))
            dve.wait_ge(s_rank, 1)
            rank = BANK[7][:, 0:NT * NE].rearrange("p (t e) -> p t e", t=NT)
            nc.vector.tensor_copy(cnt, BANK[6][:, 0:NE]).then_inc(s_cnt, 1)
            dve.wait_ge(s_cnt, 1)
            then(nc.vector.tensor_tensor(gt, cnt.unsqueeze(2).to_broadcast([P, NE, NT - 1]),
                                         thr.unsqueeze(1).to_broadcast([P, NE, NT - 1]), ALU.is_gt))
            then(nc.vector.reduce_sum(nov, gt, AX.X))
            then(nc.vector.tensor_tensor_scan(inc, ones[:, 0:NE], nov, 0.0, ALU.mult, ALU.add))
            then(nc.vector.tensor_tensor(off, inc, nov, ALU.subtract))
            then(nc.vector.tensor_scalar(off, off, float(P), float(P * (NE - 1)), ALU.mult, ALU.add))
            then(nc.vector.tensor_tensor(off, off, base, ALU.subtract))
            nc.vector.scalar_tensor_tensor(out=slot[:, :, :], in0=rank, scalar=float(P), in1=off.unsqueeze(1).to_broadcast([P, NT, NE]),
                                           op0=ALU.is_ge, op1=ALU.mult)
            then(nc.vector.tensor_tensor(probs[:, :, :], rank, base.unsqueeze(1).to_broadcast([P, NT, NE]), ALU.add))
            then(nc.vector.tensor_tensor(slot[:, :, :], slot[:, :, :], probs[:, :, :], ALU.add))
            for a, b in ((0, 2), (2, NT)):
                k = slice(TOPK * a, TOPK * b)
                then(nc.vector.tensor_tensor(PR[:, a:b], OH[:, a:b], slot[:, a:b, :].unsqueeze(2).to_broadcast([P, b - a, TOPK, NE]), ALU.mult))
                then(nc.vector.reduce_sum(slotk[:, k], PR[:, a:b].rearrange("p t k e -> p (t k) e"), AX.X))
                nc.vector.tensor_copy(sloti[:, k], slotk[:, k]).then_inc(s_slot, 1)
                if a == 0:
                    shared_mul(2)
                    shared_out(0)
            nc.vector.tensor_scalar(novi[0:1, 0:1], inc[0:1, NE - 1:NE], 1.0, None, ALU.max)
            ove = PR.rearrange("p t k e -> p (t k) e")[0:1, 0:MAXOV]
            then(nc.vector.tensor_tensor(ove, inc[0:1, :].unsqueeze(1).to_broadcast([1, MAXOV, NE]),
                                         iotaf[0:1, 0:MAXOV].unsqueeze(2).to_broadcast([1, MAXOV, NE]), ALU.is_le))
            then(nc.vector.reduce_sum(slotk[0:1, 0:MAXOV], ove, AX.X))
            nc.vector.tensor_scalar(ovei[0:1, 0:MAXOV], slotk[0:1, 0:MAXOV], float(NE - 1), None, ALU.min).then_inc(s_slot, 1)

            shared_out(1)
            for t in range(3, EARLY):
                shared_mul(t)
                shared_out(t - 1)

            def hidden_T(e1, b):
                dve.wait_ge(m_ht, e1)
                nc.vector.tensor_copy(HST[b], BANK[4 + b][0:IC, 0:2 * P]).then_inc(m_htev, 1)

            def rows_T(e1, b):
                dve.wait_ge(m_xt, e1)
                nc.vector.tensor_copy(XGT[b], BANK[2 + b][:, 0:D]).then_inc(m_xtev, 1)

            def hidden(e1, b):
                dve.wait_ge(m_silu, e1)
                nc.vector.tensor_tensor(HS[b], SL[b], BANK[b][:, I:2 * I], ALU.mult).then_inc(m_h, 1)

            def result(e, k, sent):
                dve.wait_ge(m_y, e + 1)
                if sent is not None:
                    dve.wait_ge(y_st[k % BUFS], sent)
                nc.vector.tensor_tensor(YS[k % BUFS], BANK[6 + k % 2][:, 0:D], MOD[:, 5, :], ALU.mult).then_inc(m_yev, 1)

            def expert(e, k, prev, nxt):
                if prev:
                    hidden_T(e, 1 - k % 2)
                if nxt:
                    rows_T(e + 2, 1 - k % 2)
                hidden(e + 1, k % 2)

            rows_T(1, 0)
            rows_T(2, 1)
            shared_out(EARLY - 1)
            for k in range(RING):
                expert(k, k, prev=k > 0, nxt=k > 0)
                if k >= 2:
                    result(k - 2, k - 2, 16 * ((k - 2) // BUFS) if k - 2 >= BUFS else None)
            with dve.Fori(1, LAPS - 1) as o:
                for k in range(RING):
                    expert(o * RING + k, k, prev=True, nxt=True)
                    result(o * RING + (k - 2), (k - 2) % RING, o * (16 * RING // BUFS) + 16 * ((k - 2) // BUFS))
            for e in range(NE - RING, NE + 1):
                expert(e, e, prev=True, nxt=e < NE)
                result(e - 2, e - 2, 16 * ((e - 2) // BUFS))
            hidden_T(NE + 1, 0)
            for e in (NE - 1, NE):
                result(e, e, 16 * (e // BUFS))
            dve.wait_ge(s_slot, 3)
            nov_r = dve.value_load(novi[0:1, 0:1], min_val=1, max_val=MAXOV)
            with dve.If(nov_r > 1):
                with dve.Fori(1, nov_r) as i:
                    rows_T(i + (NE + 1), 0)
                    hidden(i + (NE + 1), 0)
                    hidden_T(i + (NE + 1), 0)
                    result(i + NE, 0, i * 16 + 16 * (NE // BUFS))

            def combine(tiles):
                for t in tiles:
                    dve.wait_ge(s_yg[t], 16)
                for k in range(TOPK):
                    for t in tiles:
                        ins = nc.vector.scalar_tensor_tensor(out=x[:, t, :], in0=YG[t][:, k, :], scalar=top[:, t, k:k + 1],
                                                             in1=x[:, t, :], op0=ALU.mult, op1=ALU.add)
                        if k == TOPK - 1:
                            ins.then_inc(s_fin, 1)
                    if k < TOPK - 1:
                        then(ins)

            for t in range(EARLY, NT):
                shared_mul(t)
            dve.wait_ge(s_base, 1)
            combine((0, 1))
            for t in range(EARLY, NT):
                shared_out(t)
                dve.wait_ge(s_sh, t + 1)
                then(nc.vector.tensor_tensor(x[:, t, :], x[:, t, :], SH[:, t, :], ALU.add))
            combine((3, 4))
            combine((6,))
            combine((7,))

        @block.tensor
        def _(pe):
            mm, tr = nc.tensor.matmul, nc.tensor.transpose
            I_ = ident[:, :]

            def transpose_tiles(src, bank, tp):
                for t in range(2):
                    for c in range(NC):
                        o = (t * NC + c) * P
                        ins = tr(bank[:, o:o + P], src[:, 2 * tp + t, c * P:(c + 1) * P], I_)
                return ins

            def mod_columns(k, bank):
                for m in range(2):
                    for d in range(NC):
                        for c in range(NC):
                            o = (k + m) * D + d * P
                            at = (2 * (k > 0) + m) * NC + d
                            ins = mm(bank[:, at:at + 1], wmod[:, c, o:o + P], ccol[:, 3, c:c + 1], start=c == 0, stop=c == NC - 1)
                return ins

            pe.wait_ge(s_crep, 1)
            pe.wait_ge(ld_mod[0], 16)
            mod_columns(0, BANK[0]).then_inc(s_mod, 1)
            pe.wait_ge(s_ident, 2)
            def rows_T1(tp):
                pe.wait_ge(s_h, tp // 2 + 1)
                transpose_tiles(xh, BANK[3 + tp], tp).then_inc(s_tr, 1)

            rows_T1(0)
            rows_T1(1)
            pe.wait_ge(ld_qkv, 16)
            pe.wait_ge(s_modc, 1)
            for t in range(NT):
                if t == 2:
                    rows_T1(2)
                    rows_T1(3)
                pe.wait_ge(s_trev, max(t // 2 + 1, t - 3))
                for c in range(NC):
                    ins = mm(BANK[(7 + t) % 8][:, 0:QKV], hT[:, c, t * P:(t + 1) * P], wqkv[:, c, :], start=c == 0, stop=c == NC - 1)
                ins.then_inc(s_qkv, 1)
            pe.wait_ge(ld_mod[1], 16)
            pe.wait_ge(s_qkvev, 7)
            for b in range(2):
                for c in range(NC):
                    mm(BANK[4 + b], crep[:, c, :], wmod[:, c, 512 * (1 + b):512 * (2 + b)], start=c == 0, stop=c == NC - 1)
            mod_columns(3, BANK[3]).then_inc(s_mod, 1)

            def transpose_qk(item, bank, done):
                h, is_k, j = item
                b = bank.bitcast(bf16)
                for i in range(2):
                    for t in range(4):
                        src = (KS[:, 4 * h + t, j + i, 0:SM] if is_k else QS[:, 4 * h + t, j + i, :])
                        o = (4 * i + t) * P
                        ins = tr(b[0:SM if is_k else SR, o:o + P], src, identb[:, :])
                ins.then_inc(done, 1)

            def transpose_later(n):
                if n == QK_H1:
                    pe.wait_ge(s_qa, 2)
                pe.wait_ge(s_qkA, n - 3)
                transpose_qk(QK[n], BANK[n % 4], s_qk)

            pe.wait_ge(s_qkvev, NT)
            pe.wait_ge(s_ident, 3)
            pe.wait_ge(s_ks, 1)
            for n in range(QK_FIRST):
                if n == 1:
                    pe.wait_ge(s_qa, 1)
                if n == 3:
                    pe.wait_ge(s_modev, 3)
                transpose_qk(QK[n], BANK[n], s_qk)
            pe.wait_ge(s_ks, 2)
            transpose_qk(QK_DVE, BANK[6], s_qkd)
            pe.wait_ge(s_qkA, 3)
            pe.wait_ge(s_qkD, 1)

            took = []

            def fill(taker):
                n = len(took)
                took.append(taker)
                if n >= 3:
                    pe.wait_ge(took[n - 3], took[:n - 2].count(took[n - 3]))
                return MR[n % 3]

            def scores_for_max(k, heads):
                u, s = divmod(k, NT)
                g, qh = q_unit(u)
                q0 = (4 * qh + s // 2) * P
                for j in heads:
                    mm(fill(m_free), QT[0:SR, 4 * g + j, q0:q0 + P], KT[0:SR, g, 512 * (s % 2):512 * (s % 2) + 512], start=True, stop=True).then_inc(m_fill, 1)

            def transpose_max(u):
                pe.wait_ge(s_negm, u + 1)
                for i in range(2):
                    b = fill(a_free).bitcast(bf16)
                    for j in range(2):
                        for t in range(4):
                            o = (4 * j + t) * P
                            ins = tr(b[SR:SM, o:o + P], MS[:, u % 2, t, 2 * i + j, :], identb[:, :])
                    ins.then_inc(m_fill, 1)

            def transpose_output(u):
                pe.wait_ge(s_atev, u + 1)
                b = fill(m_free)
                if u == U - 1:
                    b = BANK[4]
                for t in range(4):
                    ins = tr(b[:, t * P:(t + 1) * P], OT[:, t * P:(t + 1) * P], I_)
                ins.then_inc(m_fill, 1)

            def scores(n, p):
                u, tt = divmod(n, NT)
                g, qh = q_unit(u)
                if n:
                    pe.wait_ge(e_done, 2 * (n - 1) + p + 1)
                for i in range(2):
                    j = 2 * p + i
                    ins = mm(EP[p][:, i, :], KT[0:SM, g, tt * P:(tt + 1) * P], QT[0:SM, 4 * g + j, 512 * qh:512 * qh + 512], start=True, stop=True)
                ins.then_inc(e_fill, 1)

            def output(n):
                u, tt = divmod(n, NT)
                g, qh = q_unit(u)
                pe.wait_ge(e_done, 2 * n + 2)
                if tt == 0 and u:
                    pe.wait_ge(s_atev, u)
                for j in range(4):
                    ins = mm(PV[HP * j:HP * j + HP, :], VA[:, tt, g, :], PT[n % 3][:, j, :], start=tt == 0, stop=tt == NT - 1)
                ins.then_inc(pv_step, 1)

            def attention_T(tp):
                transpose_tiles(AT, BANK[AT_BANK[tp]], tp).then_inc(s_at, 1)

            def project(tp):
                pe.wait_ge(s_wog, 1)
                pe.wait_ge(s_trev, NT // 2 + tp + 1)
                for t in range(2):
                    for c in range(NC):
                        ins = mm(BANK[WO_BANK[tp]][:, t * D:(t + 1) * D], hT[:, c, (2 * tp + t) * P:(2 * tp + t + 1) * P],
                                 wog[:, c, :], start=c == 0, stop=c == NC - 1)
                ins.then_inc(s_ao, 1)

            def rows_T2(tp):
                pe.wait_ge(s_h2, tp // 2 + 1)
                transpose_tiles(xh, BANK[H2_BANK[tp]], tp).then_inc(s_tr2, 1)

            LATER = {0: (4, 5), 1: (6, 7), 2: (8, 9), 4: (10, 11), 5: (12, 13), 6: (14, 15), 7: (16, 17), 8: (18,)}
            for k in range(LEAD):
                if k == NT:
                    pe.wait_ge(s_qkA, QK_H1 + 2)
                scores_for_max(k, (2, 3, 0, 1))
                for n in LATER.get(k, ()):
                    transpose_later(n)
            transpose_max(0)
            pe.wait_ge(s_qkA, len(QK))
            pe.wait_ge(s_va, 2)
            for n in range(STEPS):
                k = n + LEAD
                u = n // NT
                if n % NT == 0:
                    pe.wait_ge(a_free, 2 * u + 2)
                scores(n, 0)
                if k < STEPS:
                    scores_for_max(k, (2, 3))
                if n % NT == 2 and n > NT:
                    transpose_output(u - 1)
                if n % NT == NT - 1 and n < STEPS - 1:
                    transpose_max(u + 1)
                scores(n, 1)
                if k < STEPS:
                    scores_for_max(k, (0, 1))
                if n:
                    output(n - 1)
                if n == STEPS - 5:
                    pe.wait_ge(m_free, took.count(m_free))
                    attention_T(0)
                    attention_T(1)
                if n in (STEPS - 4, STEPS - 3):
                    project(n - STEPS + 4)
            rows_T2(0)
            rows_T2(1)
            output(STEPS - 1)
            transpose_output(U - 1)

            def logits(tiles):
                for t in tiles:
                    pe.wait_ge(s_tr2ev, t // 2 + 1)
                    for c in range(NC):
                        ins = mm(BANK[6][:, t * (NE + 1):(t + 1) * (NE + 1)], h2T[:, c, t * P:(t + 1) * P], wr[:, c, :],
                                 start=c == 0, stop=c == NC - 1)
                return ins

            def shared_half(t, part, a):
                for c in range(NC):
                    o = part * ISH + a * SHH
                    ins = mm(EP[part][:, a, 0:SHH], h2T[:, c, t * P:(t + 1) * P], segu[:, c, o:o + SHH], start=c == 0, stop=c == NC - 1)
                return ins

            def shared_in(t, part, done):
                if t:
                    pe.wait_ge(s_shh if part else s_silu, t)
                shared_half(t, part, 0)
                shared_half(t, part, 1).then_inc(done, 1)

            pe.wait_ge(ld_wr, 16)
            logits(range(NT // 2)).then_inc(s_lg, 1)
            pe.wait_ge(m_free, took.count(m_free))
            attention_T(2)
            attention_T(3)
            pe.wait_ge(ld_sh, 48)
            shared_half(0, 0, 0)
            project(2)
            project(3)
            shared_half(0, 0, 1).then_inc(s_gate, 1)
            shared_in(0, 1, s_up)
            pe.wait_ge(s_raw, 1)
            shared_half(1, 0, 0)
            rows_T2(2)
            rows_T2(3)
            shared_half(1, 0, 1).then_inc(s_gate, 1)
            logits(range(NT // 2, NT)).then_inc(s_lg, 1)

            def ranks():
                pe.wait_ge(s_mask, 2)
                for t in range(NT):
                    for s in range(t):
                        mm(BANK[7][:, t * NE:(t + 1) * NE], onesb[:, :], mask[:, s, :], start=s == 0, stop=False)
                    mm(BANK[7][:, t * NE:(t + 1) * NE], upper[:, :], mask[:, t, :], start=t == 0, stop=True)
                for t in range(NT):
                    ins = mm(BANK[6][:, 0:NE], onesb[:, :], mask[:, t, :], start=t == 0, stop=t == NT - 1)
                ins.then_inc(s_rank, 1)

            def shared_T(t):
                pe.wait_ge(s_shh, t + 1)
                if t:
                    pe.wait_ge(s_shT, t)
                for c in range(NSC):
                    w = P if c < NSC - 1 else SLAST
                    ins = tr(BANK[4 + c // 4][0:w, (c % 4) * P:(c % 4 + 1) * P], shh[t % 2][:, c * P:c * P + w], I_)
                ins.then_inc(s_shtr, 1)

            def shared_down(t):
                pe.wait_ge(s_shT, t + 1)
                if t >= 2:
                    pe.wait_ge(s_sh, t - 1)
                else:
                    pe.wait_ge((s_cnt, s_slot)[t], 1)
                for c in range(NSC):
                    w = P if c < NSC - 1 else SLAST
                    ins = mm(BANK[6 + t % 2][:, 0:D], shT[0:w, c, :], sedn[0:w, c, :], start=c == 0, stop=c == NSC - 1)
                ins.then_inc(s_dn, 1)

            shared_T(0)
            shared_in(1, 1, s_up)
            ranks()
            shared_in(2, 0, s_gate)
            shared_T(1)
            shared_in(2, 1, s_up)
            shared_down(0)
            for t in range(3, EARLY):
                shared_in(t, 0, s_gate)
                shared_down(t - 2)
                shared_T(t - 1)
                shared_in(t, 1, s_up)
            shared_down(EARLY - 2)
            shared_T(EARLY - 1)

            def rows(b, q, ld, n):
                pe.wait_ge(ld, n)
                for c in range(NC):
                    ins = tr(BANK[2 + b][:, c * P:(c + 1) * P], XG[q][:, c * P:(c + 1) * P], I_)
                ins.then_inc(m_xt, 1)

            def gate_up(e1, b, r):
                pe.wait_ge(m_xtev, e1)
                for c in range(NC):
                    ins = mm(BANK[b][:, 0:I13], XGT[b][:, c * P:(c + 1) * P], w13[:, r, c * I13:(c + 1) * I13], start=c == 0, stop=c == NC - 1)
                ins.then_inc(m_gu, 1)

            def hidden_T(e1, b):
                pe.wait_ge(m_h, e1)
                for c in range(2):
                    ins = tr(BANK[4 + b][0:IC, c * P:(c + 1) * P], HS[b][:, c * IC:(c + 1) * IC], I_)
                ins.then_inc(m_ht, 1)

            def down(e1, b, r):
                pe.wait_ge(m_htev, e1)
                for c in range(2):
                    ins = mm(BANK[6 + b][:, 0:D], HST[b][:, c * P:(c + 1) * P], w2[:, r, c * D:(c + 1) * D], start=c == 0, stop=c == 1)
                ins.then_inc(m_y, 1)

            def expert(e, k, loads, nxt, first=False):
                b = k % 2
                if k % 2 == 0:
                    pe.wait_ge(ld_w[k // 2], loads)
                gate_up(e + 1, b, k)
                if not (first and k == 0):
                    hidden_T(e, 1 - b)
                if nxt is not None:
                    q = (k + 1) % BUFS
                    rows(1 - b, q, xg_ld[q], nxt)
                if not (first and k < 2):
                    if first and k == 2:
                        pe.wait_ge(s_sh, EARLY)
                    if not (first and k < 4):
                        pe.wait_ge(m_yev, e - 3)
                    down(e - 1, b, (k - 2) % RING)

            rows(0, 0, xg_ld[0], 16)
            rows(1, 1, xg_ld[1], 16)
            shared_down(EARLY - 1)
            for k in range(RING):
                expert(k, k, 32, 16 * ((k + 1) // BUFS + 1) if k else None, first=True)
            with pe.Fori(1, LAPS - 1) as o:
                for k in range(RING):
                    expert(o * RING + k, k, o * 32 + 32, o * (16 * RING // BUFS) + 16 * ((k + 1) // BUFS + 1))
            for e in range(NE - RING, NE + 1):
                expert(e, e % RING, 32 * (e // RING + 1), 16 * ((e + 1) // BUFS + 1) if e < NE else None)
            hidden_T(NE + 1, 0)
            pe.wait_ge(m_yev, NE - 2)
            down(NE, 1, RING - 1)
            pe.wait_ge(m_yev, NE - 1)
            down(NE + 1, 0, 0)
            pe.wait_ge(s_slot, 3)
            nov = pe.value_load(novi[0:1, 0:1], min_val=1, max_val=MAXOV)
            with pe.If(nov > 1):
                with pe.Fori(1, nov) as i:
                    rows(0, 0, o_ld, i * 48)
                    gate_up(i + (NE + 1), 0, 0)
                    hidden_T(i + (NE + 1), 0)
                    pe.wait_ge(m_yev, i + NE)
                    down(i + (NE + 1), 0, 0)
            pe.wait_ge(m_yev, NE)
            for t in range(EARLY, NT):
                shared_in(t, 0, s_gate)
                if t > EARLY:
                    shared_T(t - 1)
                shared_in(t, 1, s_up)
                if t > EARLY:
                    shared_down(t - 1)
            shared_T(NT - 1)
            shared_down(NT - 1)


def kernel(**inputs):
    import numpy as np
    import concourse.bacc as bacc
    from concourse.bass_utils import run_bass_kernel_spmd

    a = {k[3:]: np.asarray(v) for k, v in inputs.items()}
    S, D = a["attn_hidden_states"].shape[1:]
    P, NC = 128, D // 128
    E, I2, _ = a["ffn_w13"].shape
    I = I2 // 2
    half = 8
    inv = (np.float32(1.0) / np.float32(10000.0) ** (np.arange(0, half, 2, dtype=np.float32) / np.float32(half))).astype(np.float32)
    ang = np.arange(S, dtype=np.float32)[:, None] * inv[None, :]
    table = lambda f: np.ascontiguousarray(f(ang).astype(np.float32).reshape(S // P, P, half // 2).transpose(1, 0, 2))
    arrays = {
        "x": a["attn_hidden_states"][0],
        "cos": table(np.cos), "sin": table(np.sin),
        "c": a["c"][0].reshape(NC, P).T,
        "wmod": a["wmod"],
        "wqkv": np.concatenate([a["attn_Wq"], a["attn_Wk"], a["attn_Wv"]], axis=1),
        "wo": a["attn_Wo"],
        "wr": np.concatenate([a["ffn_gate_w"], a["ffn_shared_gate_w"]], axis=0).T,
        "segu": a["ffn_se_gate_up_w"].T,
        "sedn": a["ffn_se_down_w"].T,
        "w13": a["ffn_w13"].reshape(E, I2, NC, P).transpose(0, 3, 2, 1).reshape(E, P, NC * I2),
        "w2": a["ffn_w2"].reshape(E, D, 2, I // 2).transpose(0, 3, 2, 1).reshape(E, I // 2, 2 * D),
    }
    arrays = {k: np.ascontiguousarray(v) for k, v in arrays.items()}
    nc = bacc.Bacc("TRN2", target_bir_lowering=False, num_devices=1)
    f32 = mybir.dt.float32
    args = [nc.dram_tensor("in_" + k, v.shape, f32, kind="ExternalInput").ap() for k, v in arrays.items()]
    rows = (E + S * 4 // P - 1) * P
    tables = [nc.dram_tensor(k, shape, f32, kind="Internal").ap() for k, shape in
              (("xdisp", (rows, D + 1)), ("ychoice", (S * 4 + 5 * P, D)))]
    o = nc.dram_tensor("out", (S, D), f32, kind="ExternalOutput").ap()
    adaln_layer(nc, *args, *tables, o)
    r = run_bass_kernel_spmd(nc, [{"in_" + k: v for k, v in arrays.items()}], core_ids=[0])
    return np.asarray(r.results[0]["out"]).reshape(1, S, D)
```
